# Optimizing a Trainium2 kernel written in Bass

```python
import numpy as np
import jax
import jax.numpy as jnp

def _softmax(x, axis=-1):
    return jax.nn.softmax(x, axis=axis)

def _gelu(x):
    return jax.nn.gelu(x, approximate=True)

def _silu(x):
    return jax.nn.silu(x)

def _sigmoid(x):
    return jax.nn.sigmoid(x)

def _layernorm(x, axis=-1, eps=1e-05):
    m = jnp.mean(x, axis=axis, keepdims=True)
    v = jnp.var(x, axis=axis, keepdims=True)
    return (x - m) / jnp.sqrt(v + eps)

def _scatter_add(tgt, idx, src, axis=0):
    return tgt.at[idx].add(src)

def _segment_sum(src, seg, n):
    return jax.ops.segment_sum(src, seg, n)
kernel_name = 'mk_vit_tower_d1_tok_img256_r4_666a66'

def setup_inputs(seed: int=0):
    np.random.seed(seed)
    _w = jnp.asarray

    def _rec_inputs():
        import jax
        import jax.numpy as jnp
        _rk = jax.random.key(seed)
        x = -0.000202321 + 1.00025 * jax.random.normal(jax.random.fold_in(_rk, 1), (8, 64, 56, 56), jnp.float32)
        return x
    x = _rec_inputs()

    def _L0_tok_setup():
        import jax, jax.numpy as jnp
        import numpy as np
        B, C, H, W = (8, 64, 56, 56)
        K = 3

        def _unfold3x3(x):
            b, c, h, w = x.shape
            xp = jnp.pad(x, ((0, 0), (0, 0), (1, 1), (1, 1)))
            patches = jnp.stack([xp[:, :, i:i + h, j:j + w] for i in range(K) for j in range(K)], axis=2)
            return patches.reshape(b, c * K * K, h * w).transpose(0, 2, 1)
        key = jax.random.key(seed)
        ks = jax.random.split(key, 8)
        d = C * K * K
        s1 = 1.0 / np.sqrt(d)
        s2 = 1.0 / np.sqrt(C)
        return {'x': jax.random.normal(ks[0], (B, C, H, W), jnp.float32), 'W1': jax.random.uniform(ks[1], (d, C), jnp.float32, -s1, s1), 'b1': jax.random.uniform(ks[2], (C,), jnp.float32, -s1, s1), 'W2': jax.random.uniform(ks[3], (C, d), jnp.float32, -s2, s2), 'b2': jax.random.uniform(ks[4], (d,), jnp.float32, -s2, s2), 'W3': jax.random.uniform(ks[5], (d, C), jnp.float32, -s1, s1), 'b3': jax.random.uniform(ks[6], (C,), jnp.float32, -s1, s1)}
    _L0_tok_all = _L0_tok_setup()
    _L0_tok_in = {k: v for k, v in _L0_tok_all.items() if k in ('W1', 'b1', 'W2', 'b2', 'W3', 'b3')}
    del _L0_tok_all

    def _L0_attn_setup():
        import jax, jax.numpy as jnp
        import numpy as np
        import math
        B_SZ, L_SEQ, IN_DIM, D_MODEL, OUT_DIM = (8, 1024, 64, 128, 64)
        RMIN, RMAX = (0.8, 0.99)

        def _reference_tuple_inner(inputs, nu_log, theta_log, gamma_log, B_re, B_im, C_re, C_im, D):
            skip = jnp.einsum('blh,dh->bld', inputs, D)
            L = inputs.shape[1]
            A = jnp.exp(jax.lax.complex(-jnp.exp(nu_log), jnp.exp(theta_log)))
            Bc = jax.lax.complex(B_re, B_im) * jnp.exp(gamma_log)[:, None]
            u = jnp.einsum('blh,dh->bld', inputs.astype(jnp.complex64), Bc)
            H = A[:, None] ** jnp.arange(L)
            n = 2 * L
            h_f = jnp.fft.fft(H, n=n, axis=1)
            u_f = jnp.fft.fft(u, n=n, axis=1)
            x = jnp.fft.ifft(u_f * h_f.T, axis=1)[:, :L]
            y = jnp.einsum('blh,nh->bln', x, jax.lax.complex(C_re, C_im)).real + skip
            return (x, y)
        key = jax.random.key(seed)
        ks = jax.random.split(key, 9)
        inputs = jax.random.normal(ks[0], (B_SZ, L_SEQ, IN_DIM), dtype=jnp.float32)
        u1 = jax.random.uniform(ks[1], (D_MODEL,), dtype=jnp.float32)
        u2 = jax.random.uniform(ks[2], (D_MODEL,), dtype=jnp.float32)
        nu_log = jnp.log(-0.5 * jnp.log(u1 * (RMAX + RMIN) * (RMAX - RMIN) + RMIN ** 2))
        theta_log = jnp.log(2 * math.pi * u2)
        gamma_log = jnp.sqrt(1.0 - jnp.exp(-jnp.exp(nu_log)) ** 2)
        B_re = jax.random.uniform(ks[3], (D_MODEL, IN_DIM), dtype=jnp.float32) / math.sqrt(2 * IN_DIM)
        B_im = jax.random.uniform(ks[4], (D_MODEL, IN_DIM), dtype=jnp.float32) / math.sqrt(2 * IN_DIM)
        C_re = jax.random.uniform(ks[5], (OUT_DIM, D_MODEL), dtype=jnp.float32) / math.sqrt(D_MODEL)
        C_im = jax.random.uniform(ks[6], (OUT_DIM, D_MODEL), dtype=jnp.float32) / math.sqrt(D_MODEL)
        D = jax.random.uniform(ks[7], (OUT_DIM, IN_DIM), dtype=jnp.float32) / math.sqrt(IN_DIM)
        return {'inputs': inputs, 'nu_log': nu_log, 'theta_log': theta_log, 'gamma_log': gamma_log, 'B_re': B_re, 'B_im': B_im, 'C_re': C_re, 'C_im': C_im, 'D': D}
    _L0_attn_all = _L0_attn_setup()
    _L0_attn_in = {k: v for k, v in _L0_attn_all.items() if k in ('nu_log', 'theta_log', 'gamma_log', 'B_re', 'B_im', 'C_re', 'C_im', 'D')}
    del _L0_attn_all

    def _L0_ffn_setup():
        import jax, jax.numpy as jnp
        import numpy as np
        BN_EPS = 0.001

        def _bn(h, g, b, m, v):
            return g * (h - m) * jax.lax.rsqrt(v + BN_EPS) + b
        key = jax.random.key(seed)
        ks = jax.random.split(key, 8)
        B, F, Df = (64, 64, 64)
        E, H, D = (8, 64, 64)
        s1 = 1.0 / np.sqrt(Df)
        s2 = 1.0 / np.sqrt(H)
        return {'x': jax.random.normal(ks[0], (B, F, Df), jnp.float32), 'Wr': jax.random.normal(ks[1], (Df, E), jnp.float32) * s1, 'br': jnp.zeros((E,), jnp.float32), 'W1': jax.random.normal(ks[2], (E, Df, H), jnp.float32) * s1, 'b1': jnp.zeros((E, H), jnp.float32), 'g1': jnp.ones((E, H), jnp.float32), 'be1': jnp.zeros((E, H), jnp.float32), 'm1': jnp.zeros((E, H), jnp.float32), 'v1': jnp.ones((E, H), jnp.float32), 'W2': jax.random.normal(ks[3], (E, H, H), jnp.float32) * s2, 'b2': jnp.zeros((E, H), jnp.float32), 'g2': jnp.ones((E, H), jnp.float32), 'be2': jnp.zeros((E, H), jnp.float32), 'm2': jnp.zeros((E, H), jnp.float32), 'v2': jnp.ones((E, H), jnp.float32), 'Wo': jax.random.normal(ks[4], (E, H, D), jnp.float32) * s2, 'bo': jnp.zeros((E, D), jnp.float32)}
    _L0_ffn_all = _L0_ffn_setup()
    _L0_ffn_in = {k: v for k, v in _L0_ffn_all.items() if k in ('Wr', 'br', 'W1', 'b1', 'g1', 'be1', 'm1', 'v1', 'W2', 'b2', 'g2', 'be2', 'm2', 'v2', 'Wo', 'bo')}
    del _L0_ffn_all
    return {'x': x, 'L0_tok_W1': _L0_tok_in['W1'], 'L0_tok_b1': _L0_tok_in['b1'], 'L0_tok_W2': _L0_tok_in['W2'], 'L0_tok_b2': _L0_tok_in['b2'], 'L0_tok_W3': _L0_tok_in['W3'], 'L0_tok_b3': _L0_tok_in['b3'], 'L0_attn_nu_log': _L0_attn_in['nu_log'], 'L0_attn_theta_log': _L0_attn_in['theta_log'], 'L0_attn_gamma_log': _L0_attn_in['gamma_log'], 'L0_attn_B_re': _L0_attn_in['B_re'], 'L0_attn_B_im': _L0_attn_in['B_im'], 'L0_attn_C_re': _L0_attn_in['C_re'], 'L0_attn_C_im': _L0_attn_in['C_im'], 'L0_attn_D': _L0_attn_in['D'], 'L0_ffn_Wr': _L0_ffn_in['Wr'], 'L0_ffn_br': _L0_ffn_in['br'], 'L0_ffn_W1': _L0_ffn_in['W1'], 'L0_ffn_b1': _L0_ffn_in['b1'], 'L0_ffn_g1': _L0_ffn_in['g1'], 'L0_ffn_be1': _L0_ffn_in['be1'], 'L0_ffn_m1': _L0_ffn_in['m1'], 'L0_ffn_v1': _L0_ffn_in['v1'], 'L0_ffn_W2': _L0_ffn_in['W2'], 'L0_ffn_b2': _L0_ffn_in['b2'], 'L0_ffn_g2': _L0_ffn_in['g2'], 'L0_ffn_be2': _L0_ffn_in['be2'], 'L0_ffn_m2': _L0_ffn_in['m2'], 'L0_ffn_v2': _L0_ffn_in['v2'], 'L0_ffn_Wo': _L0_ffn_in['Wo'], 'L0_ffn_bo': _L0_ffn_in['bo']}

def reference(x, L0_tok_W1, L0_tok_b1, L0_tok_W2, L0_tok_b2, L0_tok_W3, L0_tok_b3, L0_attn_nu_log, L0_attn_theta_log, L0_attn_gamma_log, L0_attn_B_re, L0_attn_B_im, L0_attn_C_re, L0_attn_C_im, L0_attn_D, L0_ffn_Wr, L0_ffn_br, L0_ffn_W1, L0_ffn_b1, L0_ffn_g1, L0_ffn_be1, L0_ffn_m1, L0_ffn_v1, L0_ffn_W2, L0_ffn_b2, L0_ffn_g2, L0_ffn_be2, L0_ffn_m2, L0_ffn_v2, L0_ffn_Wo, L0_ffn_bo):
    import jax
    import jax.numpy as jnp

    def _L0_tok_ref(x, W1, b1, W2, b2, W3, b3):
        import jax, jax.numpy as jnp
        import numpy as np
        B, C, H, W = (8, 64, 56, 56)
        K = 3

        def _unfold3x3(x):
            b, c, h, w = x.shape
            xp = jnp.pad(x, ((0, 0), (0, 0), (1, 1), (1, 1)))
            patches = jnp.stack([xp[:, :, i:i + h, j:j + w] for i in range(K) for j in range(K)], axis=2)
            return patches.reshape(b, c * K * K, h * w).transpose(0, 2, 1)
        t = _unfold3x3(x)
        h1 = jax.nn.relu(jnp.einsum('bld,dc->blc', t, W1) + b1)
        s = jax.nn.sigmoid(jnp.einsum('blc,cd->bld', h1, W2) + b2)
        out = jnp.einsum('bld,dc->blc', t * s, W3) + b3
        return out

    def _L0_attn_ref(inputs, nu_log, theta_log, gamma_log, B_re, B_im, C_re, C_im, D):
        import jax, jax.numpy as jnp
        import numpy as np
        import math
        B_SZ, L_SEQ, IN_DIM, D_MODEL, OUT_DIM = (8, 1024, 64, 128, 64)
        RMIN, RMAX = (0.8, 0.99)

        def _reference_tuple_inner(inputs, nu_log, theta_log, gamma_log, B_re, B_im, C_re, C_im, D):
            skip = jnp.einsum('blh,dh->bld', inputs, D)
            L = inputs.shape[1]
            A = jnp.exp(jax.lax.complex(-jnp.exp(nu_log), jnp.exp(theta_log)))
            Bc = jax.lax.complex(B_re, B_im) * jnp.exp(gamma_log)[:, None]
            u = jnp.einsum('blh,dh->bld', inputs.astype(jnp.complex64), Bc)
            H = A[:, None] ** jnp.arange(L)
            n = 2 * L
            h_f = jnp.fft.fft(H, n=n, axis=1)
            u_f = jnp.fft.fft(u, n=n, axis=1)
            x = jnp.fft.ifft(u_f * h_f.T, axis=1)[:, :L]
            y = jnp.einsum('blh,nh->bln', x, jax.lax.complex(C_re, C_im)).real + skip
            return (x, y)
        return _reference_tuple_inner(inputs, nu_log, theta_log, gamma_log, B_re, B_im, C_re, C_im, D)[1]

    def _L0_ffn_ref(x, Wr, br, W1, b1, g1, be1, m1, v1, W2, b2, g2, be2, m2, v2, Wo, bo):
        import jax, jax.numpy as jnp
        import numpy as np
        BN_EPS = 0.001

        def _bn(h, g, b, m, v):
            return g * (h - m) * jax.lax.rsqrt(v + BN_EPS) + b
        feat = jnp.mean(x, axis=0)
        w = jax.nn.softmax(feat @ Wr + br, axis=-1)
        h = jnp.einsum('bfd,edh->bfeh', x, W1) + b1
        h = jax.nn.relu(_bn(h, g1, be1, m1, v1))
        h = jnp.einsum('bfeh,ehk->bfek', h, W2) + b2
        h = jax.nn.relu(_bn(h, g2, be2, m2, v2))
        y = jnp.einsum('bfeh,ehd->bfed', h, Wo) + bo
        return jnp.einsum('bfed,fe->bfd', y, w)
    h = _L0_tok_ref(x, L0_tok_W1, L0_tok_b1, L0_tok_W2, L0_tok_b2, L0_tok_W3, L0_tok_b3)
    h = h + _L0_attn_ref(_layernorm(h, axis=-1), L0_attn_nu_log, L0_attn_theta_log, L0_attn_gamma_log, L0_attn_B_re, L0_attn_B_im, L0_attn_C_re, L0_attn_C_im, L0_attn_D)
    h = h + _L0_ffn_ref(_layernorm(h, axis=-1), L0_ffn_Wr, L0_ffn_br, L0_ffn_W1, L0_ffn_b1, L0_ffn_g1, L0_ffn_be1, L0_ffn_m1, L0_ffn_v1, L0_ffn_W2, L0_ffn_b2, L0_ffn_g2, L0_ffn_be2, L0_ffn_m2, L0_ffn_v2, L0_ffn_Wo, L0_ffn_bo)
    return h

_drawn_inputs = setup_inputs


def setup_inputs(seed=0):
    import zlib

    import numpy as np

    out = dict(_drawn_inputs(seed))
    spreads = {'L0_ffn_br': (0.0, 0.1),
     'L0_ffn_b1': (0.0, 0.328),
     'L0_ffn_g1': (1.0, 0.2),
     'L0_ffn_be1': (0.0, 0.312),
     'L0_ffn_m1': (0.0, 0.332),
     'L0_ffn_v1': (1.0, 0.555),
     'L0_ffn_b2': (0.0, 0.1),
     'L0_ffn_g2': (1.0, 0.2),
     'L0_ffn_be2': (0.0, 0.1),
     'L0_ffn_m2': (0.0, 0.1),
     'L0_ffn_v2': (1.0, 0.6),
     'L0_ffn_bo': (0.0, 0.1)}
    factors = {'L0_tok_b1': 8.0}
    for name, (base, spread) in spreads.items():
        noise = np.random.default_rng([zlib.crc32(name.encode()), seed]).standard_normal(out[name].shape)
        drawn = base * np.exp(spread * noise) if base else spread * noise
        out[name] = jnp.asarray(drawn.astype(out[name].dtype))
    for name, factor in factors.items():
        out[name] = (out[name] * factor).astype(out[name].dtype)
    return out
```

```python
from contextlib import ExitStack

import concourse.bass as bass
from concourse import mybir

F32 = mybir.dt.float32
ALU = mybir.AluOpType
ACT = mybir.ActivationFunctionType
AX_X = mybir.AxisListType.X

NB, C, HH, WW = 8, 64, 56, 56
PAIRS = HH // 2
TOK = NB * WW
TAPS = 9
NS = 128
T = 4
J = WW // T
BJ = NB * J
CH = 2 * J
NE = 8
NQ = NE // 2
LN_EPS = 1e-5
BN_EPS = 1e-3
FULL = 6
LAST = 5
GBANKS = 4
FILLS = 20

S_TILES = [("s", k) for k in range(9)]
L_TILES = [("l1", 0), ("l1", 1)]
for _k in range(8):
    if _k + 2 < 8:
        L_TILES.append(("l1", _k + 2))
    L_TILES.append(("l2", _k))
G_TILES = S_TILES + L_TILES
NG = len(G_TILES)
LAG = {"s": 1, "l1": 4, "l2": 4}
PER = {"s": 9, "l1": 8, "l2": 8}


def valid(step):
    return not isinstance(step, int) or 0 <= step < PAIRS


def g_bank(parity, idx):
    return (NG * parity + idx) % GBANKS


def g_previous(it, parity, idx):
    bank, back, i = g_bank(parity, idx), 0, idx - 1
    while back < 3:
        while i >= 0:
            kind, k = G_TILES[i]
            if g_bank((parity + back) % 2, i) == bank and valid(it - back - LAG[kind]):
                return kind, k, it - back - LAG[kind]
            i -= 1
        back, i = back + 1, NG - 1
    return None


def drive(eng, body):
    for it in range(FULL):
        body(it, it % 2)
    with eng.Fori(0, (PAIRS - FULL) // 2) as i:
        for k in range(2):
            body(2 * i + (FULL + k), (FULL + k) % 2)
    for it in range(PAIRS, PAIRS + LAST + 1):
        body(it, it % 2)


def after(eng, sem, step, per=1, n=None):
    if valid(step):
        eng.wait_ge(sem, per * step + (per if n is None else n))


def middle(ap, axis, n):
    v = ap.unsqueeze(axis)
    shape = list(v.shape)
    shape[axis] = n
    return v.broadcast_to(shape)


def build(nc, d, out):
    with ExitStack() as ctx:
        def sb(name, shape, dt=F32):
            return ctx.enter_context(nc.sbuf_tensor(name, shape, dt))

        def sem(name):
            return ctx.enter_context(nc.semaphore(name))

        bank = [ctx.enter_context(nc.psum_tensor(f"bank{i}", [128, 512], F32)) for i in range(8)]
        B_HO, B_FY, B_T, B_M = 4, 5, 6, 7

        ident = sb("ident", [128, 128])
        center = sb("center", [128, 128])
        emask = sb("emask", [16, 8])
        ehalf = sb("ehalf", [16, 128])
        pmask = sb("pmask", [16, 2])
        dup8 = sb("dup8", [8, 16])
        w_conv = sb("w_conv", [128, 6, 128])
        b1col = sb("b1col", [128, 1])
        w2raw = sb("w2raw", [128, C * TAPS])
        w_gate = sb("w_gate", [128, 6, 128])
        b2raw = sb("b2raw", [128, TAPS])
        b2col = sb("b2col", [128, 9])
        w_mixA = sb("w_mixA", [128, 2, 3, C])
        w_mixB = sb("w_mixB", [128, 3, 128])
        b3col = sb("b3col", [128, 1])
        logs = sb("logs", [128, 3])
        exps = sb("exps", [128, 3])
        mags = sb("mags", [128, 2])
        ang = sb("ang", [128, 4, 2])
        trig = sb("trig", [128, 2])
        lam = sb("lam", [128, 2, T + 1])
        nlam_i = sb("nlam_i", [128, T + 1])
        rot = sb("rot", [128, 2, CH + 2])
        stepper = sb("stepper", [128, 8, 3])
        small = sb("small", [128, 32])
        b_raw = sb("b_raw", [128, 2, 2, C])
        g_in = sb("g_in", [128, T, 2, 128])
        w_in = sb("w_in", [128, 2, T, NS])
        c_raw = sb("c_raw", [C, 2, NS])
        d_raw = sb("d_raw", [C, 2, C])
        ct = sb("ct", [128, 3, C])
        w_st = sb("w_st", [128, 2, T, C])
        w_lag = sb("w_lag", [128, T, 128])
        decay = sb("decay", [128, 2 * NB * (CH + 1)])
        bnrow = sb("bnrow", [128, 4, NE * C])
        bnhalf = sb("bnhalf", [128, NE * C])
        brow = sb("brow", [1, 6, NE * C])
        crow = sb("crow", [1, 2, NE * C])
        w_l1 = sb("w_l1", [128, NE * C])
        w_l2 = sb("w_l2", [128, NQ, 128])
        w_l3 = sb("w_l3", [128, NQ, C])
        c1col = sb("c1col", [128, NQ])
        nc2col = sb("nc2col", [128, NQ])
        c2m = sb("c2m", [128, NQ, 16])
        bo_raw = sb("bo_raw", [8, C])
        w_cst = sb("w_cst", [16, 128])
        wr_raw = sb("wr_raw", [128, NE])
        w_rt = sb("w_rt", [128, 16])
        br_row = sb("br_row", [1, 2, NE])
        ones_row = sb("ones_row", [1, 128])
        halfpow = sb("halfpow", [112, 8])

        xa = sb("xa", [128, 2, NB, WW + 2])
        xb = sb("xb", [128, 2, NB, WW + 2])
        h1 = sb("h1", [128, 2, TOK])
        gate = sb("gate", [128, 3, TOK])
        gated = sb("gated", [128, 3, TOK])
        h = sb("h", [128, 2, TOK])
        sq = sb("sq", [BJ, 2, 512])
        ssum = sb("ssum", [BJ, 2, 8])
        varr = sb("varr", [BJ, 2, 8])
        rstd = sb("rstd", [BJ, 2, 8])
        xnt = sb("xnt", [BJ, 2, 512])
        xn1 = sb("xn1", [128, 2, TOK])
        xn2 = sb("xn2", [128, 2, TOK])
        m_cos = sb("m_cos", [128, 2 * NB, CH])
        m_sin = sb("m_sin", [128, 2 * NB, CH])
        u = sb("u", [128, 2 * NB, CH + 1])
        z = sb("z", [128, 2 * NB, CH + 1])
        n_cos = sb("n_cos", [128, 2 * NB, CH])
        n_sin = sb("n_sin", [128, 2 * NB, CH])
        xst = sb("xst", [128, 2 * NB, CH])
        h2 = sb("h2", [128, 2, TOK])
        fsum = sb("fsum", [128, WW])
        lmax = sb("lmax", [WW, 2])
        lsub = sb("lsub", [WW, 16])
        lexp = sb("lexp", [WW, 16])
        lsum = sb("lsum", [WW, 2])
        lrec = sb("lrec", [WW, 2])
        wtok = sb("wtok", [128, 16])
        wmask = sb("wmask", [16, 8, WW])
        wts = sb("wts", [16, WW])
        wbs = sb("wbs", [128, 8, WW])
        z1 = sb("z1", [128, 4, TOK])
        z2 = sb("z2", [128, 4, TOK])
        fin = sb("fin", [128, TOK])
        ostage = sb("ostage", [BJ, 2, 2, T * C])

        (consts_in, tok_in, ssm_in, ffn_in, pads_zeroed, tok_weights, exps_ready, angles_ready, trig_ready, g_ready,
         win_turned, win_ready, ct_turned, ct_ready, lag_made, ssm_weights, bnvar_ready, bnpow_ready,
         crow_ready, ccol_made, c2m_ready, cst_made, ffn_weights, dve_chain) = [sem(n) for n in (
             "consts_in", "tok_in", "ssm_in", "ffn_in", "pads_zeroed", "tok_weights", "exps_ready", "angles_ready", "trig_ready",
             "g_ready", "win_turned", "win_ready", "ct_turned", "ct_ready", "lag_made", "ssm_weights",
             "bnvar_ready", "bnpow_ready", "crow_ready", "ccol_made", "c2m_ready", "cst_made", "ffn_weights", "dve_chain")]
        x_in = [sem("x_in0"), sem("x_in1")]
        stored = [sem("stored0"), sem("stored1")]
        (conv_done, h1_ready, s_done, gate_ready, gated_ready, mix_part, h_ready,
         ft_done, sq_ready, ssum_ready, var_ready, rstd_ready, xnt_ready, bt_done, xn_ready,
         u_done, m_ready, uin_ready, carry_a, carry_b, carry_ready, z_ready, n_ready, st_ready, y_done, h2_ready,
         fsum_ready, rt_done, lmax_ready, lsub_ready, lexp_ready, lsum_ready, lrec_ready, wtok_ready, wt_done, wmask_ready,
         wts_ready, wb_done, wbs_ready, l1_done, z1_ready, l2_done, z2_ready, l3_part, o_done, fin_ready,
         ot_done, out_ready) = [sem(n) for n in (
             "conv_done", "h1_ready", "s_done", "gate_ready", "gated_ready", "mix_part", "h_ready",
             "ft_done", "sq_ready", "ssum_ready", "var_ready", "rstd_ready", "xnt_ready", "bt_done", "xn_ready",
             "u_done", "m_ready", "uin_ready", "carry_a", "carry_b", "carry_ready", "z_ready", "n_ready", "st_ready", "y_done",
             "h2_ready", "fsum_ready", "rt_done", "lmax_ready", "lsub_ready", "lexp_ready", "lsum_ready", "lrec_ready", "wtok_ready",
             "wt_done", "wmask_ready", "wts_ready", "wb_done", "wbs_ready", "l1_done", "z1_ready", "l2_done",
             "z2_ready", "l3_part", "o_done", "fin_ready", "ot_done", "out_ready")]
        ft_done = [ft_done, sem("ft_done2")]
        sq_ready = [sq_ready, sem("sq_ready2")]
        ssum_ready = [ssum_ready, sem("ssum_ready2")]
        var_ready = [var_ready, sem("var_ready2")]
        rstd_ready = [rstd_ready, sem("rstd_ready2")]
        xnt_ready = [xnt_ready, sem("xnt_ready2")]
        bt_done = [bt_done, sem("bt_done2")]
        xn_ready = [xn_ready, sem("xn_ready2")]

        x_rows = d["x"].rearrange("b c (p q) w -> q p c b w", q=2)
        o_rows = out.rearrange("b (p q j t) c -> q p b j (t c)", q=2, j=J, t=T)
        w1v = d["L0_tok_W1"].rearrange("(c ki kj) n -> c ki kj n", ki=3, kj=3)
        w3v = d["L0_tok_W3"].rearrange("(c ki kj) n -> c ki kj n", ki=3, kj=3)
        halves = (slice(0, 64), slice(64, 128))

        N_CONST, N_TOK, N_SSM, N_FFN = 6, 19, 11, 24
        loads = {"consts": 0, "tok": 0, "ssm": 0, "ffn": 0}

        block = ctx.enter_context(nc.Block())

        @block.sync
        def _(sp):
            def load_x(s, q):
                if not valid(s):
                    return
                if not (isinstance(s, int) and s < 2):
                    after(sp, conv_done, s - 2)
                    after(sp, gated_ready, s - 2, 9)
                sp.dma_start(xa[0:64, q, :, 1:WW + 1], x_rows[0][s]).then_inc(x_in[q], 16)
                sp.dma_start(xa[64:128, q, :, 1:WW + 1], x_rows[1][s]).then_inc(x_in[q], 16)
                if isinstance(s, int) and s == PAIRS - 1:
                    sp.wait_ge(pads_zeroed, FILLS)
                    sp.dma_start(xb[0:64, q, :, 1:WW + 1], xz_view()).then_inc(x_in[q], 16)
                else:
                    sp.dma_start(xb[0:64, q, :, 1:WW + 1], x_rows[0][s + 1]).then_inc(x_in[q], 16)
                if isinstance(s, int) and s == 0:
                    sp.dma_start(xb[64:128, q, :, 1:WW + 1], xz_view()).then_inc(x_in[q], 16)
                else:
                    sp.dma_start(xb[64:128, q, :, 1:WW + 1], x_rows[1][s - 1]).then_inc(x_in[q], 16)

            def xz_view():
                return d["zeros"].rearrange("c (b w) -> c b w", b=NB)

            for s in range(2):
                load_x(s, s)

            def ld(group, dst, src):
                loads[group] += 1
                sp.dma_start(dst, src).then_inc({"consts": consts_in, "tok": tok_in, "ssm": ssm_in, "ffn": ffn_in}[group], 16)

            for dst, name in ((ident, "ident"), (center, "center"), (emask, "emask"), (ehalf, "ehalf"), (pmask, "pmask"),
                              (dup8, "dup8")):
                ld("consts", dst[:], d[name])
            for half, col, ki in ((0, 0, 1), (0, 1, 0), (1, 0, 2), (1, 1, 1)):
                ld("tok", w_conv[halves[half], 0:3, halves[col]], w1v[:, ki])
                ld("tok", w_mixA[halves[half], col], w3v[:, ki])
            ld("tok", w_conv[0:64, 3:6, 64:128], w1v[:, 2])
            ld("tok", w_conv[64:128, 3:6, 0:64], w1v[:, 0])
            ld("tok", w_mixB[0:64, :, 64:128], w3v[:, 2])
            ld("tok", w_mixB[64:128, :, 0:64], w3v[:, 0])
            for hf in halves:
                ld("tok", w2raw[hf, :], d["L0_tok_W2"])
                ld("tok", b2raw[hf, :], d["L0_tok_b2"].rearrange("(c k) -> c k", k=TAPS))
                ld("tok", b1col[hf, :], d["L0_tok_b1"].rearrange("(c k) -> c k", k=1))
            ld("tok", b3col[halves[0], :], d["L0_tok_b3"].rearrange("(c k) -> c k", k=1))
            ld("ssm", b3col[halves[1], :], d["L0_tok_b3"].rearrange("(c k) -> c k", k=1))
            for k, n in enumerate(("nu_log", "theta_log", "gamma_log")):
                ld("ssm", logs[:, k:k + 1], d[f"L0_attn_{n}"].rearrange("(c k) -> c k", k=1))
            for k, n in enumerate(("re", "im")):
                for hf in range(2):
                    ld("ssm", b_raw[:, k, hf, :], d[f"L0_attn_B_{n}"])
                ld("ssm", c_raw[:, k, :], d[f"L0_attn_C_{n}"])
            ld("ssm", d_raw[:, 0, :], d["L0_attn_D"])
            for k, n in enumerate(("g1", "v1", "g2", "v2")):
                ld("ffn", bnrow[:, k, :], d[f"L0_ffn_{n}"].rearrange("e h -> (e h)").partition_broadcast(128))
            for k, n in enumerate(("b1", "m1", "be1", "b2", "m2", "be2")):
                ld("ffn", brow[:, k, :], d[f"L0_ffn_{n}"].rearrange("(o e) h -> o (e h)", o=1))
            for hf in halves:
                ld("ffn", w_l1[hf, :].rearrange("p (e h) -> p e h", e=NE), d["L0_ffn_W1"].rearrange("e d h -> d e h"))
                ld("ffn", wr_raw[hf, :], d["L0_ffn_Wr"])
            w2v = d["L0_ffn_W2"].rearrange("(q e) h k -> e h q k", e=2)
            for e in range(2):
                ld("ffn", w_l2[halves[e], :, halves[e]], w2v[e])
            ld("ffn", w_l3[0:64], d["L0_ffn_Wo"].rearrange("(q e) h k -> e h q k", e=2)[0])
            ld("ffn", w_l3[64:128], d["L0_ffn_Wo"].rearrange("(q e) h k -> e h q k", e=2)[1])
            ld("ffn", bo_raw[:], d["L0_ffn_bo"])
            for k in range(2):
                ld("ffn", br_row[:, k, :], d["L0_ffn_br"].rearrange("(o e) -> o e", o=1))
            ld("ssm", d_raw[:, 1, :], d["L0_attn_D"])

            def store(s, q):
                if valid(s):
                    after(sp, out_ready, s)
                    for par in range(2):
                        sp.dma_start(o_rows[par][s], ostage[:, q, par, :]).then_inc(stored[q], 16)

            def body(it, q):
                store(it - 5 if isinstance(it, int) else it - 5, (q + 1) % 2)
                load_x(it + 1 if isinstance(it, int) else it + 1, (q + 1) % 2) if it is not None else None

            def body_io(it, q):
                s = it + 1
                if not isinstance(s, int) or s >= 2:
                    load_x(s, (q + 1) % 2)
                store(it - 5, (q + 1) % 2)

            for it in range(FULL):
                body_io(it, it % 2)
            with sp.Fori(0, (PAIRS - FULL) // 2 - 1) as i:
                for k in range(2):
                    body_io(2 * i + (FULL + k), (FULL + k) % 2)
            for it in range(PAIRS - 2, PAIRS + LAST + 1):
                body_io(it, it % 2)
            for q in range(2):
                sp.wait_ge(stored[q], 16 * PAIRS)

        @block.gpsimd
        def _(pool):
            fills = [(xa[:, :, :, 0:1], 0.0), (xa[:, :, :, WW + 1:WW + 2], 0.0), (xb[:, :, :, 0:1], 0.0),
                     (xb[:, :, :, WW + 1:WW + 2], 0.0), (w_conv[0:64, 3:6, 0:64], 0.0), (w_conv[64:128, 3:6, 64:128], 0.0),
                     (w_mixB[0:64, :, 0:64], 0.0), (w_mixB[64:128, :, 64:128], 0.0), (w_gate[0:64, 3:6, 0:64], 0.0),
                     (w_gate[64:128, 3:6, 64:128], 0.0), (w_lag[:], 0.0), (w_l2[0:64, :, 64:128], 0.0),
                     (w_l2[64:128, :, 0:64], 0.0), (c2m[:], 0.0), (wtok[:], 0.0), (w_rt[:], 0.0), (ones_row[:], 1.0),
                     (u[:], 0.0), (halfpow[:], -0.5), (bnhalf[:], -0.5)]
            assert len(fills) == FILLS
            for k, (tile, value) in enumerate(fills):
                nc.gpsimd.memset(tile, value).then_inc(pads_zeroed, 1)
                pool.wait_ge(pads_zeroed, k + 1)
            pool.wait_ge(bnvar_ready, 1)
            for k in (1, 3):
                nc.gpsimd.tensor_tensor(bnrow[:, k, :], bnrow[:, k, :], bnhalf[:], ALU.pow).then_inc(bnpow_ready, 1)
            pool.wait_ge(bnpow_ready, 2)

            def body(it, q):
                b, y = it - 2, it - 3
                if valid(b):
                    after(pool, var_ready[0], b)
                    after(pool, xnt_ready[0], b - 1)
                    nc.gpsimd.tensor_tensor(rstd[:, 0, :], varr[:, 0, :], halfpow[:], ALU.pow).then_inc(rstd_ready[0], 1)
                if valid(y):
                    after(pool, var_ready[1], y)
                    after(pool, xnt_ready[1], y - 1)
                    nc.gpsimd.tensor_tensor(rstd[:, 1, :], varr[:, 1, :], halfpow[:], ALU.pow).then_inc(rstd_ready[1], 1)
                if valid(b):
                    after(pool, m_ready, b, 4)
                    after(pool, z_ready, b - 1)
                    nc.gpsimd.tensor_tensor(u[:, 0:NB, 1:], m_cos[:, 0:NB], m_sin[:, NB:], ALU.add).then_inc(uin_ready, 1)
                    nc.gpsimd.tensor_tensor(u[:, NB:, 1:], m_cos[:, NB:], m_sin[:, 0:NB], ALU.subtract).then_inc(uin_ready, 1)
                    after(pool, n_ready, b, 2)
                    after(pool, y_done, b - 1)
                    nc.gpsimd.tensor_tensor(xst[:, 0:NB], n_cos[:, 0:NB], n_sin[:, NB:], ALU.subtract).then_inc(st_ready, 1)
                    nc.gpsimd.tensor_tensor(xst[:, NB:], n_cos[:, NB:], n_sin[:, 0:NB], ALU.add).then_inc(st_ready, 1)

            drive(pool, body)

        @block.scalar
        def _(act):
            act.wait_ge(ssm_in, 16 * loads["ssm"])
            nc.scalar.activation(exps[:], logs[:], ACT.Exp).then_inc(exps_ready, 1)
            act.wait_ge(exps_ready, 1)
            nc.scalar.activation(mags[:, 0:1], exps[:, 0:1], ACT.Exp, scale=-1.0)
            nc.scalar.activation(mags[:, 1:2], exps[:, 0:1], ACT.Exp, scale=-float(T)).then_inc(exps_ready, 1)
            act.wait_ge(angles_ready, 1)
            nc.scalar.activation(trig[:], ang[:, 3, :], ACT.Sin).then_inc(trig_ready, 1)
            act.wait_ge(win_turned, 2)
            for k in range(T):
                for c in range(2):
                    nc.scalar.copy(w_in[:, c, T - 1 - k, :], bank[k // 2][:, (2 * (k % 2) + c) * 128:(2 * (k % 2) + c) * 128 + 128])
            nc.scalar.copy(small[:, 31:32], exps[:, 0:1]).then_inc(win_ready, 1)
            act.wait_ge(tok_weights, 1)

            def square(ln, s, q):
                if valid(s):
                    after(act, ft_done[ln], s)
                    after(act, ssum_ready[ln], s - 1)
                    nc.scalar.activation(sq[:, ln, :], bank[B_T][0:BJ, :], ACT.Square).then_inc(sq_ready[ln], 1)

            def turned_back(ln, s, q, dst):
                if valid(s):
                    after(act, bt_done[ln], s)
                    v = bank[B_M][:, 0:TOK].rearrange("p (t g) -> p g t", t=T)
                    nc.scalar.copy(dst[:, q, :].rearrange("p (g t) -> p g t", t=T), v).then_inc(xn_ready[ln], 1)

            def body(it, q):
                c, a, b, y, dd, f = it, it - 1, it - 2, it - 3, it - 4, it - 5
                r = (q + 1) % 2
                if valid(dd):
                    after(act, lsub_ready, dd)
                    after(act, lsum_ready, dd - 1)
                    nc.scalar.activation(lexp[:], lsub[:], ACT.Exp).then_inc(lexp_ready, 1)
                square(0, b, q)

                def tanh(k):
                    if valid(a):
                        after(act, s_done, a, 9, k + 1)
                        after(act, gated_ready, a if k >= 3 else a - 1, 9, k - 2 if k >= 3 else k + 7)
                        g = bank[g_bank(q, k)][:, 0:TOK]
                        nc.scalar.activation(gate[:, k % 3, :], g, ACT.Tanh, bias=b2col[:, k:k + 1], scale=0.5)\
                            .then_inc(gate_ready, 1)

                for k in range(3):
                    tanh(k)
                if valid(f):
                    after(act, ot_done, f)
                    if valid(f - 2):
                        act.wait_ge(stored[r], 32 * (((f - 2) if isinstance(f, int) else f - 2) // 2) + 32) \
                            if isinstance(f, int) else act.wait_ge(stored[r], 16 * (f - 2) + (32 if r == 0 else 16))
                    nc.scalar.copy(ostage[:, r].rearrange("p q (t c) -> p t q c", t=T),
                                   bank[B_FY][0:BJ, :].rearrange("p (t q c) -> p t q c", t=T, q=2)).then_inc(out_ready, 1)
                for k in range(3, 6):
                    tanh(k)
                if valid(dd):
                    after(act, wb_done, dd)
                    after(act, z2_ready, dd - 1, 8)
                    nc.scalar.copy(wbs[:], bank[B_M][:, 0:TOK].rearrange("p (q x) -> p q x", q=8)).then_inc(wbs_ready, 1)
                square(1, y, r)
                for k in range(6, 9):
                    tanh(k)
                if valid(b):
                    after(act, y_done, b - 2)
                turned_back(0, b, q, xn1)
                if valid(c):
                    after(act, conv_done, c)
                    after(act, s_done, c - 2, 9)
                    nc.scalar.activation(h1[:, q, :], bank[B_FY][:, 0:TOK], ACT.Relu, bias=b1col[:, 0:1]).then_inc(h1_ready, 1)
                if valid(a):
                    after(act, mix_part, a, 9)
                    after(act, h2_ready, a - 2)
                    nc.scalar.activation(h[:, r, :], bank[B_HO][:, 0:TOK], ACT.Identity, bias=b3col[:, 0:1]).then_inc(h_ready, 1)
                for k in range(8):
                    if k == 4 and valid(y):
                        after(act, l1_done, y - 2, 8)
                        turned_back(1, y, r, xn2)
                    if valid(dd):
                        after(act, l1_done, dd, 8, k + 1)
                        after(act, l2_done, dd if k >= 4 else dd - 1, 8, k - 3 if k >= 4 else k + 5)
                        g = bank[g_bank(q, G_TILES.index(("l1", k)))][:, 0:TOK]
                        nc.scalar.activation(z1[:, k % 4, :], g, ACT.Relu, bias=c1col[:, k // 2:k // 2 + 1])\
                            .then_inc(z1_ready, 1)
                    elif k == 4 and not valid(y):
                        pass

            act.wait_ge(ffn_weights, 1)
            drive(act, body)

        @block.vector
        def _(dve):
            chain = [0]

            def link(ins):
                chain[0] += 1
                ins.then_inc(dve_chain, 1)
                dve.wait_ge(dve_chain, chain[0])

            V = nc.vector
            dve.wait_ge(pads_zeroed, FILLS)
            dve.wait_ge(tok_in, 16 * loads["tok"])
            w2t = w2raw[:].rearrange("p (c ki kj) -> p ki kj c", ki=3, kj=3)
            b2t = b2raw[:].rearrange("p (ki kj) -> p ki kj", ki=3)
            b2o = b2col[:].rearrange("p (kj k) -> p k kj", k=3)
            for half, col, ki in ((0, 0, 1), (0, 1, 2), (1, 0, 0), (1, 1, 1)):
                V.tensor_copy(w_gate[halves[half], 0:3, halves[col]], w2t[halves[half], ki])
                V.tensor_scalar(b2o[halves[col], half], b2t[halves[col], ki], 0.5, None, ALU.mult)
            V.tensor_copy(w_gate[0:64, 3:6, 64:128], w2t[0:64, 0])
            V.tensor_copy(w_gate[64:128, 3:6, 0:64], w2t[64:128, 2])
            V.tensor_scalar(b2o[0:64, 2], b2t[0:64, 2], 0.5, None, ALU.mult)
            V.tensor_scalar(b2o[64:128, 2], b2t[64:128, 0], 0.5, None, ALU.mult)
            V.tensor_scalar(w_mixB[:], w_mixB[:], 0.5, None, ALU.mult)
            V.tensor_scalar(w_mixA[:], w_mixA[:], 0.5, None, ALU.mult).then_inc(tok_weights, 1)

            dve.wait_ge(exps_ready, 2)
            TWO_PI_HI, TWO_PI_LO, MAGIC = 6.28125, 0.0019353071795864769, 12582912.0
            link(V.tensor_copy(ang[:, 0, 0:1], exps[:, 1:2]))
            link(V.tensor_scalar(ang[:, 0, 1:2], exps[:, 1:2], 1.5707963267948966, None, ALU.add))
            link(V.tensor_scalar(ang[:, 1, :], ang[:, 0, :], 0.15915494309189535, MAGIC, ALU.mult, ALU.add))
            link(V.tensor_scalar(ang[:, 1, :], ang[:, 1, :], MAGIC, None, ALU.subtract))
            link(V.scalar_tensor_tensor(ang[:, 2, :], ang[:, 1, :], -TWO_PI_HI, ang[:, 0, :], ALU.mult, ALU.add))
            link(V.scalar_tensor_tensor(ang[:, 3, :], ang[:, 1, :], -TWO_PI_LO, ang[:, 2, :], ALU.mult, ALU.add))
            V.tensor_scalar(ang[:, 3, :], ang[:, 3, :], 3.1415925, -3.1415925, ALU.min, ALU.max).then_inc(angles_ready, 1)
            dve.wait_ge(trig_ready, 1)

            def times(dst_r, dst_i, xr, xi, sr, si, nsi, width):
                link(V.tensor_scalar(small[:, 0:width], xr, sr, None, ALU.mult))
                link(V.scalar_tensor_tensor(dst_r, xi, nsi, small[:, 0:width], ALU.mult, ALU.add))
                link(V.tensor_scalar(small[:, 0:width], xi, sr, None, ALU.mult))
                link(V.scalar_tensor_tensor(dst_i, xr, si, small[:, 0:width], ALU.mult, ALU.add))

            link(V.memset(lam[:, 0, 0:1], 1.0))
            link(V.memset(lam[:, 1, 0:1], 0.0))
            link(V.tensor_scalar(lam[:, 0, 1:2], trig[:, 1:2], mags[:, 0:1], None, ALU.mult))
            link(V.tensor_scalar(lam[:, 1, 1:2], trig[:, 0:1], mags[:, 0:1], None, ALU.mult))
            link(V.tensor_scalar(nlam_i[:, 1:2], lam[:, 1, 1:2], -1.0, None, ALU.mult))
            for k in range(2, T + 1):
                times(lam[:, 0, k:k + 1], lam[:, 1, k:k + 1], lam[:, 0, k - 1:k], lam[:, 1, k - 1:k],
                      lam[:, 0, 1:2], lam[:, 1, 1:2], nlam_i[:, 1:2], 1)
            link(V.tensor_scalar(nlam_i[:], lam[:, 1, :], -1.0, None, ALU.mult))

            def square_of(dst, src):
                s = [stepper[:, src, c:c + 1] for c in range(3)]
                times(stepper[:, dst, 0:1], stepper[:, dst, 1:2], s[0], s[1], s[0], s[1], s[2], 1)
                link(V.tensor_scalar(stepper[:, dst, 2:3], stepper[:, dst, 1:2], -1.0, None, ALU.mult))

            link(V.tensor_copy(stepper[:, 0, 0:1], trig[:, 1:2]))
            link(V.tensor_copy(stepper[:, 0, 1:2], trig[:, 0:1]))
            link(V.tensor_scalar(stepper[:, 0, 2:3], trig[:, 0:1], -1.0, None, ALU.mult))
            for m in range(1, 7):
                square_of(m, m - 1)
            link(V.tensor_copy(rot[:, 0, 0:1], stepper[:, 2, 0:1]))
            link(V.tensor_copy(rot[:, 1, 0:1], stepper[:, 2, 2:3]))
            link(V.memset(rot[:, 0, 1:2], 1.0))
            link(V.memset(rot[:, 1, 1:2], 0.0))
            n = 1
            while n < CH + 1:
                w = min(n, CH + 1 - n)
                s = [stepper[:, 2 + n.bit_length() - 1, c:c + 1] for c in range(3)]
                times(rot[:, 0, 1 + n:1 + n + w], rot[:, 1, 1 + n:1 + n + w], rot[:, 0, 1:1 + w], rot[:, 1, 1:1 + w],
                      s[0], s[1], s[2], w)
                n += w
            link(V.tensor_scalar(stepper[:, 7, 0:1], rot[:, 1, CH + 1:CH + 2], -1.0, None, ALU.mult))
            turn_r, turn_i, nturn_i = rot[:, 0, CH + 1:CH + 2], rot[:, 1, CH + 1:CH + 2], stepper[:, 7, 0:1]

            link(V.memset(decay[:], 0.0))
            dv = decay[:].rearrange("p (g c) -> p g c", c=CH + 1)
            link(V.tensor_scalar(dv[:, :, 1:], dv[:, :, 1:], mags[:, 1:2], None, ALU.add))

            br, bi = b_raw[:, 0].rearrange("p a c -> p (a c)"), b_raw[:, 1].rearrange("p a c -> p (a c)")
            link(V.tensor_scalar(g_in[:, 0, 0, :], br, exps[:, 2:3], None, ALU.mult))
            link(V.tensor_scalar(g_in[:, 0, 1, :], bi, exps[:, 2:3], None, ALU.mult))
            for k in range(1, T):
                lr, li, nli = lam[:, 0, k:k + 1], lam[:, 1, k:k + 1], nlam_i[:, k:k + 1]
                link(V.tensor_scalar(xst[:, 0:8, 0:16], g_in[:, 0, 0, :].rearrange("p (a c) -> p a c", a=8), lr, None, ALU.mult))
                link(V.scalar_tensor_tensor(g_in[:, k, 0, :].rearrange("p (a c) -> p a c", a=8),
                                            g_in[:, 0, 1, :].rearrange("p (a c) -> p a c", a=8), nli, xst[:, 0:8, 0:16],
                                            ALU.mult, ALU.add))
                link(V.tensor_scalar(xst[:, 0:8, 0:16], g_in[:, 0, 1, :].rearrange("p (a c) -> p a c", a=8), lr, None, ALU.mult))
                link(V.scalar_tensor_tensor(g_in[:, k, 1, :].rearrange("p (a c) -> p a c", a=8),
                                            g_in[:, 0, 0, :].rearrange("p (a c) -> p a c", a=8), li, xst[:, 0:8, 0:16],
                                            ALU.mult, ALU.add))
            V.tensor_copy(small[:, 30:31], lam[:, 0, 0:1]).then_inc(g_ready, 1)
            dve.wait_ge(ct_turned, 1)
            link(V.tensor_copy(ct[:, 0:2, :], bank[2][:, 0:128].rearrange("p (a c) -> p a c", a=2)))
            link(V.tensor_scalar(ct[:, 2, :], ct[:, 1, :], -1.0, None, ALU.mult))
            V.tensor_copy(small[:, 29:30], lam[:, 0, 0:1]).then_inc(ct_ready, 1)
            for t in range(T):
                lr, li, nli = lam[:, 0, t + 1:t + 2], lam[:, 1, t + 1:t + 2], nlam_i[:, t + 1:t + 2]
                link(V.tensor_scalar(w_st[:, 0, t, :], ct[:, 0, :], lr, None, ALU.mult))
                link(V.scalar_tensor_tensor(w_st[:, 0, t, :], ct[:, 1, :], nli, w_st[:, 0, t, :], ALU.mult, ALU.add))
                link(V.tensor_scalar(w_st[:, 1, t, :], ct[:, 0, :], nli, None, ALU.mult))
                link(V.scalar_tensor_tensor(w_st[:, 1, t, :], ct[:, 2, :], lr, w_st[:, 1, t, :], ALU.mult, ALU.add))
            dve.wait_ge(lag_made, 1)
            for hf in halves:
                link(V.tensor_copy(w_lag[hf, :, hf], bank[3][hf, 0:T * C].rearrange("p (k c) -> p k c", k=T)))
            V.tensor_copy(small[:, 28:29], lam[:, 0, 0:1]).then_inc(ssm_weights, 1)

            dve.wait_ge(ffn_in, 16 * loads["ffn"])
            link(V.tensor_scalar(bnrow[:, 1, :], bnrow[:, 1, :], BN_EPS, None, ALU.add))
            V.tensor_scalar(bnrow[:, 3, :], bnrow[:, 3, :], BN_EPS, None, ALU.add).then_inc(bnvar_ready, 1)
            dve.wait_ge(bnpow_ready, 2)
            for k in (0, 2):
                link(V.tensor_tensor(bnrow[:, k, :], bnrow[:, k, :], bnrow[:, k + 1, :], ALU.mult))
            link(V.tensor_tensor(w_l1[:], w_l1[:], bnrow[:, 0, :], ALU.mult))
            a2 = bnrow[:, 2, :].rearrange("p (q k) -> p q k", q=NQ)
            link(V.tensor_tensor(w_l2[:], w_l2[:], a2, ALU.mult))
            for k in range(2):
                link(V.tensor_tensor(crow[:, k, :], brow[:, 3 * k, :], brow[:, 3 * k + 1, :], ALU.subtract))
                link(V.tensor_tensor(crow[:, k, :], crow[:, k, :], bnrow[0:1, 2 * k, :], ALU.mult))
                link(V.tensor_tensor(crow[:, k, :], crow[:, k, :], brow[:, 3 * k + 2, :], ALU.add))
            V.tensor_scalar(br_row[:], br_row[:], 1.0, None, ALU.mult).then_inc(crow_ready, 1)
            dve.wait_ge(ccol_made, 1)
            link(V.tensor_copy(c1col[:], bank[4][:, 0:NQ]))
            link(V.tensor_scalar(nc2col[:], bank[4][:, NQ:2 * NQ], -1.0, None, ALU.mult))
            for e, hf in enumerate(halves):
                for qq in range(NQ):
                    dst = c2m[hf, qq, :].rearrange("p (r e) -> p r e", r=2)[:, :, 2 * qq + e:2 * qq + e + 1]
                    link(V.tensor_copy(dst, middle(bank[4][hf, NQ + qq:NQ + qq + 1], 1, 2)))
            for k, hf in enumerate(halves):
                link(V.tensor_scalar(w_rt[hf, NE * k:NE * k + NE], wr_raw[hf, :], 1.0 / NB, None, ALU.mult))
            V.tensor_copy(small[:, 27:28], lam[:, 0, 0:1]).then_inc(c2m_ready, 1)
            dve.wait_ge(cst_made, 1)
            dve.wait_ge(consts_in, 16 * loads["consts"])
            for k, hf in enumerate(halves):
                link(V.tensor_scalar(w_cst[:, hf], bank[5][0:16, 0:C], pmask[:, k:k + 1], None, ALU.mult))
            V.tensor_copy(small[:, 26:27], lam[:, 0, 0:1]).then_inc(ffn_weights, 1)

            hct = bank[B_T][0:BJ, :].rearrange("p (g c) -> p g c", c=C)

            def variance(ln, s):
                if valid(s):
                    after(dve, sq_ready[ln], s)
                    V.tensor_reduce(ssum[:, ln, :], sq[:, ln, :].rearrange("p (g c) -> p g c", c=C), AX_X, ALU.add)\
                        .then_inc(ssum_ready[ln], 1)
                    after(dve, ssum_ready[ln], s)
                    after(dve, rstd_ready[ln], s - 1)
                    V.tensor_scalar(varr[:, ln, :], ssum[:, ln, :], 1.0 / C, LN_EPS, ALU.mult, ALU.add)\
                        .then_inc(var_ready[ln], 1)

            def normalise(ln, s):
                if valid(s):
                    after(dve, rstd_ready[ln], s)
                    after(dve, bt_done[ln], s - 1)
                    V.tensor_tensor(xnt[:, ln, :].rearrange("p (g c) -> p g c", c=C), hct, middle(rstd[:, ln, :], 2, C),
                                    ALU.mult).then_inc(xnt_ready[ln], 1)

            def body(it, q):
                c, a, b, y, dd, f = it, it - 1, it - 2, it - 3, it - 4, it - 5
                r = (q + 1) % 2
                if valid(dd):
                    lg = bank[B_M][0:WW, 0:16].rearrange("p (r e) -> p r e", r=2)
                    after(dve, rt_done, dd)
                    V.tensor_reduce(lmax[:], lg, AX_X, ALU.max).then_inc(lmax_ready, 1)
                    after(dve, lmax_ready, dd)
                    V.tensor_tensor(lsub[:].rearrange("p (r e) -> p r e", r=2), lg, middle(lmax[:], 2, NE), ALU.subtract)\
                        .then_inc(lsub_ready, 1)
                variance(0, b)
                if valid(dd):
                    after(dve, lexp_ready, dd)
                    V.tensor_reduce(lsum[:], lexp[:].rearrange("p (r e) -> p r e", r=2), AX_X, ALU.add).then_inc(lsum_ready, 1)
                    after(dve, lsum_ready, dd)
                    V.reciprocal(lrec[:], lsum[:]).then_inc(lrec_ready, 1)
                    after(dve, lrec_ready, dd)
                    after(dve, wt_done, dd - 1)
                    V.tensor_tensor(wtok[0:WW, :].rearrange("p (r e) -> p r e", r=2), lexp[:].rearrange("p (r e) -> p r e", r=2),
                                    middle(lrec[:], 2, NE), ALU.mult).then_inc(wtok_ready, 1)
                normalise(0, b)

                def gating(k):
                    if valid(a):
                        if k == 0:
                            pass
                        after(dve, gate_ready, a, 9, k + 1)
                        after(dve, mix_part, a if k >= 3 else a - 1, 9, k - 2 if k >= 3 else k + 7)
                        src = (xb if k % 3 == 2 else xa)[:, r, :, k // 3:k // 3 + WW]
                        V.scalar_tensor_tensor(gated[:, k % 3, :].rearrange("p (b w) -> p b w", b=NB),
                                               gate[:, k % 3, :].rearrange("p (b w) -> p b w", b=NB), 1.0, src,
                                               ALU.add, ALU.mult).then_inc(gated_ready, 1)

                for k in range(3):
                    gating(k)
                if valid(dd):
                    after(dve, wt_done, dd)
                    after(dve, wb_done, dd - 1)
                    V.tensor_tensor(wmask[:], middle(bank[B_M][0:16, 64:64 + WW], 1, 8), middle(emask[:], 2, WW), ALU.mult)\
                        .then_inc(wmask_ready, 1)
                    after(dve, o_done, dd - 1)
                    V.tensor_copy(wts[:], bank[B_M][0:16, 64:64 + WW]).then_inc(wts_ready, 1)
                if valid(y):
                    after(dve, y_done, y)
                    after(dve, fin_ready, y - 2)
                    after(dve, ft_done[1], y - 2)
                    V.tensor_tensor(h2[:, r, :], bank[B_FY][:, 0:TOK], h[:, r, :], ALU.add)\
                        .then_inc(h2_ready, 1)
                for k in range(3, 6):
                    gating(k)
                variance(1, y)
                gating(6)
                normalise(1, y)
                for k in range(7, 9):
                    gating(k)

                def expert(k):
                    if valid(dd):
                        after(dve, l2_done, dd, 8, k + 1)
                        after(dve, l3_part, dd if k >= 4 else dd - 1, 8, k - 3 if k >= 4 else k + 5)
                        if k == 0:
                            after(dve, wbs_ready, dd)
                        g = bank[g_bank(q, G_TILES.index(("l2", k)))][:, 0:TOK]
                        V.scalar_tensor_tensor(z2[:, k % 4, :].rearrange("p (b x) -> p b x", b=NB),
                                               g.rearrange("p (b x) -> p b x", b=NB), nc2col[:, k // 2:k // 2 + 1],
                                               middle(wbs[:, k, :], 1, NB), ALU.max, ALU.mult).then_inc(z2_ready, 1)

                if valid(b):
                    after(dve, uin_ready, b - 1, 2)
                    for par in range(2):
                        src = bank[B_T + par][:, 0:2 * BJ].rearrange("p (g j) -> p g j", j=J)
                        after(dve, u_done, b, 2, par + 1)
                        for dst, tr in ((m_cos, 0), (m_sin, 1)):
                            V.tensor_tensor(dst[:, :, J * par:J * par + J], src,
                                            middle(rot[:, tr, 1 + J * par:1 + J * par + J], 1, 2 * NB), ALU.mult)\
                                .then_inc(m_ready, 1)
                    if not (isinstance(b, int) and b == 0):
                        zl = z[:, :, CH:CH + 1].rearrange("p (k b) o -> p k (b o)", k=2)
                        uf = u[:, :, 0:1].rearrange("p (k b) o -> p k (b o)", k=2)
                        V.tensor_scalar(uf, zl, turn_r, None, ALU.mult).then_inc(carry_a, 1)
                        after(dve, carry_a, b - 1)
                        V.scalar_tensor_tensor(uf[:, 0], zl[:, 1], nturn_i, uf[:, 0], ALU.mult, ALU.add).then_inc(carry_b, 1)
                        V.scalar_tensor_tensor(uf[:, 1], zl[:, 0], turn_i, uf[:, 1], ALU.mult, ALU.add).then_inc(carry_b, 1)
                        after(dve, carry_b, b - 1, 2)
                expert(0)
                expert(1)
                if valid(b):
                    after(dve, uin_ready, b, 2)
                    after(dve, n_ready, b - 1, 2)
                    V.tensor_tensor_scan(z[:].rearrange("p g c -> p (g c)"), decay[:], u[:].rearrange("p g c -> p (g c)"),
                                         0.0, ALU.mult, ALU.add).then_inc(z_ready, 1)
                    after(dve, z_ready, b)
                    after(dve, st_ready, b - 1, 2)
                    for dst, tr in ((n_cos, 0), (n_sin, 1)):
                        V.tensor_tensor(dst[:], z[:, :, 0:CH], middle(rot[:, tr, 0:CH], 1, 2 * NB), ALU.mult)\
                            .then_inc(n_ready, 1)
                for k in range(2, 8):
                    expert(k)
                    if k == 6 and valid(y):
                        after(dve, xn_ready[1], y)
                        after(dve, rt_done, y - 1)
                        V.tensor_reduce(fsum[:], xn2[:, r, :].rearrange("p (b x) -> p x b", b=NB), AX_X, ALU.add)\
                            .then_inc(fsum_ready, 1)
                if valid(dd):
                    after(dve, o_done, dd)
                    after(dve, ot_done, dd - 1)
                    V.tensor_tensor(fin[:], bank[B_HO][:, 0:TOK], h2[:, q, :], ALU.add).then_inc(fin_ready, 1)

            drive(dve, body)

        @block.tensor
        def _(pe):
            def mm(dst, lhsT, rhs, start=True, stop=True):
                return nc.tensor.matmul(dst, lhsT, rhs, start=start, stop=stop, skip_group_check=True)

            pe.wait_ge(consts_in, 16 * loads["consts"])
            pe.wait_ge(ssm_in, 16 * loads["ssm"])
            for c in range(2):
                ins = nc.tensor.transpose(bank[2][:, C * c:C * c + C], c_raw[:, c, :], ident[0:C, 0:C])
            ins.then_inc(ct_turned, 1)
            pe.wait_ge(g_ready, 1)
            for k in range(T):
                for c in range(2):
                    o = (2 * (k % 2) + c) * 128
                    ins = nc.tensor.transpose(bank[k // 2][:, o:o + 128], g_in[:, k, c, :], ident[:])
                if k % 2:
                    ins.then_inc(win_turned, 1)
            pe.wait_ge(ct_ready, 1)
            for k in range(T):
                o = bank[3][:, C * k:C * k + C]
                mm(o, g_in[:, k, 0, :], ct[:, 0, :], True, False)
                ins = mm(o, g_in[:, k, 1, :], ct[:, 2, :], False, k > 0)
                if k == 0:
                    ins = mm(o, d_raw[:].rearrange("p a c -> p (a c)"), ident[0:C, 0:C], False, True)
            ins.then_inc(lag_made, 1)
            pe.wait_ge(pads_zeroed, FILLS)
            pe.wait_ge(crow_ready, 1)
            for k in range(2):
                for qq in range(NQ):
                    ins = mm(bank[4][:, NQ * k + qq:NQ * k + qq + 1], crow[:, k, 128 * qq:128 * qq + 128], ones_row[:, 0:1])
            ins.then_inc(ccol_made, 1)
            pe.wait_ge(c2m_ready, 1)
            for qq in range(NQ):
                mm(bank[5][0:16, 0:C], c2m[:, qq, :], w_l3[:, qq, :], qq == 0, False)
            mm(bank[5][0:16, 0:C], dup8[:], bo_raw[:], False, True).then_inc(cst_made, 1)
            pe.wait_ge(tok_weights, 1)
            pe.wait_ge(win_ready, 1)
            pe.wait_ge(ssm_weights, 1)
            pe.wait_ge(ffn_weights, 1)

            def free_bank(it, q, idx):
                prev = g_previous(it, q, idx)
                if prev:
                    kind, k, s = prev
                    after(pe, {"s": gate_ready, "l1": z1_ready, "l2": z2_ready}[kind], s, PER[kind], k + 1)
                return bank[g_bank(q, idx)][:, 0:TOK]

            def body(it, q):
                c, a, b, y, dd, f = it, it - 1, it - 2, it - 3, it - 4, it - 5
                r = (q + 1) % 2

                def gate_product(k):
                    if not valid(a):
                        return
                    if k == 0:
                        after(pe, h1_ready, a)
                    o = free_bank(it, q, k)
                    kj, which = divmod(k, 3)
                    if which < 2:
                        ins = mm(o, w_gate[halves[which], kj, :], h1[halves[which], r, :])
                    else:
                        ins = mm(o, w_gate[:, 3 + kj, :], h1[:, r, :])
                    ins.then_inc(s_done, 1)

                def mix_product(k):
                    if not valid(a):
                        return
                    kj, which = divmod(k, 3)
                    after(pe, gated_ready, a, 9, k + 1)
                    if which < 2:
                        ins = mm(bank[B_HO][halves[which], 0:TOK], w_mixA[:, which, kj, :], gated[:, k % 3, :], k < 2, False)
                    else:
                        ins = mm(bank[B_HO][:, 0:TOK], w_mixB[:, kj, :], gated[:, k % 3, :], False, k == 8)
                    ins.then_inc(mix_part, 1)

                def turn(ln, s, src):
                    if not valid(s):
                        return
                    for t in range(T):
                        ins = mm(bank[B_T][0:BJ, 128 * t:128 * t + 128], src(t), center[:])
                    ins.then_inc(ft_done[ln], 1)

                def turn_back(ln, s):
                    if not valid(s):
                        return
                    after(pe, xnt_ready[ln], s)
                    for t in range(T):
                        ins = nc.tensor.transpose(bank[B_M][:, BJ * t:BJ * t + BJ], xnt[:, ln, 128 * t:128 * t + 128],
                                                  ident[0:BJ, 0:BJ])
                    ins.then_inc(bt_done[ln], 1)

                if valid(dd):
                    after(pe, fsum_ready, dd)
                    mm(bank[B_M][0:WW, 0:16], fsum[:], w_rt[:], True, False)
                    mm(bank[B_M][0:WW, 0:16], ones_row[:, 0:WW], br_row[:].rearrange("p r e -> p (r e)"), False, True)\
                        .then_inc(rt_done, 1)
                if valid(b):
                    after(pe, h_ready, b)
                    after(pe, m_ready, b - 1, 4)
                    turn(0, b, lambda t: h[:, q, t::T])
                for k in range(3):
                    gate_product(k)
                if valid(dd):
                    after(pe, wtok_ready, dd)
                    nc.tensor.transpose(bank[B_M][0:16, 64:192], wtok[:], ident[:]).then_inc(wt_done, 1)
                if valid(f):
                    after(pe, fin_ready, f)
                    after(pe, h1_ready, it - 1)
                    for t in range(T):
                        ins = nc.tensor.transpose(bank[B_FY][0:BJ, 128 * t:128 * t + 128],
                                                  fin[:, t::T], ident[:])
                    ins.then_inc(ot_done, 1)
                gate_product(3)
                mix_product(0)
                if valid(y):
                    after(pe, st_ready, y, 2)
                    after(pe, out_ready, f)
                    after(pe, h1_ready, it - 1)
                    o = bank[B_FY][:, 0:TOK].rearrange("p (g t) -> p g t", t=T)
                    ot = bank[B_FY][:, 0:TOK].rearrange("p (b j t) -> p t b j", b=NB, t=T)
                    xn = xn1[:, r, :].rearrange("p (g t) -> p g t", t=T)
                    for k in range(T):
                        mm(o[:, :, k:T], w_lag[:, k, :], xn[:, :, 0:T - k], k == 0, False)
                    for t in range(T):
                        for cc in range(2):
                            for par in range(2):
                                ins = mm(ot[halves[par], t], w_st[:, cc, t, :],
                                         xst[:, NB * cc:NB * cc + NB, J * par:J * par + J], False, t == T - 1 and cc == 1)
                    ins.then_inc(y_done, 1)
                gate_product(4)
                mix_product(1)
                gate_product(5)
                mix_product(2)
                if valid(dd):
                    after(pe, wmask_ready, dd)
                    after(pe, wts_ready, dd)
                    mm(bank[B_M][:, 0:TOK], ehalf[:], wmask[:].rearrange("p q x -> p (q x)")).then_inc(wb_done, 1)
                gate_product(6)
                mix_product(3)
                if valid(y):
                    after(pe, h2_ready, y)
                    after(pe, xnt_ready[0], b) if valid(b) else after(pe, m_ready, b - 1, 4)
                    turn(1, y, lambda t: h2[:, r, t::T])
                gate_product(7)
                mix_product(4)
                gate_product(8)
                mix_product(5)
                after(pe, wbs_ready, dd)
                turn_back(0, b)
                mix_product(6)
                if valid(c):
                    pe.wait_ge(x_in[q], 64 * (c // 2 + 1)) if isinstance(c, int) else pe.wait_ge(x_in[q], 32 * c + (64 if q == 0 else 32))
                    after(pe, h2_ready, y)
                    for k in range(6):
                        src = (xa if k < 3 else xb)[:, q, :, k % 3:k % 3 + WW]
                        ins = mm(bank[B_FY][:, 0:TOK], w_conv[:, k, :], src, k == 0, k == 5)
                    ins.then_inc(conv_done, 1)
                mix_product(7)
                mix_product(8)

                def l1(k):
                    if valid(dd):
                        o = free_bank(it, q, G_TILES.index(("l1", k)))
                        hf = halves[k % 2]
                        mm(o, w_l1[hf, 128 * (k // 2):128 * (k // 2) + 128], xn2[hf, q, :]).then_inc(l1_done, 1)

                def l2(k):
                    if valid(dd):
                        o = free_bank(it, q, G_TILES.index(("l2", k)))
                        after(pe, z1_ready, dd, 8, k + 1)
                        mm(o, w_l2[:, k // 2, :], z1[:, k % 4, :]).then_inc(l2_done, 1)

                def l3(k):
                    if valid(dd):
                        if k == 0:
                            after(pe, h_ready, a)
                        after(pe, z2_ready, dd, 8, k + 1)
                        mm(bank[B_HO][halves[k % 2], 0:TOK], w_l3[:, k // 2, :], z2[:, k % 4, :], k < 2, False)\
                            .then_inc(l3_part, 1)

                l1(0)
                l1(1)
                if valid(b):
                    after(pe, xn_ready[0], b)
                    after(pe, xnt_ready[1], y)
                    for cc in range(2):
                        for t in range(T):
                            for par in range(2):
                                ins = mm(bank[B_T + par][:, BJ * cc:BJ * cc + BJ], w_in[halves[par], cc, t, :],
                                         xn1[halves[par], q, t::T], t == 0, t == T - 1)
                                if cc == 1 and t == T - 1:
                                    ins.then_inc(u_done, 1)
                for k in range(8):
                    if k + 2 < 8:
                        l1(k + 2)
                    l2(k)
                    if k >= 2:
                        l3(k - 2)
                    if k == 2:
                        after(pe, m_ready, b, 4) if valid(b) else after(pe, wbs_ready, dd)
                        turn_back(1, y)
                l3(6)
                l3(7)
                if valid(dd):
                    mm(bank[B_HO][:, 0:TOK], w_cst[:], middle(wts[:], 1, NB), False, True).then_inc(o_done, 1)

            drive(pe, body)


_INS = ["x", "L0_tok_W1", "L0_tok_b1", "L0_tok_W2", "L0_tok_b2", "L0_tok_W3", "L0_tok_b3",
        "L0_attn_nu_log", "L0_attn_theta_log", "L0_attn_gamma_log", "L0_attn_B_re", "L0_attn_B_im",
        "L0_attn_C_re", "L0_attn_C_im", "L0_attn_D", "L0_ffn_Wr", "L0_ffn_br", "L0_ffn_W1", "L0_ffn_b1",
        "L0_ffn_g1", "L0_ffn_be1", "L0_ffn_m1", "L0_ffn_v1", "L0_ffn_W2", "L0_ffn_b2", "L0_ffn_g2",
        "L0_ffn_be2", "L0_ffn_m2", "L0_ffn_v2", "L0_ffn_Wo", "L0_ffn_bo"]


def constants(np):
    k, m = np.arange(16), np.arange(128)
    ident = np.eye(128)
    return {
        "ident": ident,
        "center": ident - (m[:, None] // C == m[None, :] // C) / C,
        "emask": (k[:, None] // NE == np.arange(8)[None, :] % 2) & (k[:, None] % NE // 2 == np.arange(8)[None, :] // 2),
        "ehalf": k[:, None] % 2 == m[None, :] // C,
        "pmask": k[:, None] // NE == np.arange(2)[None, :],
        "dup8": np.arange(8)[:, None] == k[None, :] % NE,
        "zeros": np.zeros((C, TOK)),
    }


def kernel(**inputs):
    import numpy as _np
    import concourse.bacc as _bacc
    from concourse import mybir as _mybir
    from concourse.bass_utils import run_bass_kernel_spmd as _run

    nc = _bacc.Bacc("TRN2", target_bir_lowering=False, num_devices=1)
    arrays, d = {}, {}
    given = {name: _np.ascontiguousarray(inputs[name]) for name in _INS}
    given.update({name: _np.ascontiguousarray(a, dtype=_np.float32) for name, a in constants(_np).items()})
    for name, a in given.items():
        arrays[f"in_{name}_dram"] = a
        d[name] = nc.dram_tensor(f"in_{name}_dram", a.shape, _mybir.dt.from_np(a.dtype), kind="ExternalInput").ap()
    out = nc.dram_tensor("out_0_dram", (NB, HH * WW, C), F32, kind="ExternalOutput").ap()
    build(nc, d, out)
    r = _run(nc, [arrays], core_ids=[0])
    return r.results[0]["out_0_dram"]
```

```python
from contextlib import ExitStack

import concourse.bass as bass
from concourse import mybir

F32 = mybir.dt.float32
F32R = mybir.dt.float32r
I32 = mybir.dt.int32
ALU = mybir.AluOpType
ACT = mybir.ActivationFunctionType
AX_X = mybir.AxisListType.X

NB, C, HH, WW = 8, 64, 56, 56
PAIRS = HH // 2
TOK = NB * WW
TAPS = 9
NS = 128
T = 4
J = WW // T
BJ = NB * J
CH = 2 * J
NE = 8
NQ = NE // 2
LN_EPS = 1e-5
BN_EPS = 1e-3
FULL = 6
LAST = 5
GBANKS = 4
TURN_BACK_AT = 1
FILLS = 20

S_TILES = [("s", k) for k in range(9)]
L_TILES = [("l1", 0), ("l1", 1)]
for _k in range(8):
    if _k + 2 < 8:
        L_TILES.append(("l1", _k + 2))
    L_TILES.append(("l2", _k))
G_TILES = S_TILES + L_TILES
NG = len(G_TILES)
LAG = {"s": 1, "l1": 4, "l2": 4}
PER = {"s": 9, "l1": 8, "l2": 8}


def valid(step):
    return not isinstance(step, int) or 0 <= step < PAIRS


def g_bank(parity, idx):
    return (NG * parity + idx) % GBANKS


def g_previous(it, parity, idx):
    bank, back, i = g_bank(parity, idx), 0, idx - 1
    while back < 3:
        while i >= 0:
            kind, k = G_TILES[i]
            if g_bank((parity + back) % 2, i) == bank and valid(it - back - LAG[kind]):
                return kind, k, it - back - LAG[kind]
            i -= 1
        back, i = back + 1, NG - 1
    return None


def drive(eng, body, before=None):
    for it in range(FULL):
        if before and it in before:
            before[it]()
        body(it, it % 2)
    with eng.Fori(0, (PAIRS - FULL) // 2) as i:
        for k in range(2):
            body(2 * i + (FULL + k), (FULL + k) % 2)
    for it in range(PAIRS, PAIRS + LAST + 1):
        body(it, it % 2)


def after(eng, sem, step, per=1, n=None):
    if valid(step):
        eng.wait_ge(sem, per * step + (per if n is None else n))


def middle(ap, axis, n):
    v = ap.unsqueeze(axis)
    shape = list(v.shape)
    shape[axis] = n
    return v.broadcast_to(shape)


def build(nc, d, out):
    with ExitStack() as ctx:
        def sb(name, shape, dt=F32):
            return ctx.enter_context(nc.sbuf_tensor(name, shape, dt))

        def sem(name):
            return ctx.enter_context(nc.semaphore(name))

        bank = [ctx.enter_context(nc.psum_tensor(f"bank{i}", [128, 512], F32)) for i in range(8)]
        B_HO, B_FY, B_T, B_M = 4, 5, 6, 7

        ident = sb("ident", [128, 128])
        center = sb("center", [128, 128])
        emask = sb("emask", [32, 8])
        ehalf = sb("ehalf", [32, 128])
        ehalf_r = sb("ehalf_r", [32, 128], F32R)
        pmask = sb("pmask", [32, 2])
        dup8 = sb("dup8", [8, 32])
        w_conv = sb("w_conv", [128, 4, 128])
        w_convC = sb("w_convC", [128, 2, C])
        w_conv_hi = sb("w_conv_hi", [128, 3, 128], F32R)
        w_conv_lo = sb("w_conv_lo", [128, 3, 128], F32R)
        b1col = sb("b1col", [128, 1])
        w2raw = sb("w2raw", [128, C * TAPS])
        w_gate = sb("w_gate", [128, 8, 128])
        w_gate_hi = sb("w_gate_hi", [128, 8, 128], F32R)
        w_gate_lo = sb("w_gate_lo", [128, 8, 128], F32R)
        w_gateB = sb("w_gateB", [128, 128])
        b2raw = sb("b2raw", [128, TAPS])
        b2col = sb("b2col", [128, 9])
        w_mixA = sb("w_mixA", [128, 8, C])
        w_mixB = sb("w_mixB", [128, 128])
        b3col = sb("b3col", [128, 1])
        logs = sb("logs", [128, 3])
        exps = sb("exps", [128, 3])
        mags = sb("mags", [128, 2])
        ang = sb("ang", [128, 4, 2])
        trig = sb("trig", [128, 2])
        lam = sb("lam", [128, 2, T + 1])
        nlam_i = sb("nlam_i", [128, T + 1])
        rot = sb("rot", [128, 2, CH + 2])
        stepper = sb("stepper", [128, 8, 3])
        small = sb("small", [128, 32])
        small_i = sb("small_i", [128, 4], I32)
        gtmp = sb("gtmp", [128, 128])
        b_raw = sb("b_raw", [128, 2, 2, C])
        g_in = sb("g_in", [128, T, 2, 128])
        w_in_hi = sb("w_in_hi", [128, 2, T, NS], F32R)
        w_in_lo = sb("w_in_lo", [128, 2, T, NS], F32R)
        c_raw = sb("c_raw", [C, 2, NS])
        d_raw = sb("d_raw", [C, 2, C])
        ct = sb("ct", [128, 3, C])
        w_st = sb("w_st", [128, 2, T, C])
        w_lag = sb("w_lag", [128, T, C])
        decay = sb("decay", [128, 2 * NB * (CH + 1)])
        praw = sb("praw", [40, 128])
        pcol = sb("pcol", [128, 10, NQ])
        acol = sb("acol", [128, 2, NQ])
        bnhalf = sb("bnhalf", [128, 2 * NQ])
        adiag = sb("adiag", [128, 2 * NQ, 128])
        onesq = sb("onesq", [128, 128])
        w_l1 = sb("w_l1", [128, NE * C])
        w_l1_hi = sb("w_l1_hi", [128, NE * C], F32R)
        w_l1_lo = sb("w_l1_lo", [128, NE * C], F32R)
        w_l2 = sb("w_l2", [128, NQ, 128])
        w_l3 = sb("w_l3", [128, NQ, C])
        c1col = sb("c1col", [128, NQ])
        nc2col = sb("nc2col", [128, NQ])
        c2m = sb("c2m", [128, NQ, 32])
        bo_raw = sb("bo_raw", [8, C])
        w_cst = sb("w_cst", [32, 128])
        wr_raw = sb("wr_raw", [128, NE])
        w_rt = sb("w_rt", [128, 16])
        br_row = sb("br_row", [1, 2, NE])
        ones_row = sb("ones_row", [1, 128])
        halfpow = sb("halfpow", [112, 8])

        xa = sb("xa", [128, 2, NB, WW + 2])
        xb = sb("xb", [128, 2, NB, WW])
        xc = sb("xc", [128, 2, 2, NB, WW])
        xa_hi = sb("xa_hi", [128, NB, WW + 2], F32R)
        xa_lo = sb("xa_lo", [128, NB, WW + 2], F32R)
        h1 = sb("h1", [128, 2, TOK])
        h1s = sb("h1s", [128, 2, 2, TOK], F32R)
        gate = sb("gate", [128, 4, TOK])
        gated = sb("gated", [128, 4, TOK])
        h = sb("h", [128, 2, TOK])
        sq = sb("sq", [BJ, 2, 512])
        ssum = sb("ssum", [BJ, 2, 8])
        varr = sb("varr", [BJ, 2, 8])
        rstd = sb("rstd", [BJ, 2, 8])
        xnt = sb("xnt", [BJ, 2, 512])
        xn1 = sb("xn1", [128, 2, 2, TOK], F32R)
        xn2 = sb("xn2", [128, 2, 2, TOK], F32R)
        m_cos = sb("m_cos", [128, 2 * NB, CH])
        m_sin = sb("m_sin", [128, 2 * NB, CH])
        u = sb("u", [128, 2 * NB, CH + 1])
        z = sb("z", [128, 2 * NB, CH + 1])
        n_cos = sb("n_cos", [128, 2 * NB, CH])
        n_sin = sb("n_sin", [128, 2 * NB, CH])
        xst = sb("xst", [128, 2 * NB, CH])
        h2 = sb("h2", [128, 2, TOK])
        fsum = sb("fsum", [128, WW])
        lmax = sb("lmax", [WW, 2])
        lsub = sb("lsub", [WW, 16])
        lexp = sb("lexp", [WW, 16])
        lsum = sb("lsum", [WW, 2])
        lrec = sb("lrec", [WW, 2])
        wfull = sb("wfull", [WW, 16])
        wtok = sb("wtok", [128, 32])
        wmask = sb("wmask", [32, 8, WW], F32R)
        wts = sb("wts", [32, WW])
        csts = sb("csts", [128, WW])
        h2c = sb("h2c", [128, TOK])
        wbs = sb("wbs", [128, 8, WW])
        z1 = sb("z1", [128, 4, TOK])
        z2 = sb("z2", [128, 4, TOK])
        fin = sb("fin", [128, TOK])
        ostage = sb("ostage", [BJ, 2, 2, T * C])

        (consts_in, tok_in, ssm_in, ffn_in, pads_zeroed, tok_weights, exps_ready, angles_ready, trig_ready, g_ready,
         win_turned, win_ready, ct_turned, ct_ready, lag_made, ssm_weights, bnvar_ready, bnpow_ready,
         pcol_made, adiag_ready, arow_made, c2m_ready, cst_made, ffn_weights, dve_chain, x_split, xlo_ready,
         h1hi_ready, h1s_ready, wfull_ready, whi_ready, csts_ready, h2c_ready) = [sem(n) for n in (
             "consts_in", "tok_in", "ssm_in", "ffn_in", "pads_zeroed", "tok_weights", "exps_ready", "angles_ready", "trig_ready",
             "g_ready", "win_turned", "win_ready", "ct_turned", "ct_ready", "lag_made", "ssm_weights",
             "bnvar_ready", "bnpow_ready", "pcol_made", "adiag_ready", "arow_made", "c2m_ready", "cst_made", "ffn_weights", "dve_chain",
             "x_split", "xlo_ready", "h1hi_ready", "h1s_ready", "wfull_ready", "whi_ready", "csts_ready", "h2c_ready")]
        x_in = [sem("x_in0"), sem("x_in1")]
        stored = [sem("stored0"), sem("stored1")]
        (conv_done, h1_ready, s_done, gate_ready, gated_ready, mix_part, h_ready,
         ft_done, sq_ready, ssum_ready, var_ready, rstd_ready, xnt_ready, bt_done, xn_ready,
         u_done, m_ready, uin_ready, carry_a, carry_b, carry_ready, z_ready, n_ready, st_ready, y_done, h2_ready,
         fsum_ready, rt_done, lmax_ready, lsub_ready, lexp_ready, lsum_ready, lrec_ready, wtok_ready, wt_done, wmask_ready,
         wts_ready, wb_done, wbs_ready, l1_done, z1_ready, l2_done, z2_ready, l3_part, fin_ready,
         ot_done, out_ready) = [sem(n) for n in (
             "conv_done", "h1_ready", "s_done", "gate_ready", "gated_ready", "mix_part", "h_ready",
             "ft_done", "sq_ready", "ssum_ready", "var_ready", "rstd_ready", "xnt_ready", "bt_done", "xn_ready",
             "u_done", "m_ready", "uin_ready", "carry_a", "carry_b", "carry_ready", "z_ready", "n_ready", "st_ready", "y_done",
             "h2_ready", "fsum_ready", "rt_done", "lmax_ready", "lsub_ready", "lexp_ready", "lsum_ready", "lrec_ready", "wtok_ready",
             "wt_done", "wmask_ready", "wts_ready", "wb_done", "wbs_ready", "l1_done", "z1_ready", "l2_done",
             "z2_ready", "l3_part", "fin_ready", "ot_done", "out_ready")]
        ft_done = [ft_done, sem("ft_done2")]
        sq_ready = [sq_ready, sem("sq_ready2")]
        ssum_ready = [ssum_ready, sem("ssum_ready2")]
        var_ready = [var_ready, sem("var_ready2")]
        rstd_ready = [rstd_ready, sem("rstd_ready2")]
        xnt_ready = [xnt_ready, sem("xnt_ready2")]
        bt_done = [bt_done, sem("bt_done2")]
        xn_ready = [xn_ready, sem("xn_ready2")]
        xhi_ready = [sem("xhi_ready"), sem("xhi_ready2")]

        x_rows = d["x"].rearrange("b c (p q) w -> q p c b w", q=2)
        o_rows = out.rearrange("b (p q j t) c -> q p b j (t c)", q=2, j=J, t=T)
        w1v = d["L0_tok_W1"].rearrange("(c ki kj) n -> c ki kj n", ki=3, kj=3)
        w3v = d["L0_tok_W3"].rearrange("(c ki kj) n -> c ki kj n", ki=3, kj=3)
        halves = (slice(0, 64), slice(64, 128))
        other = (halves[1], halves[0])

        def gate_input(k, r):
            if k < 6:
                return xa[:, r, :, k // 2:k // 2 + WW]
            return xc[:, k - 6, r] if k < 8 else xb[:, r]

        loads = {"consts": 0, "tok": 0, "ssm": 0, "ffn": 0}

        block = ctx.enter_context(nc.Block())

        def x_arrived(eng, s, q):
            eng.wait_ge(x_in[q], 64 * s + (128 - 64 * q))

        @block.sync
        def _(sp):
            def load_x(s, q):
                if not valid(s):
                    return
                if not (isinstance(s, int) and s < 2):
                    after(sp, conv_done, s - 2)
                    after(sp, gated_ready, s - 2, 9)
                below = xz_view() if isinstance(s, int) and s == PAIRS - 1 else x_rows[0][s + 1]
                above = xz_view() if isinstance(s, int) and s == 0 else x_rows[1][s - 1]
                for half in range(2):
                    sp.dma_start(xa[halves[half], q, :, 1:WW + 1], x_rows[half][s]).then_inc(x_in[q], 16)
                    sp.dma_start(xb[halves[half], q, :, 0:WW - 1], (below, above)[half][:, :, 1:WW]).then_inc(x_in[q], 16)
                for par, row in ((0, above), (1, below)):
                    sp.dma_start(xc[0:64, par, q, :, 1:WW], row[:, :, 0:WW - 1]).then_inc(x_in[q], 16)
                    sp.dma_start(xc[64:128, par, q], row).then_inc(x_in[q], 16)

            def xz_view():
                return d["zeros"].rearrange("c (b w) -> c b w", b=NB)

            for s in range(2):
                load_x(s, s)

            def ld(group, dst, src):
                loads[group] += 1
                sp.dma_start(dst, src).then_inc({"consts": consts_in, "tok": tok_in, "ssm": ssm_in, "ffn": ffn_in}[group], 16)

            for dst, name in ((ident, "ident"), (center, "center"), (emask, "emask"), (ehalf, "ehalf"), (pmask, "pmask"),
                              (dup8, "dup8")):
                ld("consts", dst[:], d[name])
            for half, col, ki in ((0, 0, 1), (0, 1, 0), (1, 0, 2), (1, 1, 1)):
                ld("tok", w_conv[halves[half], 0:3, halves[col]], w1v[:, ki])
                ld("tok", w_mixA[:, 0:6].rearrange("p (kj k) n -> p k kj n", k=2)[halves[half], col], w3v[:, ki])
            for par, ki in ((0, 0), (1, 2)):
                for kj in range(2):
                    ld("tok", w_convC[halves[kj], par], w1v[:, ki, kj])
                    ld("tok", w_mixA[halves[kj], 6 + par], w3v[:, ki, kj])
                ld("tok", w_conv[other[par], 3, halves[par]], w1v[:, ki, 2])
                ld("tok", w_mixB[other[par], halves[par]], w3v[:, ki, 2])
            for hf in halves:
                ld("tok", w2raw[hf, :], d["L0_tok_W2"])
                ld("tok", b2raw[hf, :], d["L0_tok_b2"].rearrange("(c k) -> c k", k=TAPS))
                ld("tok", b1col[hf, :], d["L0_tok_b1"].rearrange("(c k) -> c k", k=1))
            ld("tok", b3col[halves[0], :], d["L0_tok_b3"].rearrange("(c k) -> c k", k=1))
            ld("ssm", b3col[halves[1], :], d["L0_tok_b3"].rearrange("(c k) -> c k", k=1))
            for k, n in enumerate(("nu_log", "theta_log", "gamma_log")):
                ld("ssm", logs[:, k:k + 1], d[f"L0_attn_{n}"].rearrange("(c k) -> c k", k=1))
            for k, n in enumerate(("re", "im")):
                for hf in range(2):
                    ld("ssm", b_raw[:, k, hf, :], d[f"L0_attn_B_{n}"])
                ld("ssm", c_raw[:, k, :], d[f"L0_attn_C_{n}"])
            ld("ssm", d_raw[:, 0, :], d["L0_attn_D"])
            for k, n in enumerate(("b1", "m1", "be1", "b2", "m2", "be2", "g1", "g2", "v1", "v2")):
                ld("ffn", praw[NQ * k:NQ * k + NQ, :], d[f"L0_ffn_{n}"].rearrange("(q e) h -> q (e h)", e=2))
            for hf in halves:
                ld("ffn", w_l1[hf, :].rearrange("p (e h) -> p e h", e=NE), d["L0_ffn_W1"].rearrange("e d h -> d e h"))
                ld("ffn", wr_raw[hf, :], d["L0_ffn_Wr"])
            w2v = d["L0_ffn_W2"].rearrange("(q e) h k -> e h q k", e=2)
            for e in range(2):
                ld("ffn", w_l2[halves[e], :, halves[e]], w2v[e])
            ld("ffn", w_l3[0:64], d["L0_ffn_Wo"].rearrange("(q e) h k -> e h q k", e=2)[0])
            ld("ffn", w_l3[64:128], d["L0_ffn_Wo"].rearrange("(q e) h k -> e h q k", e=2)[1])
            ld("ffn", bo_raw[:], d["L0_ffn_bo"])
            for k in range(2):
                ld("ffn", br_row[:, k, :], d["L0_ffn_br"].rearrange("(o e) -> o e", o=1))
            ld("ssm", d_raw[:, 1, :], d["L0_attn_D"])

            def store(s, q):
                if valid(s):
                    after(sp, out_ready, s)
                    for par in range(2):
                        sp.dma_start(o_rows[par][s], ostage[:, q, par, :]).then_inc(stored[q], 16)

            def body_io(it, q):
                s = it + 1
                if not isinstance(s, int) or s >= 2:
                    load_x(s, (q + 1) % 2)
                store(it - 5, (q + 1) % 2)

            for it in range(FULL):
                body_io(it, it % 2)
            with sp.Fori(0, (PAIRS - FULL) // 2 - 1) as i:
                for k in range(2):
                    body_io(2 * i + (FULL + k), (FULL + k) % 2)
            for it in range(PAIRS - 2, PAIRS + LAST + 1):
                body_io(it, it % 2)
            for q in range(2):
                sp.wait_ge(stored[q], 16 * PAIRS)

        @block.gpsimd
        def _(pool):
            fills = [(xa[:, :, :, 0:1], 0.0), (xa[:, :, :, WW + 1:WW + 2], 0.0), (xb[:, :, :, WW - 1:WW], 0.0),
                     (xc[0:64, :, :, :, 0:1], 0.0), (w_conv[0:64, 3, 0:64], 0.0), (w_conv[64:128, 3, 64:128], 0.0),
                     (w_mixB[0:64, 0:64], 0.0), (w_mixB[64:128, 64:128], 0.0), (w_gateB[0:64, 0:64], 0.0),
                     (w_gateB[64:128, 64:128], 0.0), (w_l2[0:64, :, 64:128], 0.0), (ones_row[:], 1.0), (onesq[:], 1.0),
                     (w_l2[64:128, :, 0:64], 0.0), (c2m[:], 0.0), (wtok[:], 0.0), (w_rt[:], 0.0),
                     (u[:], 0.0), (halfpow[:], -0.5), (bnhalf[:], -0.5)]
            assert len(fills) == FILLS
            for k, (tile, value) in enumerate(fills):
                nc.gpsimd.memset(tile, value).then_inc(pads_zeroed, 1)
                pool.wait_ge(pads_zeroed, k + 1)
            def batch_norms():
                pool.wait_ge(bnvar_ready, 1)
                nc.gpsimd.tensor_tensor(acol[:].rearrange("p a q -> p (a q)"),
                                        acol[:].rearrange("p a q -> p (a q)"), bnhalf[:], ALU.pow).then_inc(bnpow_ready, 1)

            def body(it, q):
                c, b, y, dd = it, it - 2, it - 3, it - 4
                if valid(b):
                    after(pool, var_ready[0], b)
                    after(pool, xnt_ready[0], b - 1)
                    nc.gpsimd.tensor_tensor(rstd[:, 0, :], varr[:, 0, :], halfpow[:], ALU.pow).then_inc(rstd_ready[0], 1)
                if valid(c):
                    after(pool, x_split, c)
                    nc.gpsimd.tensor_tensor(xa_lo[:], xa[:, q], xa_hi[:].bitcast(F32), ALU.subtract).then_inc(xlo_ready, 1)
                if valid(y):
                    after(pool, var_ready[1], y)
                    after(pool, xnt_ready[1], y - 1)
                    nc.gpsimd.tensor_tensor(rstd[:, 1, :], varr[:, 1, :], halfpow[:], ALU.pow).then_inc(rstd_ready[1], 1)
                if valid(b):
                    after(pool, m_ready, b, 2)
                    after(pool, z_ready, b - 1)
                    nc.gpsimd.tensor_tensor(u[:, 0:NB, 1:], m_cos[:, 0:NB], m_sin[:, NB:], ALU.add).then_inc(uin_ready, 1)
                    nc.gpsimd.tensor_tensor(u[:, NB:, 1:], m_cos[:, NB:], m_sin[:, 0:NB], ALU.subtract).then_inc(uin_ready, 1)
                    after(pool, n_ready, b, 2)
                    after(pool, y_done, b - 1)
                    nc.gpsimd.tensor_tensor(xst[:, 0:NB], n_cos[:, 0:NB], n_sin[:, NB:], ALU.subtract).then_inc(st_ready, 1)
                    nc.gpsimd.tensor_tensor(xst[:, NB:], n_cos[:, NB:], n_sin[:, 0:NB], ALU.add).then_inc(st_ready, 1)

                if valid(dd):
                    after(pool, csts_ready, dd)
                    after(pool, h2_ready, dd)
                    after(pool, fin_ready, dd - 1)
                    nc.gpsimd.tensor_tensor(h2c[:].rearrange("p (b w) -> p b w", b=NB),
                                            h2[:, q, :].rearrange("p (b w) -> p b w", b=NB), middle(csts[:], 1, NB),
                                            ALU.add).then_inc(h2c_ready, 1)

            drive(pool, body, {3: batch_norms})

        @block.scalar
        def _(act):
            act.wait_ge(angles_ready, 1)
            nc.scalar.activation(trig[:], ang[:, 3, :], ACT.Sin).then_inc(trig_ready, 1)
            act.wait_ge(tok_weights, 1)

            def square(ln, s, q):
                if valid(s):
                    after(act, ft_done[ln], s)
                    after(act, ssum_ready[ln], s - 1)
                    nc.scalar.activation(sq[:, ln, :], bank[B_T][0:BJ, :], ACT.Square).then_inc(sq_ready[ln], 1)

            def turned_back(ln, s, q, dst):
                if valid(s):
                    after(act, bt_done[ln], s)
                    for par in range(2):
                        v = bank[B_M][halves[par], 0:TOK].rearrange("p (t g) -> p g t", t=T)
                        nc.scalar.copy(dst[halves[par], q, par, :].rearrange("p (g t) -> p g t", t=T), v)\
                            .then_inc(xhi_ready[ln], 1)

            def body(it, q):
                c, a, b, y, dd, f = it, it - 1, it - 2, it - 3, it - 4, it - 5
                r = (q + 1) % 2
                def tanh(k):
                    if valid(a):
                        after(act, s_done, a, 9, k + 1)
                        after(act, gated_ready, a if k >= 4 else a - 1, 9, k - 3 if k >= 4 else k + 6)
                        g = bank[g_bank(q, k)][:, 0:TOK]
                        nc.scalar.activation(gate[:, k % 4, :], g, ACT.Tanh, bias=b2col[:, k:k + 1], scale=0.5)\
                            .then_inc(gate_ready, 1)

                tanh(0)
                tanh(1)
                if valid(dd):
                    after(act, lsub_ready, dd)
                    after(act, lsum_ready, dd - 1)
                    nc.scalar.activation(lexp[:], lsub[:], ACT.Exp).then_inc(lexp_ready, 1)
                square(0, b, q)
                tanh(2)
                tanh(3)
                if valid(f):
                    after(act, ot_done, f)
                    if valid(f - 2):
                        act.wait_ge(stored[r], 32 * (((f - 2) if isinstance(f, int) else f - 2) // 2) + 32) \
                            if isinstance(f, int) else act.wait_ge(stored[r], 16 * (f - 2) + (32 if r == 0 else 16))
                    nc.scalar.copy(ostage[:, r].rearrange("p q (t c) -> p t q c", t=T),
                                   bank[B_FY][0:BJ, :].rearrange("p (t q c) -> p t q c", t=T, q=2)).then_inc(out_ready, 1)
                tanh(4)
                if valid(dd):
                    after(act, wb_done, dd)
                    after(act, z2_ready, dd - 1, 8)
                    nc.scalar.copy(wbs[:], bank[B_M][:, 0:TOK].rearrange("p (q x) -> p q x", q=8)).then_inc(wbs_ready, 1)
                    after(act, h2c_ready, dd - 1)
                    nc.scalar.copy(csts[:], bank[B_M][:, TOK:TOK + WW]).then_inc(csts_ready, 1)
                tanh(5)
                tanh(6)
                if valid(b):
                    after(act, y_done, b - 2)
                turned_back(0, b, q, xn1)
                square(1, y, r)
                tanh(7)
                tanh(8)
                if valid(c):
                    after(act, conv_done, c)
                    after(act, s_done, c - 2, 9)
                    for par in range(2):
                        nc.scalar.activation(h1s[halves[par], q, par, :], bank[B_FY][halves[par], 0:TOK], ACT.Relu,
                                             bias=b1col[halves[par], 0:1]).then_inc(h1hi_ready, 1)
                    nc.scalar.activation(h1[:, q, :], bank[B_FY][:, 0:TOK], ACT.Relu, bias=b1col[:, 0:1]).then_inc(h1_ready, 1)
                if valid(a):
                    after(act, mix_part, a, 9)
                    after(act, h2_ready, a - 2)
                    nc.scalar.activation(h[:, r, :], bank[B_HO][:, 0:TOK], ACT.Identity, bias=b3col[:, 0:1]).then_inc(h_ready, 1)
                for k in range(8):
                    if k == TURN_BACK_AT + 2 and valid(y):
                        after(act, l1_done, y - 2, 8)
                        turned_back(1, y, r, xn2)
                    if valid(dd):
                        after(act, l1_done, dd, 8, k + 1)
                        after(act, l2_done, dd if k >= 4 else dd - 1, 8, k - 3 if k >= 4 else k + 5)
                        g = bank[g_bank(q, G_TILES.index(("l1", k)))][:, 0:TOK]
                        nc.scalar.activation(z1[:, k % 4, :], g, ACT.Relu, bias=c1col[:, k // 2:k // 2 + 1])\
                            .then_inc(z1_ready, 1)

            drive(act, body, {4: lambda: act.wait_ge(ffn_weights, 1)})

        @block.vector
        def _(dve):
            chain = [0]

            def link(ins):
                chain[0] += 1
                ins.then_inc(dve_chain, 1)
                dve.wait_ge(dve_chain, chain[0])

            V = nc.vector
            def exp_of(dst, x, width):
                n, p, sc = small[:, 0:width], small[:, 8:8 + width], small_i[:, 0:width]
                red = small[:, 16:16 + width]
                link(V.tensor_scalar(n, x, 1.4426950408889634, MAGIC, ALU.mult, ALU.add))
                link(V.tensor_scalar(n, n, MAGIC, None, ALU.subtract))
                link(V.tensor_scalar(n, n, -126.0, 127.0, ALU.max, ALU.min))
                link(V.scalar_tensor_tensor(red, n, -0.693145751953125, x, ALU.mult, ALU.add))
                link(V.scalar_tensor_tensor(red, n, -1.4286068203094172e-06, red, ALU.mult, ALU.add))
                link(V.tensor_scalar(p, red, 1.0 / 5040.0, None, ALU.mult))
                for f in (720.0, 120.0, 24.0, 6.0, 2.0, 1.0):
                    link(V.scalar_tensor_tensor(p, p, 1.0 / f, red, ALU.add, ALU.mult))
                link(V.tensor_scalar(p, p, 1.0, None, ALU.add))
                link(V.tensor_scalar(sc, n, 127.0, 8388608.0, ALU.add, ALU.mult))
                link(V.tensor_tensor(dst, p, sc.bitcast(F32), ALU.mult))

            TWO_PI_HI, TWO_PI_LO, MAGIC = 6.28125, 0.0019353071795864769, 12582912.0
            dve.wait_ge(ssm_in, 16 * loads["ssm"])
            exp_of(exps[:], logs[:], 3)
            link(V.tensor_scalar(small[:, 24:25], exps[:, 0:1], -1.0, None, ALU.mult))
            link(V.tensor_scalar(small[:, 25:26], exps[:, 0:1], -float(T), None, ALU.mult))
            exp_of(mags[:], small[:, 24:26], 2)
            link(V.tensor_copy(ang[:, 0, 0:1], exps[:, 1:2]))
            link(V.tensor_scalar(ang[:, 0, 1:2], exps[:, 1:2], 1.5707963267948966, None, ALU.add))
            link(V.tensor_scalar(ang[:, 1, :], ang[:, 0, :], 0.15915494309189535, MAGIC, ALU.mult, ALU.add))
            link(V.tensor_scalar(ang[:, 1, :], ang[:, 1, :], MAGIC, None, ALU.subtract))
            link(V.scalar_tensor_tensor(ang[:, 2, :], ang[:, 1, :], -TWO_PI_HI, ang[:, 0, :], ALU.mult, ALU.add))
            link(V.scalar_tensor_tensor(ang[:, 3, :], ang[:, 1, :], -TWO_PI_LO, ang[:, 2, :], ALU.mult, ALU.add))
            V.tensor_scalar(ang[:, 3, :], ang[:, 3, :], 3.1415925, -3.1415925, ALU.min, ALU.max).then_inc(angles_ready, 1)

            def split(hi, lo, w):
                link(V.tensor_copy(hi, w))
                link(V.tensor_tensor(lo, w, hi.bitcast(F32), ALU.subtract))

            dve.wait_ge(pads_zeroed, FILLS)
            dve.wait_ge(tok_in, 16 * loads["tok"])
            w2t = w2raw[:].rearrange("p (c ki kj) -> p ki kj c", ki=3, kj=3)
            b2t = b2raw[:].rearrange("p (ki kj) -> p ki kj", ki=3)
            wg = w_gate[:, 0:6].rearrange("p (kj k) n -> p k kj n", k=2)
            b2o = b2col[:, 0:6].rearrange("p (kj k) -> p k kj", k=2)
            for par, col, ki in ((0, 0, 1), (0, 1, 2), (1, 0, 0), (1, 1, 1)):
                V.tensor_copy(wg[:, par, :, halves[col]], w2t[:, ki])
                V.tensor_scalar(b2o[halves[col], par], b2t[halves[col], ki], 0.5, None, ALU.mult)
            for par, ki in ((0, 0), (1, 2)):
                for kj in range(2):
                    V.tensor_copy(w_gate[:, 6 + par, halves[kj]], w2t[:, ki, kj])
                    V.tensor_scalar(b2col[halves[kj], 6 + par:7 + par], b2t[halves[kj], ki, kj:kj + 1], 0.5, None, ALU.mult)
                V.tensor_copy(w_gateB[halves[par], other[par]], w2t[halves[par], ki, 2])
                V.tensor_scalar(b2col[other[par], 8:9], b2t[other[par], ki, 2:3], 0.5, None, ALU.mult)
            V.tensor_scalar(w_mixB[:], w_mixB[:], 0.5, None, ALU.mult)
            link(V.tensor_scalar(w_mixA[:], w_mixA[:], 0.5, None, ALU.mult))
            split(w_conv_hi[:], w_conv_lo[:], w_conv[:, 0:3])
            link(V.tensor_copy(w_gate_hi[:], w_gate[:]))
            V.tensor_tensor(w_gate_lo[:], w_gate[:], w_gate_hi[:].bitcast(F32), ALU.subtract).then_inc(tok_weights, 1)
            dve.wait_ge(trig_ready, 1)

            def times(dst_r, dst_i, xr, xi, sr, si, nsi, width):
                link(V.tensor_scalar(small[:, 0:width], xr, sr, None, ALU.mult))
                link(V.scalar_tensor_tensor(dst_r, xi, nsi, small[:, 0:width], ALU.mult, ALU.add))
                link(V.tensor_scalar(small[:, 0:width], xi, sr, None, ALU.mult))
                link(V.scalar_tensor_tensor(dst_i, xr, si, small[:, 0:width], ALU.mult, ALU.add))

            link(V.memset(lam[:, 0, 0:1], 1.0))
            link(V.memset(lam[:, 1, 0:1], 0.0))
            link(V.tensor_scalar(lam[:, 0, 1:2], trig[:, 1:2], mags[:, 0:1], None, ALU.mult))
            link(V.tensor_scalar(lam[:, 1, 1:2], trig[:, 0:1], mags[:, 0:1], None, ALU.mult))
            link(V.tensor_scalar(nlam_i[:, 1:2], lam[:, 1, 1:2], -1.0, None, ALU.mult))
            for k in range(2, T + 1):
                times(lam[:, 0, k:k + 1], lam[:, 1, k:k + 1], lam[:, 0, k - 1:k], lam[:, 1, k - 1:k],
                      lam[:, 0, 1:2], lam[:, 1, 1:2], nlam_i[:, 1:2], 1)
            link(V.tensor_scalar(nlam_i[:], lam[:, 1, :], -1.0, None, ALU.mult))

            def square_of(dst, src):
                s = [stepper[:, src, c:c + 1] for c in range(3)]
                times(stepper[:, dst, 0:1], stepper[:, dst, 1:2], s[0], s[1], s[0], s[1], s[2], 1)
                link(V.tensor_scalar(stepper[:, dst, 2:3], stepper[:, dst, 1:2], -1.0, None, ALU.mult))

            link(V.tensor_copy(stepper[:, 0, 0:1], trig[:, 1:2]))
            link(V.tensor_copy(stepper[:, 0, 1:2], trig[:, 0:1]))
            link(V.tensor_scalar(stepper[:, 0, 2:3], trig[:, 0:1], -1.0, None, ALU.mult))
            for m in range(1, 7):
                square_of(m, m - 1)
            link(V.tensor_copy(rot[:, 0, 0:1], stepper[:, 2, 0:1]))
            link(V.tensor_copy(rot[:, 1, 0:1], stepper[:, 2, 2:3]))
            link(V.memset(rot[:, 0, 1:2], 1.0))
            link(V.memset(rot[:, 1, 1:2], 0.0))
            n = 1
            while n < CH + 1:
                w = min(n, CH + 1 - n)
                s = [stepper[:, 2 + n.bit_length() - 1, c:c + 1] for c in range(3)]
                times(rot[:, 0, 1 + n:1 + n + w], rot[:, 1, 1 + n:1 + n + w], rot[:, 0, 1:1 + w], rot[:, 1, 1:1 + w],
                      s[0], s[1], s[2], w)
                n += w
            link(V.tensor_scalar(stepper[:, 7, 0:1], rot[:, 1, CH + 1:CH + 2], -1.0, None, ALU.mult))
            turn_r, turn_i, nturn_i = rot[:, 0, CH + 1:CH + 2], rot[:, 1, CH + 1:CH + 2], stepper[:, 7, 0:1]

            link(V.memset(decay[:], 0.0))
            dv = decay[:].rearrange("p (g c) -> p g c", c=CH + 1)
            link(V.tensor_scalar(dv[:, :, 1:], dv[:, :, 1:], mags[:, 1:2], None, ALU.add))

            br, bi = b_raw[:, 0].rearrange("p a c -> p (a c)"), b_raw[:, 1].rearrange("p a c -> p (a c)")
            link(V.tensor_scalar(g_in[:, 0, 0, :], br, exps[:, 2:3], None, ALU.mult))
            link(V.tensor_scalar(g_in[:, 0, 1, :], bi, exps[:, 2:3], None, ALU.mult))
            for k in range(1, T):
                lr, li, nli = lam[:, 0, k:k + 1], lam[:, 1, k:k + 1], nlam_i[:, k:k + 1]
                for c, (x, w, s) in enumerate(((0, 1, nli), (1, 0, li))):
                    link(V.tensor_scalar(gtmp[:], g_in[:, 0, x, :], lr, None, ALU.mult))
                    link(V.scalar_tensor_tensor(g_in[:, k, c, :], g_in[:, 0, w, :], s, gtmp[:], ALU.mult, ALU.add))
            V.tensor_copy(small[:, 30:31], lam[:, 0, 0:1]).then_inc(g_ready, 1)
            dve.wait_ge(ct_turned, 1)
            link(V.tensor_copy(ct[:, 0:2, :], bank[2][:, 0:128].rearrange("p (a c) -> p a c", a=2)))
            link(V.tensor_scalar(ct[:, 2, :], ct[:, 1, :], -1.0, None, ALU.mult))
            V.tensor_copy(small[:, 29:30], lam[:, 0, 0:1]).then_inc(ct_ready, 1)
            for t in range(T):
                lr, li, nli = lam[:, 0, t + 1:t + 2], lam[:, 1, t + 1:t + 2], nlam_i[:, t + 1:t + 2]
                link(V.tensor_scalar(w_st[:, 0, t, :], ct[:, 0, :], lr, None, ALU.mult))
                link(V.scalar_tensor_tensor(w_st[:, 0, t, :], ct[:, 1, :], nli, w_st[:, 0, t, :], ALU.mult, ALU.add))
                link(V.tensor_scalar(w_st[:, 1, t, :], ct[:, 0, :], nli, None, ALU.mult))
                link(V.scalar_tensor_tensor(w_st[:, 1, t, :], ct[:, 2, :], lr, w_st[:, 1, t, :], ALU.mult, ALU.add))
            dve.wait_ge(lag_made, 1)
            link(V.tensor_copy(w_lag[:], bank[3][:, 0:T * C].rearrange("p (k c) -> p k c", k=T)))
            dve.wait_ge(win_turned, 2)
            for k in range(T):
                src = bank[k // 2][:, 256 * (k % 2):256 * (k % 2) + 256].rearrange("p (c n) -> p c n", c=2)
                link(V.tensor_copy(w_in_hi[:, :, T - 1 - k], src))
                link(V.tensor_tensor(w_in_lo[:, :, T - 1 - k], src, w_in_hi[:, :, T - 1 - k].bitcast(F32), ALU.subtract))
            V.tensor_copy(small[:, 28:29], lam[:, 0, 0:1]).then_inc(ssm_weights, 1)

            def expert_weights():
                dve.wait_ge(ffn_in, 16 * loads["ffn"])
                dve.wait_ge(pcol_made, 1)
                link(V.tensor_copy(pcol[:].rearrange("p a q -> p (a q)"), bank[0][:, 0:40]))
                V.tensor_scalar(acol[:], pcol[:, 8:10], BN_EPS, None, ALU.add).then_inc(bnvar_ready, 1)
                dve.wait_ge(bnpow_ready, 1)
                link(V.tensor_tensor(acol[:], acol[:], pcol[:, 6:8], ALU.mult))
                dve.wait_ge(consts_in, 16 * loads["consts"])
                for k in range(2 * NQ):
                    link(V.tensor_scalar(adiag[:, k, :], ident[:], acol[:, k // NQ, k % NQ:k % NQ + 1], None, ALU.mult))
                pv = pcol[:, 0:6].rearrange("p (l v) q -> p v l q", v=3)
                link(V.tensor_tensor(pv[:, 0], pv[:, 0], pv[:, 1], ALU.subtract))
                link(V.tensor_tensor(pv[:, 0], pv[:, 0], acol[:], ALU.mult))
                link(V.tensor_tensor(pv[:, 0], pv[:, 0], pv[:, 2], ALU.add))
                link(V.tensor_copy(c1col[:], pcol[:, 0]))
                link(V.tensor_scalar(nc2col[:], pcol[:, 3], -1.0, None, ALU.mult))
                for e, hf in enumerate(halves):
                    for qq in range(NQ):
                        dst = c2m[hf, qq, :].rearrange("p (r e) -> p r e", r=4)[:, :, 2 * qq + e:2 * qq + e + 1]
                        V.tensor_copy(dst, middle(pcol[hf, 3, qq:qq + 1], 1, 4))
                for k, hf in enumerate(halves):
                    V.tensor_scalar(w_rt[hf, NE * k:NE * k + NE], wr_raw[hf, :], 1.0 / NB, None, ALU.mult)
                link(V.tensor_copy(ehalf_r[:], ehalf[:]))
                V.tensor_copy(small[:, 27:28], lam[:, 0, 0:1]).then_inc(adiag_ready, 1)
                dve.wait_ge(arow_made, 2)
                link(V.tensor_tensor(w_l1[:], w_l1[:], bank[1][:], ALU.mult))
                link(V.tensor_tensor(w_l2[:].rearrange("p q k -> p (q k)"), w_l2[:].rearrange("p q k -> p (q k)"),
                                     bank[2][:], ALU.mult))
                split(w_l1_hi[:], w_l1_lo[:], w_l1[:])
                dve.wait_ge(cst_made, 1)
                for k, hf in enumerate(halves):
                    link(V.tensor_scalar(w_cst[:, hf], bank[3][0:32, 0:C], pmask[:, k:k + 1], None, ALU.mult))
                V.tensor_copy(small[:, 26:27], lam[:, 0, 0:1]).then_inc(ffn_weights, 1)

            hct = bank[B_T][0:BJ, :].rearrange("p (g c) -> p g c", c=C)

            def channel_sums(ln, s):
                if valid(s):
                    after(dve, sq_ready[ln], s)
                    V.tensor_reduce(ssum[:, ln, :], sq[:, ln, :].rearrange("p (g c) -> p g c", c=C), AX_X, ALU.add)\
                        .then_inc(ssum_ready[ln], 1)

            def variance(ln, s):
                if valid(s):
                    after(dve, ssum_ready[ln], s)
                    after(dve, rstd_ready[ln], s - 1)
                    V.tensor_scalar(varr[:, ln, :], ssum[:, ln, :], 1.0 / C, LN_EPS, ALU.mult, ALU.add)\
                        .then_inc(var_ready[ln], 1)

            def normalise(ln, s):
                if valid(s):
                    after(dve, rstd_ready[ln], s)
                    after(dve, bt_done[ln], s - 1)
                    V.tensor_tensor(xnt[:, ln, :].rearrange("p (g c) -> p g c", c=C), hct, middle(rstd[:, ln, :], 2, C),
                                    ALU.mult).then_inc(xnt_ready[ln], 1)

            def body(it, q):
                c, a, b, y, dd, f = it, it - 1, it - 2, it - 3, it - 4, it - 5
                r = (q + 1) % 2
                def gating(k):
                    if valid(a):
                        after(dve, gate_ready, a, 9, k + 1)
                        after(dve, mix_part, a if k >= 4 else a - 1, 9, k - 3 if k >= 4 else k + 6)
                        V.scalar_tensor_tensor(gated[:, k % 4, :].rearrange("p (b w) -> p b w", b=NB),
                                               gate[:, k % 4, :].rearrange("p (b w) -> p b w", b=NB), 1.0, gate_input(k, r),
                                               ALU.add, ALU.mult).then_inc(gated_ready, 1)

                def low_parts(ln, s, buf, dst):
                    if valid(s):
                        for par in range(2):
                            after(dve, xhi_ready[ln], s, 2, par + 1)
                            v = bank[B_M][halves[par], 0:TOK].rearrange("p (t g) -> p g t", t=T)
                            hi, lo = (dst[hf, buf, par, :].rearrange("p (g t) -> p g t", t=T) for hf in (halves[par], other[par]))
                            V.tensor_tensor(lo, v, hi.bitcast(F32), ALU.subtract).then_inc(xn_ready[ln], 1)

                def softmax_max():
                    if valid(dd):
                        lg = bank[B_M][0:WW, 0:16].rearrange("p (r e) -> p r e", r=2)
                        after(dve, rt_done, dd)
                        V.tensor_reduce(lmax[:], lg, AX_X, ALU.max).then_inc(lmax_ready, 1)
                        after(dve, lmax_ready, dd)
                        V.tensor_tensor(lsub[:].rearrange("p (r e) -> p r e", r=2), lg, middle(lmax[:], 2, NE), ALU.subtract)\
                            .then_inc(lsub_ready, 1)

                def softmax_sum():
                    if valid(dd):
                        after(dve, lexp_ready, dd)
                        V.tensor_reduce(lsum[:], lexp[:].rearrange("p (r e) -> p r e", r=2), AX_X, ALU.add)\
                            .then_inc(lsum_ready, 1)

                def softmax_reciprocal():
                    if valid(dd):
                        after(dve, lsum_ready, dd)
                        V.reciprocal(lrec[:], lsum[:]).then_inc(lrec_ready, 1)

                def softmax_weights():
                    if valid(dd):
                        after(dve, lrec_ready, dd)
                        after(dve, wt_done, dd - 1)
                        V.tensor_tensor(wfull[:].rearrange("p (r e) -> p r e", r=2), lexp[:].rearrange("p (r e) -> p r e", r=2),
                                        middle(lrec[:], 2, NE), ALU.mult).then_inc(wfull_ready, 1)

                def weights_high():
                    if valid(dd):
                        after(dve, wfull_ready, dd)
                        V.tensor_copy(wtok[0:WW, 0:16].bitcast(F32R), wfull[:]).then_inc(whi_ready, 1)

                def weights_low():
                    if valid(dd):
                        after(dve, whi_ready, dd)
                        V.tensor_tensor(wtok[0:WW, 16:32], wfull[:], wtok[0:WW, 0:16], ALU.subtract).then_inc(wtok_ready, 1)

                def split_rows():
                    if valid(c):
                        x_arrived(dve, c, q)
                        after(dve, conv_done, c - 1)
                        V.tensor_copy(xa_hi[:], xa[:, q]).then_inc(x_split, 1)

                def spread_weights():
                    if valid(dd):
                        after(dve, wt_done, dd)
                        after(dve, wb_done, dd - 1)
                        V.tensor_tensor(wmask[:], middle(bank[B_M][0:32, 64:64 + WW], 1, 8), middle(emask[:], 2, WW),
                                        ALU.mult).then_inc(wmask_ready, 1)
                        V.tensor_copy(wts[:], bank[B_M][0:32, 64:64 + WW]).then_inc(wts_ready, 1)

                def second_residual():
                    if valid(y):
                        after(dve, y_done, y)
                        after(dve, h2c_ready, y - 2)
                        after(dve, ft_done[1], y - 2)
                        V.tensor_tensor(h2[:, r, :], bank[B_FY][:, 0:TOK], h[:, r, :], ALU.add).then_inc(h2_ready, 1)

                softmax_max()
                gating(0)
                gating(1)
                softmax_sum()
                channel_sums(0, b)
                softmax_reciprocal()
                variance(0, b)
                softmax_weights()
                gating(2)
                weights_high()
                gating(3)
                weights_low()
                gating(4)
                normalise(0, b)
                spread_weights()
                split_rows()
                gating(5)
                second_residual()
                gating(6)
                low_parts(0, b, q, xn1)
                channel_sums(1, y)
                variance(1, y)
                gating(7)
                gating(8)
                normalise(1, y)
                if valid(c):
                    after(dve, h1_ready, c)
                    for par in range(2):
                        after(dve, h1hi_ready, c, 2, par + 1)
                        V.tensor_tensor(h1s[other[par], q, par, :], h1[halves[par], q, :],
                                        h1s[halves[par], q, par, :].bitcast(F32), ALU.subtract).then_inc(h1s_ready, 1)

                def expert(k):
                    if valid(dd):
                        after(dve, l2_done, dd, 8, k + 1)
                        after(dve, l3_part, dd if k >= 4 else dd - 1, 8, k - 3 if k >= 4 else k + 5)
                        if k == 0:
                            after(dve, wbs_ready, dd)
                        g = bank[g_bank(q, G_TILES.index(("l2", k)))][:, 0:TOK]
                        V.scalar_tensor_tensor(z2[:, k % 4, :].rearrange("p (b x) -> p b x", b=NB),
                                               g.rearrange("p (b x) -> p b x", b=NB), nc2col[:, k // 2:k // 2 + 1],
                                               middle(wbs[:, k, :], 1, NB), ALU.max, ALU.mult).then_inc(z2_ready, 1)

                if valid(b):
                    after(dve, uin_ready, b - 1, 2)
                    after(dve, u_done, b)
                    src = bank[B_T][:, 0:4 * BJ].rearrange("p (g c) -> p g c", c=CH)
                    for dst, tr in ((m_cos, 0), (m_sin, 1)):
                        V.tensor_tensor(dst[:], src, middle(rot[:, tr, 1:1 + CH], 1, 2 * NB), ALU.mult).then_inc(m_ready, 1)
                    if not (isinstance(b, int) and b == 0):
                        zl = z[:, :, CH:CH + 1].rearrange("p (k b) o -> p k (b o)", k=2)
                        uf = u[:, :, 0:1].rearrange("p (k b) o -> p k (b o)", k=2)
                        V.tensor_scalar(uf, zl, turn_r, None, ALU.mult).then_inc(carry_a, 1)
                        after(dve, carry_a, b - 1)
                        V.scalar_tensor_tensor(uf[:, 0], zl[:, 1], nturn_i, uf[:, 0], ALU.mult, ALU.add).then_inc(carry_b, 1)
                        V.scalar_tensor_tensor(uf[:, 1], zl[:, 0], turn_i, uf[:, 1], ALU.mult, ALU.add).then_inc(carry_b, 1)
                        after(dve, carry_b, b - 1, 2)
                expert(0)
                if valid(b):
                    after(dve, uin_ready, b, 2)
                    after(dve, n_ready, b - 1, 2)
                    V.tensor_tensor_scan(z[:].rearrange("p g c -> p (g c)"), decay[:], u[:].rearrange("p g c -> p (g c)"),
                                         0.0, ALU.mult, ALU.add).then_inc(z_ready, 1)
                expert(1)
                if valid(b):
                    after(dve, z_ready, b)
                    after(dve, st_ready, b - 1, 2)
                    for dst, tr in ((n_cos, 0), (n_sin, 1)):
                        V.tensor_tensor(dst[:], z[:, :, 0:CH], middle(rot[:, tr, 0:CH], 1, 2 * NB), ALU.mult)\
                            .then_inc(n_ready, 1)
                expert(2)
                low_parts(1, y, r, xn2)
                expert(3)
                if valid(y):
                    after(dve, rt_done, y - 1)
                    V.tensor_reduce(fsum[:].rearrange("p (j t) -> p j t", t=T),
                                    bank[B_M][:, 0:TOK].rearrange("p (t b j) -> p j t b", t=T, b=NB), AX_X, ALU.add)\
                        .then_inc(fsum_ready, 1)
                for k in range(4, 8):
                    expert(k)
                if valid(dd):
                    after(dve, l3_part, dd, 8)
                    after(dve, ot_done, dd - 1)
                    after(dve, h2c_ready, dd)
                    V.tensor_tensor(fin[:], bank[B_HO][:, 0:TOK], h2c[:], ALU.add).then_inc(fin_ready, 1)

            drive(dve, body, {3: expert_weights})

        @block.tensor
        def _(pe):
            def mm(dst, lhsT, rhs, start=True, stop=True):
                return nc.tensor.matmul(dst, lhsT, rhs, start=start, stop=stop, skip_group_check=True)

            pe.wait_ge(consts_in, 16 * loads["consts"])
            pe.wait_ge(ssm_in, 16 * loads["ssm"])
            for c in range(2):
                ins = nc.tensor.transpose(bank[2][:, C * c:C * c + C], c_raw[:, c, :], ident[0:C, 0:C])
            ins.then_inc(ct_turned, 1)
            pe.wait_ge(g_ready, 1)
            for k in range(T):
                for c in range(2):
                    o = (2 * (k % 2) + c) * 128
                    ins = nc.tensor.transpose(bank[k // 2][:, o:o + 128], g_in[:, k, c, :], ident[:])
                if k % 2:
                    ins.then_inc(win_turned, 1)
            pe.wait_ge(ct_ready, 1)
            for k in range(T):
                o = bank[3][:, C * k:C * k + C]
                mm(o, g_in[:, k, 0, :], ct[:, 0, :], True, False)
                ins = mm(o, g_in[:, k, 1, :], ct[:, 2, :], False, k > 0)
                if k == 0:
                    ins = mm(o, d_raw[:].rearrange("p a c -> p (a c)"), ident[0:C, 0:C], False, True)
            ins.then_inc(lag_made, 1)
            pe.wait_ge(tok_weights, 1)
            pe.wait_ge(ssm_weights, 1)

            def expert_weights():
                after(pe, gate_ready, 1, 9)
                pe.wait_ge(ffn_in, 16 * loads["ffn"])
                nc.tensor.transpose(bank[0][:, 0:40], praw[:], ident[0:40, 0:40]).then_inc(pcol_made, 1)
                pe.wait_ge(adiag_ready, 1)
                for k in range(2):
                    mm(bank[1 + k][:], onesq[:], adiag[:, NQ * k:NQ * k + NQ, :]).then_inc(arow_made, 1)
                for qq in range(NQ):
                    mm(bank[3][0:32, 0:C], c2m[:, qq, :], w_l3[:, qq, :], qq == 0, False)
                mm(bank[3][0:32, 0:C], dup8[:], bo_raw[:], False, True).then_inc(cst_made, 1)
                pe.wait_ge(ffn_weights, 1)

            def free_bank(it, q, idx):
                prev = g_previous(it, q, idx)
                if prev:
                    kind, k, s = prev
                    after(pe, {"s": gate_ready, "l1": z1_ready, "l2": z2_ready}[kind], s, PER[kind], k + 1)
                return bank[g_bank(q, idx)][:, 0:TOK]

            def body(it, q):
                c, a, b, y, dd, f = it, it - 1, it - 2, it - 3, it - 4, it - 5
                r = (q + 1) % 2

                def gate_product(k):
                    if not valid(a):
                        return
                    if k == 0:
                        after(pe, h1s_ready, a, 2)
                    o = free_bank(it, q, k)
                    if k < 8:
                        mm(o, w_gate_hi[:, k, :], h1s[:, r, k % 2, :], True, False)
                        ins = mm(o, w_gate_lo[:, k, :], h1s[:, r, k % 2, :], False, True)
                    else:
                        ins = mm(o, w_gateB[:], h1[:, r, :])
                    ins.then_inc(s_done, 1)

                def mix_product(k):
                    if not valid(a):
                        return
                    after(pe, gated_ready, a, 9, k + 1)
                    if k < 8:
                        ins = mm(bank[B_HO][halves[k % 2], 0:TOK], w_mixA[:, k, :], gated[:, k % 4, :], k < 2, False)
                    else:
                        ins = mm(bank[B_HO][:, 0:TOK], w_mixB[:], gated[:, k % 4, :], False, True)
                    ins.then_inc(mix_part, 1)

                def turn(ln, s, src):
                    if not valid(s):
                        return
                    for t in range(T):
                        ins = mm(bank[B_T][0:BJ, 128 * t:128 * t + 128], src(t), center[:])
                    ins.then_inc(ft_done[ln], 1)

                def turn_back(ln, s):
                    if not valid(s):
                        return
                    after(pe, xnt_ready[ln], s)
                    for t in range(T):
                        ins = nc.tensor.transpose(bank[B_M][:, BJ * t:BJ * t + BJ], xnt[:, ln, 128 * t:128 * t + 128],
                                                  ident[0:BJ, 0:BJ])
                    ins.then_inc(bt_done[ln], 1)

                def logits():
                    if valid(dd):
                        after(pe, fsum_ready, dd)
                        mm(bank[B_M][0:WW, 0:16], fsum[:], w_rt[:], True, False)
                        mm(bank[B_M][0:WW, 0:16], ones_row[:, 0:WW], br_row[:].rearrange("p r e -> p (r e)"), False, True)\
                            .then_inc(rt_done, 1)

                def output_turn():
                    if valid(f):
                        after(pe, fin_ready, f)
                        after(pe, h1_ready, it - 1)
                        for t in range(T):
                            ins = nc.tensor.transpose(bank[B_FY][0:BJ, 128 * t:128 * t + 128], fin[:, t::T], ident[:])
                        ins.then_inc(ot_done, 1)

                def own_tokens():
                    if valid(y):
                        after(pe, out_ready, f)
                        after(pe, h1_ready, it - 1)
                        o = bank[B_FY][:, 0:TOK].rearrange("p (g t) -> p g t", t=T)
                        for k in range(T):
                            for par in range(2):
                                mm(o[halves[par], :, k:T], w_lag[:, k, :],
                                   xn1[:, r, par, :].bitcast(F32).rearrange("p (g t) -> p g t", t=T)[:, :, 0:T - k],
                                   k == 0, False)

                def states_to_output():
                    if valid(y):
                        after(pe, st_ready, y, 2)
                        ot = bank[B_FY][:, 0:TOK].rearrange("p (b j t) -> p t b j", b=NB, t=T)
                        for t in range(T):
                            for cc in range(2):
                                for par in range(2):
                                    ins = mm(ot[halves[par], t], w_st[:, cc, t, :],
                                             xst[:, NB * cc:NB * cc + NB, J * par:J * par + J], False,
                                             t == T - 1 and cc == 1)
                        ins.then_inc(y_done, 1)

                def weights_turn():
                    if valid(dd):
                        after(pe, wtok_ready, dd)
                        nc.tensor.transpose(bank[B_M][0:32, 64:192], wtok[:], ident[:]).then_inc(wt_done, 1)

                def weights_spread():
                    if valid(dd):
                        after(pe, wmask_ready, dd)
                        after(pe, wts_ready, dd)
                        mm(bank[B_M][:, 0:TOK], ehalf_r[:], wmask[:].rearrange("p q x -> p (q x)"))
                        mm(bank[B_M][:, TOK:TOK + WW], w_cst[:], wts[:]).then_inc(wb_done, 1)

                def conv_taps():
                    if valid(c):
                        x_arrived(pe, c, q)
                        after(pe, xlo_ready, c)
                        after(pe, h2_ready, y)
                        o = bank[B_FY][:, 0:TOK]
                        for k in range(3):
                            hi, lo = (v[:, :, k:k + WW] for v in (xa_hi, xa_lo))
                            mm(o, w_conv_hi[:, k, :], hi, k == 0, False)
                            mm(o, w_conv_hi[:, k, :], lo, False, False)
                            mm(o, w_conv_lo[:, k, :], hi, False, False)

                def conv_outer():
                    if valid(c):
                        for par in range(2):
                            mm(bank[B_FY][halves[par], 0:TOK], w_convC[:, par, :], xc[:, par, q], False, False)
                        mm(bank[B_FY][:, 0:TOK], w_conv[:, 3, :], xb[:, q], False, True).then_inc(conv_done, 1)

                logits()
                gate_product(0)
                gate_product(1)
                if valid(b):
                    after(pe, h_ready, b)
                    after(pe, m_ready, b - 1, 2)
                    turn(0, b, lambda t: h[:, q, t::T])
                gate_product(2)
                gate_product(3)
                mix_product(0)
                mix_product(1)
                output_turn()
                gate_product(4)
                mix_product(2)
                mix_product(3)
                weights_turn()
                own_tokens()
                weights_spread()
                gate_product(5)
                states_to_output()
                gate_product(6)
                mix_product(4)
                mix_product(5)
                after(pe, csts_ready, dd)
                turn_back(0, b)
                gate_product(7)
                if valid(y):
                    after(pe, h2_ready, y)
                    after(pe, xnt_ready[0], b) if valid(b) else after(pe, m_ready, b - 1, 2)
                    turn(1, y, lambda t: h2[:, r, t::T])
                gate_product(8)
                conv_taps()
                mix_product(6)
                mix_product(7)
                conv_outer()
                mix_product(8)

                def l1(k):
                    if valid(dd):
                        o = free_bank(it, q, G_TILES.index(("l1", k)))
                        ws = slice(128 * (k // 2), 128 * (k // 2) + 128)
                        if k == 0:
                            after(pe, xn_ready[1], dd, 2)
                        mm(o, w_l1_hi[:, ws], xn2[:, q, k % 2, :], True, False)
                        mm(o, w_l1_lo[:, ws], xn2[:, q, k % 2, :], False, True).then_inc(l1_done, 1)

                def l2(k):
                    if valid(dd):
                        o = free_bank(it, q, G_TILES.index(("l2", k)))
                        after(pe, z1_ready, dd, 8, k + 1)
                        mm(o, w_l2[:, k // 2, :], z1[:, k % 4, :]).then_inc(l2_done, 1)

                def l3(k):
                    if valid(dd):
                        if k == 0:
                            after(pe, h_ready, a)
                        after(pe, z2_ready, dd, 8, k + 1)
                        mm(bank[B_HO][halves[k % 2], 0:TOK], w_l3[:, k // 2, :], z2[:, k % 4, :], k < 2, k >= 6)\
                            .then_inc(l3_part, 1)

                l1(0)
                l1(1)
                if valid(b):
                    after(pe, xn_ready[0], b, 2)
                    after(pe, xnt_ready[1], y)
                    xn = xn1[:, q].rearrange("p r (b j t) -> p t b r j", b=NB, t=T)
                    for cc in range(2):
                        o = bank[B_T][:, 2 * BJ * cc:2 * BJ * cc + 2 * BJ].rearrange("p (b r j) -> p b r j", b=NB, r=2)
                        for t in range(T):
                            mm(o, w_in_hi[:, cc, t, :], xn[:, t], t == 0, False)
                            ins = mm(o, w_in_lo[:, cc, t, :], xn[:, t], False, t == T - 1)
                    ins.then_inc(u_done, 1)
                for k in range(8):
                    if k + 2 < 8:
                        l1(k + 2)
                    l2(k)
                    if k in (3, 5, 7):
                        l3(k - 3)
                        l3(k - 2)
                    if k == TURN_BACK_AT:
                        after(pe, xn_ready[0], b, 2) if valid(b) else after(pe, csts_ready, dd)
                        turn_back(1, y)
                l3(6)
                l3(7)
            drive(pe, body, {3: expert_weights})


_INS = ["x", "L0_tok_W1", "L0_tok_b1", "L0_tok_W2", "L0_tok_b2", "L0_tok_W3", "L0_tok_b3",
        "L0_attn_nu_log", "L0_attn_theta_log", "L0_attn_gamma_log", "L0_attn_B_re", "L0_attn_B_im",
        "L0_attn_C_re", "L0_attn_C_im", "L0_attn_D", "L0_ffn_Wr", "L0_ffn_br", "L0_ffn_W1", "L0_ffn_b1",
        "L0_ffn_g1", "L0_ffn_be1", "L0_ffn_m1", "L0_ffn_v1", "L0_ffn_W2", "L0_ffn_b2", "L0_ffn_g2",
        "L0_ffn_be2", "L0_ffn_m2", "L0_ffn_v2", "L0_ffn_Wo", "L0_ffn_bo"]


def constants(np):
    k, m = np.arange(32) % 16, np.arange(128)
    ident = np.eye(128)
    return {
        "ident": ident,
        "center": ident - (m[:, None] // C == m[None, :] // C) / C,
        "emask": (k[:, None] // NE == np.arange(8)[None, :] % 2) & (k[:, None] % NE // 2 == np.arange(8)[None, :] // 2),
        "ehalf": k[:, None] % 2 == m[None, :] // C,
        "pmask": k[:, None] // NE == np.arange(2)[None, :],
        "dup8": np.arange(8)[:, None] == k[None, :] % NE,
        "zeros": np.zeros((C, TOK)),
    }


def kernel(**inputs):
    import numpy as _np
    import concourse.bacc as _bacc
    from concourse import mybir as _mybir
    from concourse.bass_utils import run_bass_kernel_spmd as _run

    nc = _bacc.Bacc("TRN2", target_bir_lowering=False, num_devices=1)
    arrays, d = {}, {}
    given = {name: _np.ascontiguousarray(inputs[name]) for name in _INS}
    given.update({name: _np.ascontiguousarray(a, dtype=_np.float32) for name, a in constants(_np).items()})
    for name, a in given.items():
        arrays[f"in_{name}_dram"] = a
        d[name] = nc.dram_tensor(f"in_{name}_dram", a.shape, _mybir.dt.from_np(a.dtype), kind="ExternalInput").ap()
    out = nc.dram_tensor("out_0_dram", (NB, HH * WW, C), F32, kind="ExternalOutput").ap()
    build(nc, d, out)
    r = _run(nc, [arrays], core_ids=[0])
    return r.results[0]["out_0_dram"]
```

```python
from contextlib import ExitStack

import concourse.bass as bass
from concourse import mybir

F32 = mybir.dt.float32
F32R = mybir.dt.float32r
I32 = mybir.dt.int32
ALU = mybir.AluOpType
ACT = mybir.ActivationFunctionType
AX_X = mybir.AxisListType.X

NB, C, HH, WW = 8, 64, 56, 56
PAIRS = HH // 2
TOK = NB * WW
TAPS = 9
NS = 128
T = 4
J = WW // T
BJ = NB * J
CH = 2 * J
NE = 8
NQ = NE // 2
LN_EPS = 1e-5
BN_EPS = 1e-3
FULL = 6
LAST = 5
GBANKS = 4
SPLIT_FROM = 3
TURN_BACK_AT = 1
FILLS = 20

S_TILES = [("s", k) for k in range(9)]
LEAD = 3
L_TILES = [("l1", _k) for _k in range(LEAD)]
for _k in range(8):
    if _k + LEAD < 8:
        L_TILES.append(("l1", _k + LEAD))
    L_TILES.append(("l2", _k))
G_TILES = S_TILES + L_TILES
NG = len(G_TILES)
LAG = {"s": 1, "l1": 4, "l2": 4}
PER = {"s": 9, "l1": 8, "l2": 8}


CONST_AT = {"ident": (128, 0, 128), "emask": (32, 128, 8), "ehalf": (32, 136, 128),
            "pmask": (32, 264, 2), "dup8": (8, 266, 32)}
CONST_COLUMNS = 298


def valid(step):
    return not isinstance(step, int) or 0 <= step < PAIRS


def first_router(it):
    return isinstance(it, int) and it == 4


def g_bank(parity, idx):
    return (NG * parity + idx) % GBANKS


def g_previous(it, parity, idx):
    bank, back, i = g_bank(parity, idx), 0, idx - 1
    while back < 3:
        while i >= 0:
            kind, k = G_TILES[i]
            if g_bank((parity + back) % 2, i) == bank and valid(it - back - LAG[kind]):
                return kind, k, it - back - LAG[kind]
            i -= 1
        back, i = back + 1, NG - 1
    return None


def drive(eng, body, before=None):
    for it in range(FULL):
        if before and it in before:
            before[it]()
        body(it, it % 2)
    with eng.Fori(0, (PAIRS - FULL) // 2) as i:
        for k in range(2):
            body(2 * i + (FULL + k), (FULL + k) % 2)
    for it in range(PAIRS, PAIRS + LAST):
        body(it, it % 2)


def after(eng, sem, step, per=1, n=None):
    if valid(step):
        eng.wait_ge(sem, per * step + (per if n is None else n))


def middle(ap, axis, n):
    v = ap.unsqueeze(axis)
    shape = list(v.shape)
    shape[axis] = n
    return v.broadcast_to(shape)


def build(nc, d, out):
    with ExitStack() as ctx:
        def sb(name, shape, dt=F32):
            return ctx.enter_context(nc.sbuf_tensor(name, shape, dt))

        def sem(name):
            return ctx.enter_context(nc.semaphore(name))

        bank = [ctx.enter_context(nc.psum_tensor(f"bank{i}", [128, 512], F32)) for i in range(8)]
        B_HO, B_FY, B_T, B_M = 4, 5, 6, 7
        G_TURNED = (B_T, B_M)

        consts = sb("consts", [128, CONST_COLUMNS])

        def constant(name):
            rows, at, columns = CONST_AT[name]
            return consts[0:rows, at:at + columns]

        ident, emask, ehalf, pmask, dup8 = (constant(n) for n in CONST_AT)
        ehalf_r = sb("ehalf_r", [32, 128], F32R)
        w_conv = sb("w_conv", [128, 4, 128])
        w_convC = sb("w_convC", [128, 2, C])
        w_conv_hi = sb("w_conv_hi", [128, 4, 128], F32R)
        w_conv_lo = sb("w_conv_lo", [128, 4, 128], F32R)
        b1col = sb("b1col", [128, 1])
        w2raw = sb("w2raw", [128, C * TAPS])
        w_gate = sb("w_gate", [128, 9, 128])
        w_gate_hi = sb("w_gate_hi", [128, 9, 128], F32R)
        w_gate_lo = sb("w_gate_lo", [128, 9, 128], F32R)
        b2raw = sb("b2raw", [128, TAPS])
        b2col = sb("b2col", [128, 9])
        w_mixA = sb("w_mixA", [128, 8, C])
        w_mixB = sb("w_mixB", [128, 128])
        w_mixB_hi = sb("w_mixB_hi", [128, 128], F32R)
        w_mixB_lo = sb("w_mixB_lo", [128, 128], F32R)
        b3col = sb("b3col", [128, 1])
        logs = sb("logs", [128, 3])
        exps = sb("exps", [128, 3])
        mags = sb("mags", [128, 2])
        ang = sb("ang", [128, 4, 2])
        trig = sb("trig", [128, 2])
        lam = sb("lam", [128, 3, T + 1])
        rot = sb("rot", [128, 2, CH + 2])
        stepper = sb("stepper", [128, 3, 7])
        nturn = sb("nturn", [128, 1])
        powers = sb("powers", [128, 3, 16])
        small = sb("small", [128, 32])
        small_i = sb("small_i", [128, 4], I32)
        b_raw = sb("b_raw", [128, 2, 2, C])
        g_in = sb("g_in", [128, T, 2, 128])
        w_in_hi = sb("w_in_hi", [128, 2, T, NS], F32R)
        w_in_lo = sb("w_in_lo", [128, 2, T, NS], F32R)
        c_raw = sb("c_raw", [C, 2, NS])
        d_raw = sb("d_raw", [C, 2, C])
        ct = sb("ct", [128, 3, C])
        w_st = sb("w_st", [128, 2, T, C])
        w_lag = sb("w_lag", [128, T, C])
        decay = sb("decay", [128, 2 * NB * (CH + 1)])
        praw = sb("praw", [40, 128])
        pcol = sb("pcol", [128, 10, NQ])
        acol = sb("acol", [128, 2, NQ])
        bnhalf = sb("bnhalf", [128, 2 * NQ])
        adiag = sb("adiag", [128, 2 * NQ, 128])
        onesq = sb("onesq", [128, 128])
        w_l1 = sb("w_l1", [128, NE * C])
        w_l1_hi = sb("w_l1_hi", [128, NE * C], F32R)
        w_l1_lo = sb("w_l1_lo", [128, NE * C], F32R)
        w_l2 = sb("w_l2", [128, NQ, 128])
        w_l2_hi = sb("w_l2_hi", [128, NQ, 128], F32R)
        w_l2_lo = sb("w_l2_lo", [128, NQ, 128], F32R)
        w_l3 = sb("w_l3", [128, NQ, C])
        c1col = sb("c1col", [128, NQ])
        nc2col = sb("nc2col", [128, NQ])
        c2m = sb("c2m", [128, NQ, 32])
        bo_raw = sb("bo_raw", [8, C])
        w_cst = sb("w_cst", [32, 128])
        wr_raw = sb("wr_raw", [128, NE])
        w_rt = sb("w_rt", [128, 16])
        br_row = sb("br_row", [1, 2, NE])
        ones_row = sb("ones_row", [1, 128])
        halfpow = sb("halfpow", [112, 8])

        xa = sb("xa", [128, 2, NB, WW + 2])
        xb = sb("xb", [128, 2, NB, WW])
        xc = sb("xc", [128, 2, 2, NB, WW])
        xa_hi = sb("xa_hi", [128, NB, WW + 2], F32R)
        xa_lo = sb("xa_lo", [128, NB, WW + 2], F32R)
        xb_hi = sb("xb_hi", [128, NB, WW], F32R)
        xb_lo = sb("xb_lo", [128, NB, WW], F32R)
        h1 = sb("h1", [128, 2, TOK])
        h1_hi = sb("h1_hi", [128, TOK], F32R)
        h1_lo = sb("h1_lo", [128, TOK], F32R)
        h1s = sb("h1s", [128, 2, 2, TOK], F32R)
        gate = sb("gate", [128, 4, TOK])
        gated = sb("gated", [128, 4, TOK])
        gated8_hi = sb("gated8_hi", [128, TOK], F32R)
        gated8_lo = sb("gated8_lo", [128, TOK], F32R)
        h = sb("h", [128, 2, TOK])
        hsum = sb("hsum", [BJ, 2, 8])
        hcent = sb("hcent", [BJ, 2, 512])
        sq = sb("sq", [BJ, 2, 512])
        ssum = sb("ssum", [BJ, 2, 8])
        varr = sb("varr", [BJ, 2, 8])
        rstd = sb("rstd", [BJ, 2, 8])
        xnt = sb("xnt", [BJ, 2, 512])
        xn1 = sb("xn1", [128, 2, 2, TOK], F32R)
        xn2 = sb("xn2", [128, 2, 2, TOK], F32R)
        m_cos = sb("m_cos", [128, 2 * NB, CH])
        m_sin = sb("m_sin", [128, 2 * NB, CH])
        u = sb("u", [128, 2 * NB, CH + 1])
        z = sb("z", [128, 2 * NB, CH + 1])
        n_cos = sb("n_cos", [128, 2 * NB, CH])
        n_sin = sb("n_sin", [128, 2 * NB, CH])
        xst = sb("xst", [128, 2 * NB, CH])
        h2 = sb("h2", [128, 2, TOK])
        fsum = sb("fsum", [128, WW])
        lmax = sb("lmax", [WW, 2])
        lsub = sb("lsub", [WW, 16])
        lexp = sb("lexp", [WW, 16])
        lsum = sb("lsum", [WW, 2])
        lrec = sb("lrec", [WW, 2])
        wfull = sb("wfull", [WW, 16])
        wtok = sb("wtok", [128, 32])
        wmask = sb("wmask", [32, 8, WW], F32R)
        wts = sb("wts", [32, WW])
        csts = sb("csts", [128, WW])
        h2c = sb("h2c", [128, TOK])
        wbs = sb("wbs", [128, 8, WW])
        z1 = sb("z1", [128, 4, TOK])
        z1_hi = sb("z1_hi", [128, 4, TOK], F32R)
        z1_lo = sb("z1_lo", [128, 4, TOK], F32R)
        z2 = sb("z2", [128, 4, TOK])
        fin = sb("fin", [128, TOK])
        ostage = sb("ostage", [BJ, 2, 2, T * C])

        consts_in = sem("consts_in")
        gate_in = sem("gate_in")
        conv_in = sem("conv_in")
        mix_in = sem("mix_in")
        logs_in = sem("logs_in")
        ssm_in = sem("ssm_in")
        ffn_in = sem("ffn_in")
        pads_zeroed = sem("pads_zeroed")
        gate_assembled = sem("gate_assembled")
        tok_high = sem("tok_high")
        tok_weights = sem("tok_weights")
        mixb_ready = sem("mixb_ready")
        angles_ready = sem("angles_ready")
        trig_ready = sem("trig_ready")
        g_ready = sem("g_ready")
        ct_turned = sem("ct_turned")
        ct_ready = sem("ct_ready")
        lag_made = sem("lag_made")
        win_turned = sem("win_turned")
        ssm_weights = sem("ssm_weights")
        bnvar_ready = sem("bnvar_ready")
        bnpow_ready = sem("bnpow_ready")
        pcol_made = sem("pcol_made")
        adiag_ready = sem("adiag_ready")
        arow_made = sem("arow_made")
        cst_made = sem("cst_made")
        ffn_weights = sem("ffn_weights")
        dve_chain = sem("dve_chain")
        x_split = sem("x_split")
        xlo_ready = sem("xlo_ready")
        xb_split = sem("xb_split")
        xblo_ready = sem("xblo_ready")
        conv_done = sem("conv_done")
        h1hi_ready = sem("h1hi_ready")
        h1s_ready = sem("h1s_ready")
        h1_ready = sem("h1_ready")
        h1r_ready = sem("h1r_ready")
        h1lo_ready = sem("h1lo_ready")
        s_done = sem("s_done")
        gate_ready = sem("gate_ready")
        gated_ready = sem("gated_ready")
        g8_split = sem("g8_split")
        g8lo_ready = sem("g8lo_ready")
        mix_part = sem("mix_part")
        h_ready = sem("h_ready")
        u_done = sem("u_done")
        m_ready = sem("m_ready")
        uin_ready = sem("uin_ready")
        carry_a = sem("carry_a")
        carry_b = sem("carry_b")
        z_ready = sem("z_ready")
        n_ready = sem("n_ready")
        st_ready = sem("st_ready")
        y_done = sem("y_done")
        h2_ready = sem("h2_ready")
        fsum_ready = sem("fsum_ready")
        rt_done = sem("rt_done")
        lmax_ready = sem("lmax_ready")
        lsub_ready = sem("lsub_ready")
        lexp_ready = sem("lexp_ready")
        lsum_ready = sem("lsum_ready")
        lrec_ready = sem("lrec_ready")
        wfull_ready = sem("wfull_ready")
        whi_ready = sem("whi_ready")
        wtok_ready = sem("wtok_ready")
        wt_done = sem("wt_done")
        wmask_ready = sem("wmask_ready")
        wts_ready = sem("wts_ready")
        wb_done = sem("wb_done")
        wbs_ready = sem("wbs_ready")
        csts_ready = sem("csts_ready")
        h2c_ready = sem("h2c_ready")
        l1_done = sem("l1_done")
        z1_ready = sem("z1_ready")
        z1lo_ready = sem("z1lo_ready")
        l2_done = sem("l2_done")
        z2_ready = sem("z2_ready")
        l3_part = sem("l3_part")
        fin_ready = sem("fin_ready")
        ot_done = sem("ot_done")
        out_ready = sem("out_ready")
        x_in = [sem("x_in0"), sem("x_in1")]
        stored = [sem("stored0"), sem("stored1")]
        ft_done = [sem("ft_done0"), sem("ft_done1")]
        hsum_ready = [sem("hsum_ready0"), sem("hsum_ready1")]
        hcent_ready = [sem("hcent_ready0"), sem("hcent_ready1")]
        sq_ready = [sem("sq_ready0"), sem("sq_ready1")]
        ssum_ready = [sem("ssum_ready0"), sem("ssum_ready1")]
        var_ready = [sem("var_ready0"), sem("var_ready1")]
        rstd_ready = [sem("rstd_ready0"), sem("rstd_ready1")]
        xnt_ready = [sem("xnt_ready0"), sem("xnt_ready1")]
        bt_done = [sem("bt_done0"), sem("bt_done1")]
        xhi_ready = [sem("xhi_ready0"), sem("xhi_ready1")]
        xn_ready = [sem("xn_ready0"), sem("xn_ready1")]

        x_rows = d["x"].rearrange("b c (p q) w -> q p c b w", q=2)
        o_rows = out.rearrange("b (p q j t) c -> q p b j (t c)", q=2, j=J, t=T)
        w1v = d["L0_tok_W1"].rearrange("(c ki kj) n -> c ki kj n", ki=3, kj=3)
        w3v = d["L0_tok_W3"].rearrange("(c ki kj) n -> c ki kj n", ki=3, kj=3)
        halves = (slice(0, 64), slice(64, 128))
        other = (halves[1], halves[0])

        def gate_input(k, r):
            if k < 6:
                return xa[:, r, :, k // 2:k // 2 + WW]
            return xc[:, k - 6, r] if k < 8 else xb[:, r]

        loads = {"consts": 1, "gate": 4, "conv": 0, "mix": 0, "logs": 3, "ssm": 0, "ffn": 0}

        def twice(src, axis=0):
            return middle(src, axis, 2)

        block = ctx.enter_context(nc.Block())

        def x_arrived(eng, s, q):
            eng.wait_ge(x_in[q], 64 * s + (128 - 64 * q))

        @block.sync
        def _(sp):
            def load_x(s, q):
                if not valid(s):
                    return
                if not (isinstance(s, int) and s < 2):
                    after(sp, conv_done, s - 2)
                    after(sp, gated_ready, s - 2, 9)
                below = xz_view() if isinstance(s, int) and s == PAIRS - 1 else x_rows[0][s + 1]
                above = xz_view() if isinstance(s, int) and s == 0 else x_rows[1][s - 1]
                for half in range(2):
                    sp.dma_start(xa[halves[half], q, :, 1:WW + 1], x_rows[half][s]).then_inc(x_in[q], 16)
                    sp.dma_start(xb[halves[half], q, :, 0:WW - 1], (below, above)[half][:, :, 1:WW]).then_inc(x_in[q], 16)
                for par, row in ((0, above), (1, below)):
                    sp.dma_start(xc[0:64, par, q, :, 1:WW], row[:, :, 0:WW - 1]).then_inc(x_in[q], 16)
                    sp.dma_start(xc[64:128, par, q], row).then_inc(x_in[q], 16)

            def xz_view():
                return d["zeros"].rearrange("c (b w) -> c b w", b=NB)

            def ld(group, dst, src):
                loads[group] += 1
                sp.dma_start(dst, src).then_inc({"conv": conv_in, "mix": mix_in, "ssm": ssm_in, "ffn": ffn_in}[group], 16)

            for k, n in enumerate(("nu_log", "theta_log", "gamma_log")):
                sp.dma_start(logs[:, k:k + 1], d[f"L0_attn_{n}"].rearrange("(c k) -> c k", k=1)).then_inc(logs_in, 16)
            for k, n in enumerate(("re", "im")):
                ld("ssm", c_raw[:, k, :], d[f"L0_attn_C_{n}"])
                ld("ssm", b_raw[:, k], twice(d[f"L0_attn_B_{n}"], 1))
            ld("ssm", d_raw[:], twice(d["L0_attn_D"], 1))
            for w, src in (("conv", w1v), ("mix", w3v)):
                for half, col, ki in ((0, 0, 1), (0, 1, 0), (1, 0, 2), (1, 1, 1)):
                    if w == "conv":
                        dst = w_conv[halves[half], 0:3, halves[col]]
                    else:
                        dst = w_mixA[:, 0:6].rearrange("p (kj k) n -> p k kj n", k=2)[halves[half], col]
                    ld(w, dst, src[:, ki])
                for par, ki in ((0, 0), (1, 2)):
                    ld(w, w_convC[:, par] if w == "conv" else w_mixA[:, 6 + par],
                       src[:, ki, 0:2].rearrange("c kj n -> kj c n"))
                    ld(w, (w_conv[:, 3] if w == "conv" else w_mixB)[other[par], halves[par]], src[:, ki, 2])
                if w == "conv":
                    load_x(0, 0)
            load_x(1, 1)
            for k, n in enumerate(("b1", "m1", "be1", "b2", "m2", "be2", "g1", "g2", "v1", "v2")):
                ld("ffn", praw[NQ * k:NQ * k + NQ, :], d[f"L0_ffn_{n}"].rearrange("(q e) h -> q (e h)", e=2))
            for hf in halves:
                ld("ffn", w_l1[hf, :].rearrange("p (e h) -> p e h", e=NE), d["L0_ffn_W1"].rearrange("e d h -> d e h"))
            ld("ffn", wr_raw[:], twice(d["L0_ffn_Wr"]))
            w2v = d["L0_ffn_W2"].rearrange("(q e) h k -> e h q k", e=2)
            for e in range(2):
                ld("ffn", w_l2[halves[e], :, halves[e]], w2v[e])
            ld("ffn", w_l3[:], d["L0_ffn_Wo"].rearrange("(q e) h k -> (e h) q k", e=2))
            ld("ffn", bo_raw[:], d["L0_ffn_bo"])
            ld("ffn", br_row[:], twice(d["L0_ffn_br"].rearrange("(o e) -> o e", o=1), 1))

            def store(s, q):
                if valid(s):
                    after(sp, out_ready, s)
                    for par in range(2):
                        sp.dma_start(o_rows[par][s], ostage[:, q, par, :]).then_inc(stored[q], 16)

            def body_io(it, q):
                s = it + 1
                if not isinstance(s, int) or s >= 2:
                    load_x(s, (q + 1) % 2)
                store(it - 5, (q + 1) % 2)

            for it in range(FULL):
                body_io(it, it % 2)
            with sp.Fori(0, (PAIRS - FULL) // 2 - 1) as i:
                for k in range(2):
                    body_io(2 * i + (FULL + k), (FULL + k) % 2)
            for it in range(PAIRS - 2, PAIRS + LAST):
                body_io(it, it % 2)
            for q in range(2):
                sp.wait_ge(stored[q], 16 * PAIRS)

        @block.gpsimd
        def _(pool):
            fills = [(xa[:, :, :, 0:1], 0.0), (xa[:, :, :, WW + 1:WW + 2], 0.0), (xb[:, :, :, WW - 1:WW], 0.0),
                     (xc[0:64, :, :, :, 0:1], 0.0), (w_conv[0:64, 3, 0:64], 0.0), (w_conv[64:128, 3, 64:128], 0.0),
                     (w_mixB[0:64, 0:64], 0.0), (w_mixB[64:128, 64:128], 0.0), (w_gate[0:64, 8, 0:64], 0.0),
                     (w_gate[64:128, 8, 64:128], 0.0), (w_l2[0:64, :, 64:128], 0.0), (ones_row[:], 1.0), (onesq[:], 1.0),
                     (w_l2[64:128, :, 0:64], 0.0), (c2m[:], 0.0), (wtok[:], 0.0), (w_rt[:], 0.0),
                     (u[:], 0.0), (halfpow[:], -0.5), (bnhalf[:], -0.5)]
            assert len(fills) == FILLS
            for k, (tile, value) in enumerate(fills):
                nc.gpsimd.memset(tile, value).then_inc(pads_zeroed, 1)
                pool.wait_ge(pads_zeroed, k + 1)

            pool.wait_ge(tok_high, 1)
            nc.gpsimd.tensor_tensor(w_gate_lo[:], w_gate[:], w_gate_hi[:].bitcast(F32), ALU.subtract)\
                .then_inc(tok_weights, 1)
            pool.wait_ge(tok_high, 2)
            nc.gpsimd.tensor_tensor(w_conv_lo[:], w_conv[:], w_conv_hi[:].bitcast(F32), ALU.subtract)\
                .then_inc(tok_weights, 1)
            def mix_weights():
                pool.wait_ge(mix_in, 16 * loads["mix"])
                nc.gpsimd.tensor_scalar(w_mixB[:], w_mixB[:], 0.5, None, ALU.mult).then_inc(mixb_ready, 1)
                pool.wait_ge(mixb_ready, 1)
                nc.gpsimd.tensor_copy(w_mixB_hi[:], w_mixB[:]).then_inc(mixb_ready, 1)
                pool.wait_ge(mixb_ready, 2)
                nc.gpsimd.tensor_tensor(w_mixB_lo[:], w_mixB[:], w_mixB_hi[:].bitcast(F32), ALU.subtract).then_inc(tok_weights, 1)
                nc.gpsimd.tensor_scalar(w_mixA[:], w_mixA[:], 0.5, None, ALU.mult).then_inc(tok_weights, 1)

            def batch_norms():
                pool.wait_ge(bnvar_ready, 1)
                nc.gpsimd.tensor_tensor(acol[:].rearrange("p a q -> p (a q)"),
                                        acol[:].rearrange("p a q -> p (a q)"), bnhalf[:], ALU.pow).then_inc(bnpow_ready, 1)

            def body(it, q):
                c, a, b, y, dd = it, it - 1, it - 2, it - 3, it - 4
                if valid(b):
                    after(pool, var_ready[0], b)
                    after(pool, xnt_ready[0], b - 1)
                    nc.gpsimd.tensor_tensor(rstd[:, 0, :], varr[:, 0, :], halfpow[:], ALU.pow).then_inc(rstd_ready[0], 1)
                if valid(c):
                    after(pool, x_split, c)
                    nc.gpsimd.tensor_tensor(xa_lo[:], xa[:, q], xa_hi[:].bitcast(F32), ALU.subtract).then_inc(xlo_ready, 1)
                    after(pool, xb_split, c)
                    nc.gpsimd.tensor_tensor(xb_lo[:], xb[:, q], xb_hi[:].bitcast(F32), ALU.subtract).then_inc(xblo_ready, 1)
                if isinstance(it, int) and it == 0:
                    mix_weights()
                if valid(dd):
                    after(pool, csts_ready, dd)
                    after(pool, h2_ready, dd)
                    after(pool, fin_ready, dd - 1)
                    nc.gpsimd.tensor_tensor(h2c[:].rearrange("p (b w) -> p b w", b=NB),
                                            h2[:, q, :].rearrange("p (b w) -> p b w", b=NB), middle(csts[:], 1, NB),
                                            ALU.add).then_inc(h2c_ready, 1)

                if valid(a):
                    after(pool, g8_split, a)
                    nc.gpsimd.tensor_tensor(gated8_lo[:], gated[:, 8 % 4, :], gated8_hi[:].bitcast(F32), ALU.subtract)\
                        .then_inc(g8lo_ready, 1)
                if valid(y):
                    after(pool, var_ready[1], y)
                    after(pool, xnt_ready[1], y - 1)
                    nc.gpsimd.tensor_tensor(rstd[:, 1, :], varr[:, 1, :], halfpow[:], ALU.pow).then_inc(rstd_ready[1], 1)
                def low_hidden(k):
                    if valid(dd):
                        after(pool, z1_ready, dd, 8, k + 1)
                        nc.gpsimd.tensor_tensor(z1_lo[:, k % 4, :], z1[:, k % 4, :], z1_hi[:, k % 4, :].bitcast(F32),
                                                ALU.subtract).then_inc(z1lo_ready, 1)

                if valid(b):
                    after(pool, m_ready, b, 2)
                    after(pool, z_ready, b - 1)
                    nc.gpsimd.tensor_tensor(u[:, 0:NB, 1:], m_cos[:, 0:NB], m_sin[:, NB:], ALU.add).then_inc(uin_ready, 1)
                    nc.gpsimd.tensor_tensor(u[:, NB:, 1:], m_cos[:, NB:], m_sin[:, 0:NB], ALU.subtract).then_inc(uin_ready, 1)
                for k in range(SPLIT_FROM, 8):
                    low_hidden(k)
                if valid(b):
                    after(pool, n_ready, b, 2)
                    after(pool, y_done, b - 1)
                    nc.gpsimd.tensor_tensor(xst[:, 0:NB], n_cos[:, 0:NB], n_sin[:, NB:], ALU.subtract).then_inc(st_ready, 1)
                    nc.gpsimd.tensor_tensor(xst[:, NB:], n_cos[:, NB:], n_sin[:, 0:NB], ALU.add).then_inc(st_ready, 1)

                if valid(c):
                    after(pool, h1r_ready, c)
                    nc.gpsimd.tensor_tensor(h1_lo[:], h1[:, q, :], h1_hi[:].bitcast(F32), ALU.subtract).then_inc(h1lo_ready, 1)

            drive(pool, body, {2: batch_norms})

        @block.scalar
        def _(act):
            act.dma_start(consts[:], d["consts"]).then_inc(consts_in, 16)
            act.dma_start(w2raw[:], twice(d["L0_tok_W2"])).then_inc(gate_in, 16)
            act.dma_start(b2raw[:], twice(d["L0_tok_b2"].rearrange("(c k) -> c k", k=TAPS))).then_inc(gate_in, 16)
            act.dma_start(b1col[:], twice(d["L0_tok_b1"].rearrange("(c k) -> c k", k=1))).then_inc(gate_in, 16)
            act.dma_start(b3col[:], twice(d["L0_tok_b3"].rearrange("(c k) -> c k", k=1))).then_inc(gate_in, 16)
            act.wait_ge(angles_ready, 1)
            nc.scalar.activation(trig[:], ang[:, 3, :], ACT.Sin).then_inc(trig_ready, 1)
            act.wait_ge(pads_zeroed, FILLS)
            act.wait_ge(gate_in, 16 * loads["gate"])
            w2t = w2raw[:].rearrange("p (c ki kj) -> p ki kj c", ki=3, kj=3)
            b2t = b2raw[:].rearrange("p (ki kj) -> p ki kj", ki=3)
            wg = w_gate[:, 0:6].rearrange("p (kj k) n -> p k kj n", k=2)
            b2o = b2col[:, 0:6].rearrange("p (kj k) -> p k kj", k=2)
            for par, col, ki in ((0, 0, 1), (0, 1, 2), (1, 0, 0), (1, 1, 1)):
                nc.scalar.copy(wg[:, par, :, halves[col]], w2t[:, ki])
                nc.scalar.activation(b2o[halves[col], par], b2t[halves[col], ki], ACT.Copy, scale=0.5)
            for par, ki in ((0, 0), (1, 2)):
                for kj in range(2):
                    nc.scalar.copy(w_gate[:, 6 + par, halves[kj]], w2t[:, ki, kj])
                    nc.scalar.activation(b2col[halves[kj], 6 + par:7 + par], b2t[halves[kj], ki, kj:kj + 1], ACT.Copy,
                                         scale=0.5)
                nc.scalar.activation(b2col[other[par], 8:9], b2t[other[par], ki, 2:3], ACT.Copy, scale=0.5)
                nc.scalar.copy(w_gate[halves[par], 8, other[par]], w2t[halves[par], ki, 2]).then_inc(gate_assembled, 1)
            act.wait_ge(gate_assembled, 2)
            nc.scalar.copy(w_gate_hi[:], w_gate[:]).then_inc(tok_high, 1)
            act.wait_ge(conv_in, 16 * loads["conv"])
            nc.scalar.copy(w_conv_hi[:], w_conv[:]).then_inc(tok_high, 1)

            def square(ln, s, q):
                if valid(s):
                    after(act, hcent_ready[ln], s)
                    after(act, ssum_ready[ln], s - 1)
                    nc.scalar.activation(sq[:, ln, :], hcent[:, ln, :], ACT.Square).then_inc(sq_ready[ln], 1)

            def turned_back(ln, s, q, dst):
                if valid(s):
                    after(act, bt_done[ln], s)
                    for par in range(2):
                        v = bank[B_M][halves[par], 0:TOK].rearrange("p (t g) -> p g t", t=T)
                        nc.scalar.copy(dst[halves[par], q, par, :].rearrange("p (g t) -> p g t", t=T), v)\
                            .then_inc(xhi_ready[ln], 1)

            def body(it, q):
                c, a, b, y, dd, f = it, it - 1, it - 2, it - 3, it - 4, it - 5
                r = (q + 1) % 2
                def tanh(k):
                    if valid(a):
                        after(act, s_done, a, 9, k + 1)
                        after(act, gated_ready, a if k >= 4 else a - 1, 9, k - 3 if k >= 4 else k + 6)
                        g = bank[g_bank(q, k)][:, 0:TOK]
                        nc.scalar.activation(gate[:, k % 4, :], g, ACT.Tanh, bias=b2col[:, k:k + 1], scale=0.5)\
                            .then_inc(gate_ready, 1)

                def softmax_exp():
                    if valid(dd):
                        after(act, lsub_ready, dd)
                        after(act, lsum_ready, dd - 1)
                        nc.scalar.activation(lexp[:], lsub[:], ACT.Exp).then_inc(lexp_ready, 1)

                tanh(0)
                tanh(1)
                if not first_router(it):
                    softmax_exp()
                if valid(f):
                    after(act, ot_done, f)
                    if valid(f - 2):
                        act.wait_ge(stored[r], 32 * (((f - 2) if isinstance(f, int) else f - 2) // 2) + 32) \
                            if isinstance(f, int) else act.wait_ge(stored[r], 16 * (f - 2) + (32 if r == 0 else 16))
                    nc.scalar.copy(ostage[:, r].rearrange("p q (t c) -> p t q c", t=T),
                                   bank[B_FY][0:BJ, :].rearrange("p (t q c) -> p t q c", t=T, q=2)).then_inc(out_ready, 1)
                tanh(2)
                tanh(3)
                square(0, b, q)
                if first_router(it):
                    softmax_exp()
                tanh(4)
                tanh(5)
                if valid(c):
                    x_arrived(act, c, q)
                    after(act, conv_done, c - 1)
                    nc.scalar.copy(xb_hi[:], xb[:, q]).then_inc(xb_split, 1)
                if valid(dd):
                    after(act, wb_done, dd)
                    after(act, z2_ready, dd - 1, 8)
                    nc.scalar.copy(wbs[:], bank[B_M][:, 0:TOK].rearrange("p (q x) -> p q x", q=8)).then_inc(wbs_ready, 1)
                    after(act, h2c_ready, dd - 1)
                    nc.scalar.copy(csts[:], bank[B_M][:, TOK:TOK + WW]).then_inc(csts_ready, 1)
                tanh(6)
                tanh(7)
                if valid(b):
                    after(act, y_done, b - 2)
                turned_back(0, b, q, xn1)
                tanh(8)
                if valid(a):
                    after(act, gated_ready, a, 9)
                    after(act, mix_part, a - 1, 9)
                    nc.scalar.copy(gated8_hi[:], gated[:, 8 % 4, :]).then_inc(g8_split, 1)
                square(1, y, r)
                if valid(c):
                    after(act, conv_done, c)
                    after(act, s_done, c - 2, 9)
                    for par in range(2):
                        nc.scalar.activation(h1s[halves[par], q, par, :], bank[B_FY][halves[par], 0:TOK], ACT.Relu,
                                             bias=b1col[halves[par], 0:1]).then_inc(h1hi_ready, 1)
                    nc.scalar.activation(h1[:, q, :], bank[B_FY][:, 0:TOK], ACT.Relu, bias=b1col[:, 0:1]).then_inc(h1_ready, 1)
                if valid(a):
                    after(act, mix_part, a, 9)
                    after(act, h2_ready, a - 2)
                    nc.scalar.activation(h[:, r, :], bank[B_HO][:, 0:TOK], ACT.Identity, bias=b3col[:, 0:1]).then_inc(h_ready, 1)
                for k in range(8):
                    if k == TURN_BACK_AT + LEAD + 1 and valid(y):
                        after(act, l1_done, y - 2, 8)
                        turned_back(1, y, r, xn2)
                    if valid(dd):
                        after(act, l1_done, dd, 8, k + 1)
                        after(act, l2_done, dd if k >= 4 else dd - 1, 8, k - 3 if k >= 4 else k + 5)
                        g = bank[g_bank(q, G_TILES.index(("l1", k)))][:, 0:TOK]
                        if k >= SPLIT_FROM:
                            nc.scalar.activation(z1_hi[:, k % 4, :], g, ACT.Relu, bias=c1col[:, k // 2:k // 2 + 1])
                        nc.scalar.activation(z1[:, k % 4, :], g, ACT.Relu, bias=c1col[:, k // 2:k // 2 + 1])\
                            .then_inc(z1_ready, 1)

                if valid(c):
                    after(act, h1_ready, c)
                    after(act, s_done, c - 1, 9)
                    nc.scalar.copy(h1_hi[:], h1[:, q, :]).then_inc(h1r_ready, 1)

            drive(act, body, {4: lambda: act.wait_ge(ffn_weights, 1)})

        @block.vector
        def _(dve):
            chain = [0]

            def link(ins):
                chain[0] += 1
                ins.then_inc(dve_chain, 1)
                dve.wait_ge(dve_chain, chain[0])

            V = nc.vector
            def exp_of(dst, x, width):
                n, p, sc = small[:, 0:width], small[:, 8:8 + width], small_i[:, 0:width]
                red = small[:, 16:16 + width]
                link(V.tensor_scalar(n, x, 1.4426950408889634, MAGIC, ALU.mult, ALU.add))
                link(V.tensor_scalar(n, n, MAGIC, None, ALU.subtract))
                link(V.tensor_scalar(n, n, -126.0, 127.0, ALU.max, ALU.min))
                link(V.scalar_tensor_tensor(red, n, -0.693145751953125, x, ALU.mult, ALU.add))
                link(V.scalar_tensor_tensor(red, n, -1.4286068203094172e-06, red, ALU.mult, ALU.add))
                link(V.tensor_scalar(p, red, 1.0 / 5040.0, None, ALU.mult))
                for f in (720.0, 120.0, 24.0, 6.0, 2.0, 1.0):
                    link(V.scalar_tensor_tensor(p, p, 1.0 / f, red, ALU.add, ALU.mult))
                link(V.tensor_scalar(p, p, 1.0, None, ALU.add))
                link(V.tensor_scalar(sc, n, 127.0, 8388608.0, ALU.add, ALU.mult))
                link(V.tensor_tensor(dst, p, sc.bitcast(F32), ALU.mult))

            TWO_PI_HI, TWO_PI_LO, MAGIC = 6.28125, 0.0019353071795864769, 12582912.0
            dve.wait_ge(logs_in, 16 * loads["logs"])
            exp_of(exps[:], logs[:], 3)
            V.tensor_copy(ang[:, 0, 0:1], exps[:, 1:2])
            link(V.tensor_scalar(ang[:, 0, 1:2], exps[:, 1:2], 1.5707963267948966, None, ALU.add))
            link(V.tensor_scalar(ang[:, 1, :], ang[:, 0, :], 0.15915494309189535, MAGIC, ALU.mult, ALU.add))
            link(V.tensor_scalar(ang[:, 1, :], ang[:, 1, :], MAGIC, None, ALU.subtract))
            link(V.scalar_tensor_tensor(ang[:, 2, :], ang[:, 1, :], -TWO_PI_HI, ang[:, 0, :], ALU.mult, ALU.add))
            link(V.scalar_tensor_tensor(ang[:, 3, :], ang[:, 1, :], -TWO_PI_LO, ang[:, 2, :], ALU.mult, ALU.add))
            V.tensor_scalar(ang[:, 3, :], ang[:, 3, :], 3.1415925, -3.1415925, ALU.min, ALU.max).then_inc(angles_ready, 1)

            V.tensor_scalar(small[:, 24:25], exps[:, 0:1], -1.0, None, ALU.mult)
            link(V.tensor_scalar(small[:, 25:26], exps[:, 0:1], -float(T), None, ALU.mult))
            exp_of(mags[:], small[:, 24:26], 2)
            dve.wait_ge(ssm_in, 16 * loads["ssm"])
            dve.wait_ge(pads_zeroed, FILLS)
            dve.wait_ge(trig_ready, 1)
            def first_term(at, x, s, w):
                return V.tensor_scalar(powers[:, 0:x.shape[1], at:at + w], x, s[0], None, ALU.mult)

            def second_term(dst, at, x, s, w):
                V.scalar_tensor_tensor(dst[:, 0], x[:, 1], s[2], powers[:, 0, at:at + w], ALU.mult, ALU.add)
                ins = V.scalar_tensor_tensor(dst[:, 1], x[:, 0], s[1], powers[:, 1, at:at + w], ALU.mult, ALU.add)
                if dst.shape[1] == 3:
                    ins = V.scalar_tensor_tensor(dst[:, 2], x[:, 0], s[2], powers[:, 2, at:at + w], ALU.mult, ALU.add)
                return ins

            def column(numbers, k):
                return [numbers[:, c, k:k + 1] for c in range(3)]

            V.memset(lam[:, 0, 0:1], 1.0)
            V.memset(lam[:, 1:3, 0:1], 0.0)
            V.memset(rot[:, 0, 1:2], 1.0)
            V.memset(rot[:, 1, 1:2], 0.0)
            V.memset(decay[:], 0.0)
            for first, m in ((lam[:, :, 1:2], mags[:, 0:1]), (stepper[:, :, 0:1], 1.0)):
                V.tensor_scalar(first[:, 0], trig[:, 1:2], m, None, ALU.mult)
                V.tensor_scalar(first[:, 1], trig[:, 0:1], m, None, ALU.mult)
                ins = V.tensor_scalar(first[:, 2], trig[:, 0:1], m, -1.0, ALU.mult, ALU.mult)
            link(ins)
            dv = decay[:].rearrange("p (g c) -> p g c", c=CH + 1)
            V.tensor_scalar(dv[:, :, 1:], dv[:, :, 1:], mags[:, 1:2], None, ALU.add)
            V.tensor_scalar(g_in[:, 0], b_raw[:].rearrange("p k a c -> p k (a c)"), exps[:, 2:3], None, ALU.mult)
            for m in range(1, 8):
                s, n = column(stepper, m - 1), 1 << max(m - 3, 0)
                w = min(n, CH + 1 - n)
                if m < 3:
                    first_term(4, lam[:, :, 1:1 + m], column(lam, m), m)
                if m < 7:
                    ins = first_term(6, stepper[:, :, m - 1:m], s, 1)
                if m >= 3:
                    ins = V.tensor_scalar(rot[:, :, 1 + n:1 + n + w], rot[:, :, 1:1 + w], s[0], None, ALU.mult)
                link(ins)
                if m < 3:
                    second_term(lam[:, :, m + 1:2 * m + 1], 4, lam[:, :, 1:1 + m], column(lam, m), m)
                if m < 7:
                    ins = second_term(stepper[:, :, m:m + 1], 6, stepper[:, :, m - 1:m], s, 1)
                if m >= 3:
                    for c, other_c, si in ((0, 1, s[2]), (1, 0, s[1])):
                        dst = rot[:, c, 1 + n:1 + n + w]
                        ins = V.scalar_tensor_tensor(dst, rot[:, other_c, 1:1 + w], si, dst, ALU.mult, ALU.add)
                if m == 3:
                    V.tensor_copy(rot[:, 0, 0:1], stepper[:, 0, 2:3])
                    ins = V.tensor_copy(rot[:, 1, 0:1], stepper[:, 2, 2:3])
                link(ins)
            turn_r, turn_i, nturn_i = rot[:, 0, CH + 1:CH + 2], rot[:, 1, CH + 1:CH + 2], nturn[:]
            V.tensor_scalar(nturn_i, turn_i, -1.0, None, ALU.mult)

            x_arrived(dve, 0, 0)
            V.tensor_copy(xa_hi[:], xa[:, 0]).then_inc(x_split, 1)
            for k in range(1, T):
                ins = V.tensor_scalar(g_in[:, k], g_in[:, 0], lam[:, 0, k:k + 1], None, ALU.mult)
            link(ins)
            for k in range(1, T):
                for c, si in ((0, 2), (1, 1)):
                    ins = V.scalar_tensor_tensor(g_in[:, k, c], g_in[:, 0, 1 - c], lam[:, si, k:k + 1], g_in[:, k, c],
                                                 ALU.mult, ALU.add)
            ins.then_inc(g_ready, 1)
            dve.wait_ge(ct_turned, 1)
            V.tensor_copy(ct[:, 0, :], bank[2][:, 0:C])
            V.tensor_copy(ct[:, 2, :], bank[2][:, C:2 * C])
            V.tensor_scalar(ct[:, 1, :], bank[2][:, C:2 * C], -1.0, None, ALU.mult).then_inc(ct_ready, 1)
            dve.wait_ge(ct_ready, 1)
            for t in range(T):
                ins = V.tensor_scalar(w_st[:, :, t, :], ct[:, 0:2, :], lam[:, 0, t + 1:t + 2], None, ALU.mult)
            link(ins)
            for t in range(T):
                for cc, x in ((0, 2), (1, 0)):
                    V.scalar_tensor_tensor(w_st[:, cc, t, :], ct[:, x, :], lam[:, 2, t + 1:t + 2], w_st[:, cc, t, :],
                                           ALU.mult, ALU.add)

            def lag_weights():
                dve.wait_ge(lag_made, 1)
                V.tensor_copy(w_lag[:], bank[B_HO][:, 0:T * C].rearrange("p (k c) -> p k c", k=T))

            def chunk_input_weights():
                dve.wait_ge(win_turned, 2)
                turned = [bank[G_TURNED[k // 2]][:, 256 * (k % 2):256 * (k % 2) + 256].rearrange("p (c n) -> p c n", c=2)
                          for k in range(T)]
                for k in range(T):
                    ins = V.tensor_copy(w_in_hi[:, :, T - 1 - k], turned[k])
                link(ins)
                for k in range(T):
                    ins = V.tensor_tensor(w_in_lo[:, :, T - 1 - k], turned[k], w_in_hi[:, :, T - 1 - k].bitcast(F32),
                                          ALU.subtract)
                ins.then_inc(ssm_weights, 1)

            def batch_norm_columns():
                dve.wait_ge(ffn_in, 16 * loads["ffn"])
                dve.wait_ge(pcol_made, 1)
                link(V.tensor_copy(pcol[:].rearrange("p a q -> p (a q)"), bank[B_M][:, 0:40]))
                V.tensor_scalar(acol[:], pcol[:, 8:10], BN_EPS, None, ALU.add).then_inc(bnvar_ready, 1)

            def batch_norm_factors():
                dve.wait_ge(bnpow_ready, 1)
                link(V.tensor_tensor(acol[:], acol[:], pcol[:, 6:8], ALU.mult))
                dve.wait_ge(consts_in, 16 * loads["consts"])
                for k in range(2 * NQ):
                    V.tensor_scalar(adiag[:, k, :], ident, acol[:, k // NQ, k % NQ:k % NQ + 1], None, ALU.mult)
                pv = pcol[:, 0:6].rearrange("p (l v) q -> p v l q", v=3)
                link(V.tensor_tensor(pv[:, 0], pv[:, 0], pv[:, 1], ALU.subtract))
                link(V.tensor_tensor(pv[:, 0], pv[:, 0], acol[:], ALU.mult))
                link(V.tensor_tensor(pv[:, 0], pv[:, 0], pv[:, 2], ALU.add))
                V.tensor_copy(c1col[:], pcol[:, 0])
                V.tensor_scalar(nc2col[:], pcol[:, 3], -1.0, None, ALU.mult)
                for e, hf in enumerate(halves):
                    for qq in range(NQ):
                        dst = c2m[hf, qq, :].rearrange("p (r e) -> p r e", r=4)[:, :, 2 * qq + e:2 * qq + e + 1]
                        V.tensor_copy(dst, middle(pcol[hf, 3, qq:qq + 1], 1, 4))
                for k, hf in enumerate(halves):
                    V.tensor_scalar(w_rt[hf, NE * k:NE * k + NE], wr_raw[hf, :], 1.0 / NB, None, ALU.mult)
                V.tensor_copy(ehalf_r[:], ehalf).then_inc(adiag_ready, 1)

            def expert_factors():
                dve.wait_ge(cst_made, 1)
                for k, hf in enumerate(halves):
                    V.tensor_scalar(w_cst[:, hf], bank[B_HO][0:32, 0:C], pmask[:, k:k + 1], None, ALU.mult)
                dve.wait_ge(arow_made, 2)
                V.tensor_tensor(w_l2[:].rearrange("p q k -> p (q k)"), w_l2[:].rearrange("p q k -> p (q k)"),
                                bank[B_FY][:], ALU.mult)
                link(V.tensor_tensor(w_l1[:], w_l1[:], bank[B_M][:], ALU.mult))

            def expert_split():
                V.tensor_copy(w_l2_hi[:], w_l2[:])
                link(V.tensor_copy(w_l1_hi[:], w_l1[:]))
                V.tensor_tensor(w_l2_lo[:], w_l2[:], w_l2_hi[:].bitcast(F32), ALU.subtract)
                V.tensor_tensor(w_l1_lo[:], w_l1[:], w_l1_hi[:].bitcast(F32), ALU.subtract).then_inc(ffn_weights, 1)

            between = {1: chunk_input_weights, 2: batch_norm_factors, 3: expert_split}

            def centre(ln, s):
                if valid(s):
                    ht = bank[B_T][0:BJ, :].rearrange("p (g c) -> p g c", c=C)
                    after(dve, ft_done[ln], s)
                    V.tensor_reduce(hsum[:, ln, :], ht, AX_X, ALU.add).then_inc(hsum_ready[ln], 1)
                    after(dve, hsum_ready[ln], s)
                    V.scalar_tensor_tensor(hcent[:, ln, :].rearrange("p (g c) -> p g c", c=C), middle(hsum[:, ln, :], 2, C),
                                           -1.0 / C, ht, ALU.mult, ALU.add).then_inc(hcent_ready[ln], 1)

            def channel_sums(ln, s):
                if valid(s):
                    after(dve, sq_ready[ln], s)
                    V.tensor_reduce(ssum[:, ln, :], sq[:, ln, :].rearrange("p (g c) -> p g c", c=C), AX_X, ALU.add)\
                        .then_inc(ssum_ready[ln], 1)

            def variance(ln, s):
                if valid(s):
                    after(dve, ssum_ready[ln], s)
                    after(dve, rstd_ready[ln], s - 1)
                    V.tensor_scalar(varr[:, ln, :], ssum[:, ln, :], 1.0 / C, LN_EPS, ALU.mult, ALU.add)\
                        .then_inc(var_ready[ln], 1)

            def normalise(ln, s):
                if valid(s):
                    after(dve, rstd_ready[ln], s)
                    after(dve, bt_done[ln], s - 1)
                    V.tensor_tensor(xnt[:, ln, :].rearrange("p (g c) -> p g c", c=C),
                                    hcent[:, ln, :].rearrange("p (g c) -> p g c", c=C), middle(rstd[:, ln, :], 2, C),
                                    ALU.mult).then_inc(xnt_ready[ln], 1)

            def body(it, q):
                c, a, b, y, dd, f = it, it - 1, it - 2, it - 3, it - 4, it - 5
                r = (q + 1) % 2
                def gating(k):
                    if valid(a):
                        after(dve, gate_ready, a, 9, k + 1)
                        after(dve, mix_part, a if k >= 4 else a - 1, 9, k - 3 if k >= 4 else k + 6)
                        V.scalar_tensor_tensor(gated[:, k % 4, :].rearrange("p (b w) -> p b w", b=NB),
                                               gate[:, k % 4, :].rearrange("p (b w) -> p b w", b=NB), 1.0, gate_input(k, r),
                                               ALU.add, ALU.mult).then_inc(gated_ready, 1)

                def low_parts(ln, s, buf, dst):
                    if valid(s):
                        for par in range(2):
                            after(dve, xhi_ready[ln], s, 2, par + 1)
                            v = bank[B_M][halves[par], 0:TOK].rearrange("p (t g) -> p g t", t=T)
                            hi, lo = (dst[hf, buf, par, :].rearrange("p (g t) -> p g t", t=T) for hf in (halves[par], other[par]))
                            V.tensor_tensor(lo, v, hi.bitcast(F32), ALU.subtract).then_inc(xn_ready[ln], 1)

                def softmax_max():
                    if valid(dd):
                        lg = bank[B_M][0:WW, 0:16].rearrange("p (r e) -> p r e", r=2)
                        after(dve, rt_done, dd)
                        V.tensor_reduce(lmax[:], lg, AX_X, ALU.max).then_inc(lmax_ready, 1)
                        after(dve, lmax_ready, dd)
                        V.tensor_tensor(lsub[:].rearrange("p (r e) -> p r e", r=2), lg, middle(lmax[:], 2, NE), ALU.subtract)\
                            .then_inc(lsub_ready, 1)

                def softmax_sum():
                    if valid(dd):
                        after(dve, lexp_ready, dd)
                        V.tensor_reduce(lsum[:], lexp[:].rearrange("p (r e) -> p r e", r=2), AX_X, ALU.add)\
                            .then_inc(lsum_ready, 1)

                def softmax_reciprocal():
                    if valid(dd):
                        after(dve, lsum_ready, dd)
                        V.reciprocal(lrec[:], lsum[:]).then_inc(lrec_ready, 1)

                def softmax_weights():
                    if valid(dd):
                        after(dve, lrec_ready, dd)
                        after(dve, wt_done, dd - 1)
                        V.tensor_tensor(wfull[:].rearrange("p (r e) -> p r e", r=2), lexp[:].rearrange("p (r e) -> p r e", r=2),
                                        middle(lrec[:], 2, NE), ALU.mult).then_inc(wfull_ready, 1)

                def weights_high():
                    if valid(dd):
                        after(dve, wfull_ready, dd)
                        V.tensor_copy(wtok[0:WW, 0:16].bitcast(F32R), wfull[:]).then_inc(whi_ready, 1)

                def weights_low():
                    if valid(dd):
                        after(dve, whi_ready, dd)
                        V.tensor_tensor(wtok[0:WW, 16:32], wfull[:], wtok[0:WW, 0:16], ALU.subtract).then_inc(wtok_ready, 1)

                def split_rows():
                    if valid(c):
                        x_arrived(dve, c, q)
                        after(dve, conv_done, c - 1)
                        V.tensor_copy(xa_hi[:], xa[:, q]).then_inc(x_split, 1)

                def spread_weights():
                    if valid(dd):
                        after(dve, wt_done, dd)
                        after(dve, wb_done, dd - 1)
                        V.tensor_tensor(wmask[:], middle(bank[B_M][0:32, 64:64 + WW], 1, 8), middle(emask, 2, WW),
                                        ALU.mult).then_inc(wmask_ready, 1)
                        V.tensor_copy(wts[:], bank[B_M][0:32, 64:64 + WW]).then_inc(wts_ready, 1)

                def second_residual():
                    if valid(y):
                        after(dve, y_done, y)
                        after(dve, h2c_ready, y - 2)
                        after(dve, ft_done[1], y - 2)
                        V.tensor_tensor(h2[:, r, :], bank[B_FY][:, 0:TOK], h[:, r, :], ALU.add).then_inc(h2_ready, 1)

                if first_router(it):
                    for k in range(3):
                        gating(k)
                    centre(0, b)
                    gating(3)
                    channel_sums(0, b)
                    softmax_max()
                    variance(0, b)
                    softmax_sum()
                    softmax_reciprocal()
                    softmax_weights()
                    weights_high()
                    weights_low()
                else:
                    softmax_max()
                    gating(0)
                    gating(1)
                    softmax_sum()
                    gating(2)
                    softmax_reciprocal()
                    centre(0, b)
                    softmax_weights()
                    gating(3)
                    weights_high()
                    channel_sums(0, b)
                    weights_low()
                    variance(0, b)
                gating(4)
                spread_weights()
                if not (isinstance(it, int) and it == 0):
                    split_rows()
                gating(5)
                normalise(0, b)
                second_residual()
                gating(6)
                gating(7)
                low_parts(0, b, q, xn1)
                gating(8)
                centre(1, y)
                channel_sums(1, y)
                variance(1, y)
                if valid(b):
                    after(dve, uin_ready, b - 1, 2)
                    if not (isinstance(b, int) and b == 0):
                        zl = z[:, :, CH:CH + 1].rearrange("p (k b) o -> p k (b o)", k=2)
                        uf = u[:, :, 0:1].rearrange("p (k b) o -> p k (b o)", k=2)
                        V.tensor_scalar(uf, zl, turn_r, None, ALU.mult).then_inc(carry_a, 1)
                        after(dve, carry_a, b - 1)
                        V.scalar_tensor_tensor(uf[:, 0], zl[:, 1], nturn_i, uf[:, 0], ALU.mult, ALU.add).then_inc(carry_b, 1)
                        V.scalar_tensor_tensor(uf[:, 1], zl[:, 0], turn_i, uf[:, 1], ALU.mult, ALU.add).then_inc(carry_b, 1)
                        after(dve, carry_b, b - 1, 2)
                if isinstance(it, int) and it in between:
                    between[it]()
                if valid(c):
                    after(dve, h1_ready, c)
                    for par in range(2):
                        after(dve, h1hi_ready, c, 2, par + 1)
                        V.tensor_tensor(h1s[other[par], q, par, :], h1[halves[par], q, :],
                                        h1s[halves[par], q, par, :].bitcast(F32), ALU.subtract).then_inc(h1s_ready, 1)

                def expert(k):
                    if valid(dd):
                        after(dve, l2_done, dd, 8, k + 1)
                        after(dve, l3_part, dd if k >= 4 else dd - 1, 8, k - 3 if k >= 4 else k + 5)
                        if k == 0:
                            after(dve, wbs_ready, dd)
                        g = bank[g_bank(q, G_TILES.index(("l2", k)))][:, 0:TOK]
                        V.scalar_tensor_tensor(z2[:, k % 4, :].rearrange("p (b x) -> p b x", b=NB),
                                               g.rearrange("p (b x) -> p b x", b=NB), nc2col[:, k // 2:k // 2 + 1],
                                               middle(wbs[:, k, :], 1, NB), ALU.max, ALU.mult).then_inc(z2_ready, 1)

                if valid(b):
                    after(dve, uin_ready, b - 1, 2)
                    after(dve, u_done, b)
                    src = bank[B_T][:, 0:4 * BJ].rearrange("p (g c) -> p g c", c=CH)
                    for dst, tr in ((m_cos, 0), (m_sin, 1)):
                        V.tensor_tensor(dst[:], src, middle(rot[:, tr, 1:1 + CH], 1, 2 * NB), ALU.mult).then_inc(m_ready, 1)
                normalise(1, y)
                expert(0)
                expert(1)
                if valid(b):
                    after(dve, uin_ready, b, 2)
                    after(dve, n_ready, b - 1, 2)
                    V.tensor_tensor_scan(z[:].rearrange("p g c -> p (g c)"), decay[:], u[:].rearrange("p g c -> p (g c)"),
                                         0.0, ALU.mult, ALU.add).then_inc(z_ready, 1)
                expert(2)
                if valid(b):
                    after(dve, z_ready, b)
                    after(dve, st_ready, b - 1, 2)
                    for dst, tr in ((n_cos, 0), (n_sin, 1)):
                        V.tensor_tensor(dst[:], z[:, :, 0:CH], middle(rot[:, tr, 0:CH], 1, 2 * NB), ALU.mult)\
                            .then_inc(n_ready, 1)
                low_parts(1, y, r, xn2)
                expert(3)
                if valid(y):
                    after(dve, rt_done, y - 1)
                    V.tensor_reduce(fsum[:].rearrange("p (j t) -> p j t", t=T),
                                    bank[B_M][:, 0:TOK].rearrange("p (t b j) -> p j t b", t=T, b=NB), AX_X, ALU.add)\
                        .then_inc(fsum_ready, 1)
                for k in range(4, 8):
                    expert(k)
                if valid(dd):
                    after(dve, l3_part, dd, 8)
                    after(dve, ot_done, dd - 1)
                    after(dve, h2c_ready, dd)
                    V.tensor_tensor(fin[:], bank[B_HO][:, 0:TOK], h2c[:], ALU.add).then_inc(fin_ready, 1)

            drive(dve, body, {1: lag_weights, 2: batch_norm_columns, 3: expert_factors})

        @block.tensor
        def _(pe):
            def mm(dst, lhsT, rhs, start=True, stop=True):
                return nc.tensor.matmul(dst, lhsT, rhs, start=start, stop=stop, skip_group_check=True)

            pe.wait_ge(consts_in, 16 * loads["consts"])
            pe.wait_ge(ssm_in, 16 * loads["ssm"])
            for c in range(2):
                ins = nc.tensor.transpose(bank[2][:, C * c:C * c + C], c_raw[:, c, :], ident[0:C, 0:C])
            ins.then_inc(ct_turned, 1)
            pe.wait_ge(tok_weights, 2)

            def recurrence_weights():
                pe.wait_ge(g_ready, 1)
                pe.wait_ge(ct_ready, 1)
                for k in range(T):
                    o = bank[B_HO][:, C * k:C * k + C]
                    mm(o, g_in[:, k, 0, :], ct[:, 0, :], True, False)
                    ins = mm(o, g_in[:, k, 1, :], ct[:, 1, :], False, k > 0)
                    if k == 0:
                        ins = mm(o, d_raw[:].rearrange("p a c -> p (a c)"), ident[0:C, 0:C], False, True)
                ins.then_inc(lag_made, 1)
                for k in range(T):
                    for c in range(2):
                        o = (2 * (k % 2) + c) * 128
                        ins = nc.tensor.transpose(bank[G_TURNED[k // 2]][:, o:o + 128], g_in[:, k, c, :], ident)
                    if k % 2:
                        ins.then_inc(win_turned, 1)
                pe.wait_ge(tok_weights, 4)

            def batch_norm_columns():
                pe.wait_ge(ssm_weights, 1)
                pe.wait_ge(ffn_in, 16 * loads["ffn"])
                nc.tensor.transpose(bank[B_M][:, 0:40], praw[:], ident[0:40, 0:40]).then_inc(pcol_made, 1)

            def expert_factors():
                pe.wait_ge(adiag_ready, 1)
                after(pe, h_ready, 1)
                for qq in range(NQ):
                    mm(bank[B_HO][0:32, 0:C], c2m[:, qq, :], w_l3[:, qq, :], qq == 0, False)
                mm(bank[B_HO][0:32, 0:C], dup8, bo_raw[:], False, True).then_inc(cst_made, 1)
                after(pe, h1_ready, 2)
                mm(bank[B_FY][:], onesq[:], adiag[:, NQ:2 * NQ, :]).then_inc(arow_made, 1)
                after(pe, xn_ready[0], 0, 2)
                mm(bank[B_M][:], onesq[:], adiag[:, 0:NQ, :]).then_inc(arow_made, 1)

            def free_bank(it, q, idx):
                prev = g_previous(it, q, idx)
                if prev:
                    kind, k, s = prev
                    after(pe, {"s": gate_ready, "l1": z1_ready, "l2": z2_ready}[kind], s, PER[kind], k + 1)
                return bank[g_bank(q, idx)][:, 0:TOK]

            def body(it, q):
                c, a, b, y, dd, f = it, it - 1, it - 2, it - 3, it - 4, it - 5
                r = (q + 1) % 2

                def gate_product(k):
                    if not valid(a):
                        return
                    if k == 0:
                        after(pe, h1s_ready, a, 2)
                    o = free_bank(it, q, k)
                    if k < 8:
                        mm(o, w_gate_hi[:, k, :], h1s[:, r, k % 2, :], True, False)
                        ins = mm(o, w_gate_lo[:, k, :], h1s[:, r, k % 2, :], False, True)
                    else:
                        after(pe, h1lo_ready, a)
                        mm(o, w_gate_hi[:, 8, :], h1_hi[:], True, False)
                        mm(o, w_gate_lo[:, 8, :], h1_hi[:], False, False)
                        ins = mm(o, w_gate_hi[:, 8, :], h1_lo[:], False, True)
                    ins.then_inc(s_done, 1)

                def mix_product(k):
                    if not valid(a):
                        return
                    after(pe, gated_ready, a, 9, k + 1)
                    if k < 8:
                        ins = mm(bank[B_HO][halves[k % 2], 0:TOK], w_mixA[:, k, :], gated[:, k % 4, :], k < 2, False)
                    else:
                        after(pe, g8lo_ready, a)
                        mm(bank[B_HO][:, 0:TOK], w_mixB_hi[:], gated8_hi[:], False, False)
                        mm(bank[B_HO][:, 0:TOK], w_mixB_lo[:], gated8_hi[:], False, False)
                        ins = mm(bank[B_HO][:, 0:TOK], w_mixB_hi[:], gated8_lo[:], False, True)
                    ins.then_inc(mix_part, 1)

                def turn(ln, s, src):
                    if not valid(s):
                        return
                    for t in range(T):
                        ins = nc.tensor.transpose(bank[B_T][0:BJ, 128 * t:128 * t + 128], src(t), ident)
                    ins.then_inc(ft_done[ln], 1)

                def turn_back(ln, s):
                    if not valid(s):
                        return
                    after(pe, xnt_ready[ln], s)
                    for t in range(T):
                        ins = nc.tensor.transpose(bank[B_M][:, BJ * t:BJ * t + BJ], xnt[:, ln, 128 * t:128 * t + 128],
                                                  ident[0:BJ, 0:BJ])
                    ins.then_inc(bt_done[ln], 1)

                def logits():
                    if valid(dd):
                        after(pe, fsum_ready, dd)
                        mm(bank[B_M][0:WW, 0:16], fsum[:], w_rt[:], True, False)
                        mm(bank[B_M][0:WW, 0:16], ones_row[:, 0:WW], br_row[:].rearrange("p r e -> p (r e)"), False, True)\
                            .then_inc(rt_done, 1)

                def output_turn():
                    if valid(f):
                        after(pe, fin_ready, f)
                        after(pe, h1_ready, it - 1)
                        for t in range(T):
                            ins = nc.tensor.transpose(bank[B_FY][0:BJ, 128 * t:128 * t + 128], fin[:, t::T], ident)
                        ins.then_inc(ot_done, 1)

                def own_tokens():
                    if valid(y):
                        after(pe, out_ready, f)
                        after(pe, h1_ready, it - 1)
                        o = bank[B_FY][:, 0:TOK].rearrange("p (g t) -> p g t", t=T)
                        for k in range(T):
                            for par in range(2):
                                mm(o[halves[par], :, k:T], w_lag[:, k, :],
                                   xn1[:, r, par, :].bitcast(F32).rearrange("p (g t) -> p g t", t=T)[:, :, 0:T - k],
                                   k == 0, False)

                def states_to_output():
                    if valid(y):
                        after(pe, st_ready, y, 2)
                        ot = bank[B_FY][:, 0:TOK].rearrange("p (b j t) -> p t b j", b=NB, t=T)
                        for t in range(T):
                            for cc in range(2):
                                for par in range(2):
                                    ins = mm(ot[halves[par], t], w_st[:, cc, t, :],
                                             xst[:, NB * cc:NB * cc + NB, J * par:J * par + J], False,
                                             t == T - 1 and cc == 1)
                        ins.then_inc(y_done, 1)

                def weights_turn():
                    if valid(dd):
                        after(pe, wtok_ready, dd)
                        nc.tensor.transpose(bank[B_M][0:32, 64:192], wtok[:], ident).then_inc(wt_done, 1)

                def weights_spread():
                    if valid(dd):
                        after(pe, wmask_ready, dd)
                        after(pe, wts_ready, dd)
                        mm(bank[B_M][:, 0:TOK], ehalf_r[:], wmask[:].rearrange("p q x -> p (q x)"))
                        mm(bank[B_M][:, TOK:TOK + WW], w_cst[:], wts[:]).then_inc(wb_done, 1)

                def conv_taps():
                    if valid(c):
                        x_arrived(pe, c, q)
                        after(pe, xlo_ready, c)
                        after(pe, h2_ready, y)
                        o = bank[B_FY][:, 0:TOK]
                        for k in range(3):
                            hi, lo = (v[:, :, k:k + WW] for v in (xa_hi, xa_lo))
                            mm(o, w_conv_hi[:, k, :], hi, k == 0, False)
                            mm(o, w_conv_hi[:, k, :], lo, False, False)
                            mm(o, w_conv_lo[:, k, :], hi, False, False)

                def conv_outer(part):
                    if valid(c) and part == 0:
                        for par in range(2):
                            mm(bank[B_FY][halves[par], 0:TOK], w_convC[:, par, :], xc[:, par, q], False, False)
                    if valid(c) and part == 1:
                        after(pe, xblo_ready, c)
                        o = bank[B_FY][:, 0:TOK]
                        mm(o, w_conv_hi[:, 3, :], xb_hi[:], False, False)
                        mm(o, w_conv_lo[:, 3, :], xb_hi[:], False, False)
                        mm(o, w_conv_hi[:, 3, :], xb_lo[:], False, True).then_inc(conv_done, 1)

                if not first_router(it):
                    logits()
                gate_product(0)
                gate_product(1)
                if valid(b):
                    after(pe, h_ready, b)
                    after(pe, m_ready, b - 1, 2)
                    turn(0, b, lambda t: h[:, q, t::T])
                output_turn()
                gate_product(2)
                gate_product(3)
                gate_product(4)
                if first_router(it):
                    logits()
                mix_product(0)
                mix_product(1)
                own_tokens()
                mix_product(2)
                mix_product(3)
                gate_product(5)
                weights_turn()
                states_to_output()
                mix_product(4)
                mix_product(5)
                weights_spread()
                gate_product(6)
                gate_product(7)
                if valid(y):
                    after(pe, h2_ready, y)
                    after(pe, hcent_ready[0], b) if valid(b) else after(pe, m_ready, b - 1, 2)
                    turn(1, y, lambda t: h2[:, r, t::T])
                after(pe, csts_ready, dd)
                turn_back(0, b)
                gate_product(8)
                conv_taps()
                conv_outer(0)
                mix_product(6)
                mix_product(7)
                conv_outer(1)

                def l1(k):
                    if valid(dd):
                        o = free_bank(it, q, G_TILES.index(("l1", k)))
                        ws = slice(128 * (k // 2), 128 * (k // 2) + 128)
                        if k == 0:
                            after(pe, xn_ready[1], dd, 2)
                        mm(o, w_l1_hi[:, ws], xn2[:, q, k % 2, :], True, False)
                        mm(o, w_l1_lo[:, ws], xn2[:, q, k % 2, :], False, True).then_inc(l1_done, 1)

                def l2(k):
                    if valid(dd):
                        o = free_bank(it, q, G_TILES.index(("l2", k)))
                        if k < SPLIT_FROM:
                            after(pe, z1_ready, dd, 8, k + 1)
                            mm(o, w_l2[:, k // 2, :], z1[:, k % 4, :]).then_inc(l2_done, 1)
                            return
                        after(pe, z1lo_ready, dd, 8 - SPLIT_FROM, k - SPLIT_FROM + 1)
                        mm(o, w_l2_hi[:, k // 2, :], z1_hi[:, k % 4, :], True, False)
                        mm(o, w_l2_lo[:, k // 2, :], z1_hi[:, k % 4, :], False, False)
                        mm(o, w_l2_hi[:, k // 2, :], z1_lo[:, k % 4, :], False, True).then_inc(l2_done, 1)

                def l3(k):
                    if valid(dd):
                        if k == 0:
                            after(pe, h_ready, a)
                        after(pe, z2_ready, dd, 8, k + 1)
                        mm(bank[B_HO][halves[k % 2], 0:TOK], w_l3[:, k // 2, :], z2[:, k % 4, :], k < 2, k >= 6)\
                            .then_inc(l3_part, 1)

                mix_product(8)
                l1(0)
                l1(1)
                if valid(b):
                    after(pe, xn_ready[0], b, 2)
                    after(pe, hcent_ready[1], y)
                    xn = xn1[:, q].rearrange("p r (b j t) -> p t b r j", b=NB, t=T)
                    for cc in range(2):
                        o = bank[B_T][:, 2 * BJ * cc:2 * BJ * cc + 2 * BJ].rearrange("p (b r j) -> p b r j", b=NB, r=2)
                        for t in range(T):
                            mm(o, w_in_hi[:, cc, t, :], xn[:, t], t == 0, False)
                            ins = mm(o, w_in_lo[:, cc, t, :], xn[:, t], False, t == T - 1)
                    ins.then_inc(u_done, 1)
                l1(2)
                for k in range(8):
                    if k + LEAD < 8:
                        l1(k + LEAD)
                    l2(k)
                    if k in (3, 5, 7):
                        l3(k - 3)
                        l3(k - 2)
                    if k == TURN_BACK_AT:
                        after(pe, xn_ready[0], b, 2) if valid(b) else after(pe, csts_ready, dd)
                        turn_back(1, y)
                l3(6)
                l3(7)
            drive(pe, body, {1: recurrence_weights, 2: batch_norm_columns, 3: expert_factors, 4: lambda: pe.wait_ge(ffn_weights, 1)})


_INS = ["x", "L0_tok_W1", "L0_tok_b1", "L0_tok_W2", "L0_tok_b2", "L0_tok_W3", "L0_tok_b3",
        "L0_attn_nu_log", "L0_attn_theta_log", "L0_attn_gamma_log", "L0_attn_B_re", "L0_attn_B_im",
        "L0_attn_C_re", "L0_attn_C_im", "L0_attn_D", "L0_ffn_Wr", "L0_ffn_br", "L0_ffn_W1", "L0_ffn_b1",
        "L0_ffn_g1", "L0_ffn_be1", "L0_ffn_m1", "L0_ffn_v1", "L0_ffn_W2", "L0_ffn_b2", "L0_ffn_g2",
        "L0_ffn_be2", "L0_ffn_m2", "L0_ffn_v2", "L0_ffn_Wo", "L0_ffn_bo"]


def constants(np):
    k, m = np.arange(32) % 16, np.arange(128)
    values = {
        "ident": np.eye(128),
        "emask": (k[:, None] // NE == np.arange(8)[None, :] % 2) & (k[:, None] % NE // 2 == np.arange(8)[None, :] // 2),
        "ehalf": k[:, None] % 2 == m[None, :] // C,
        "pmask": k[:, None] // NE == np.arange(2)[None, :],
        "dup8": np.arange(8)[:, None] == k[None, :] % NE,
    }
    packed = np.zeros((128, CONST_COLUMNS))
    for name, (rows, at, columns) in CONST_AT.items():
        packed[0:rows, at:at + columns] = values[name]
    return {"consts": packed, "zeros": np.zeros((C, TOK))}


def kernel(**inputs):
    import numpy as _np
    import concourse.bacc as _bacc
    from concourse import mybir as _mybir
    from concourse.bass_utils import run_bass_kernel_spmd as _run

    nc = _bacc.Bacc("TRN2", target_bir_lowering=False, num_devices=1)
    arrays, d = {}, {}
    given = {name: _np.ascontiguousarray(inputs[name]) for name in _INS}
    given.update({name: _np.ascontiguousarray(a, dtype=_np.float32) for name, a in constants(_np).items()})
    for name, a in given.items():
        arrays[f"in_{name}_dram"] = a
        d[name] = nc.dram_tensor(f"in_{name}_dram", a.shape, _mybir.dt.from_np(a.dtype), kind="ExternalInput").ap()
    out = nc.dram_tensor("out_0_dram", (NB, HH * WW, C), F32, kind="ExternalOutput").ap()
    build(nc, d, out)
    r = _run(nc, [arrays], core_ids=[0])
    return r.results[0]["out_0_dram"]
```
